# Optimizing a Trainium2 kernel written in Bass

```python
import numpy as np
import jax
import jax.numpy as jnp

def _softmax(x, axis=-1):
    return jax.nn.softmax(x, axis=axis)

def _gelu(x):
    return jax.nn.gelu(x, approximate=True)

def _silu(x):
    return jax.nn.silu(x)

def _sigmoid(x):
    return jax.nn.sigmoid(x)

def _layernorm(x, axis=-1, eps=1e-05):
    m = jnp.mean(x, axis=axis, keepdims=True)
    v = jnp.var(x, axis=axis, keepdims=True)
    return (x - m) / jnp.sqrt(v + eps)

def _scatter_add(tgt, idx, src, axis=0):
    return tgt.at[idx].add(src)

def _segment_sum(src, seg, n):
    return jax.ops.segment_sum(src, seg, n)
kernel_name = 'mk_decoder_postln_d1_seqx_r8_f54803'

def setup_inputs(seed: int=0):
    np.random.seed(seed)
    _w = jnp.asarray

    def _rec_inputs():
        import jax
        import jax.numpy as jnp
        _rk = jax.random.key(seed)
        x = 7.22e-05 + 1 * jax.random.normal(jax.random.fold_in(_rk, 1), (4, 256, 256), jnp.float32)
        _lenS = 256 - jax.random.randint(jax.random.fold_in(_rk, 7), (4,), 0, max(1, 256 // 4) + 1, jnp.int32)
        _lenS2 = 256 - jax.random.randint(jax.random.fold_in(_rk, 8), (4,), 0, max(1, 256 // 4) + 1, jnp.int32)
        _ctx_1024P = jax.random.normal(jax.random.fold_in(_rk, 11), (4, 16, 128), jnp.float32)
        _ctx_1024c = jax.random.dirichlet(jax.random.fold_in(_rk, 511), 0.3 * jnp.ones((16,), jnp.float32), (4, 256))
        _ctx_1024t = jnp.einsum('bsk,bkd->bsd', _ctx_1024c, _ctx_1024P)
        _ctx_1024t = _ctx_1024t * jax.lax.rsqrt(jnp.mean(jnp.square(_ctx_1024t)) + 1e-12) * 0.953939
        ctx_1024 = 2.81802e-05 + 1.00001 * (_ctx_1024t + 0.3 * jax.random.normal(jax.random.fold_in(_rk, 611), (4, 256, 128), jnp.float32))
        return (x, ctx_1024)
    x, ctx_1024 = _rec_inputs()

    def _L0_attn_setup():
        import jax, jax.numpy as jnp
        import numpy as np
        B, S, H = (4, 256, 256)
        key = jax.random.key(seed)
        k1, k2, k3 = jax.random.split(key, 3)
        xav_qkv = float(np.sqrt(6.0 / (H + 3 * H)))
        xav_out = float(np.sqrt(6.0 / (H + H)))
        return {'hidden_states': jax.random.normal(k1, (B, S, H), dtype=jnp.float32), 'w_qkv': jax.random.uniform(k2, (3 * H, H), minval=-xav_qkv, maxval=xav_qkv, dtype=jnp.float32), 'b_qkv': jnp.zeros((3 * H,), dtype=jnp.float32), 'w_out': jax.random.uniform(k3, (H, H), minval=-xav_out, maxval=xav_out, dtype=jnp.float32), 'b_out': jnp.zeros((H,), dtype=jnp.float32)}
    _L0_attn_all = _L0_attn_setup()
    _L0_attn_in = {k: v for k, v in _L0_attn_all.items() if k in ('w_qkv', 'b_qkv', 'w_out', 'b_out')}
    del _L0_attn_all

    def _L0_xattn_setup():
        import jax, jax.numpy as jnp
        import numpy as np
        key = jax.random.key(seed)
        ks = jax.random.split(key, 6)
        B, L, N, C, D = (8, 64, 256, 128, 128)
        return {'teacher_logits': jax.random.normal(ks[0], (B, L, N), dtype=jnp.float32), 'teacher_features': jax.random.normal(ks[1], (B, N, C), dtype=jnp.float32), 'Wq': jax.random.normal(ks[2], (D, C), dtype=jnp.float32) * (1.0 / np.sqrt(C)), 'bq': jnp.zeros((D,), dtype=jnp.float32), 'Wk': jax.random.normal(ks[3], (D, C), dtype=jnp.float32) * (1.0 / np.sqrt(C)), 'bk': jnp.zeros((D,), dtype=jnp.float32)}
    _L0_xattn_all = _L0_xattn_setup()
    _L0_xattn_in = {k: v for k, v in _L0_xattn_all.items() if k in ('Wq', 'bq', 'Wk', 'bk')}
    del _L0_xattn_all

    def _L0_ffn_setup():
        import jax, jax.numpy as jnp
        import numpy as np
        H = 256
        NH = 16
        NOPE = 128
        ROPE = 64
        VD = 128
        QHD = NOPE + ROPE
        E = 16
        I = 176
        TOPK = 4
        NSH = 2
        SHI = I * NSH
        EPS = 1e-06
        B, S = (2, 128)

        def rmsnorm(x, w):
            return x * jax.lax.rsqrt(jnp.mean(x * x, axis=-1, keepdims=True) + EPS) * w
        key = jax.random.key(seed)
        ks = jax.random.split(key, 12)
        sd = lambda fan_in: 1.0 / np.sqrt(fan_in)
        return {'hidden_states': jax.random.normal(ks[0], (B, S, H), jnp.float32), 'positions': jnp.broadcast_to(jnp.arange(S, dtype=jnp.int32), (B, S)), 'ln1_w': jnp.ones((H,), jnp.float32), 'ln2_w': jnp.ones((H,), jnp.float32), 'q_w': jax.random.normal(ks[1], (NH * QHD, H), jnp.float32) * sd(H), 'kv_w': jax.random.normal(ks[2], (NH * (NOPE + VD) + ROPE, H), jnp.float32) * sd(H), 'o_w': jax.random.normal(ks[3], (H, NH * VD), jnp.float32) * sd(NH * VD), 'gate_w': jax.random.normal(ks[4], (E, H), jnp.float32) * sd(H), 'w1': jax.random.normal(ks[5], (E, 2 * I, H), jnp.float32) * sd(H), 'w2': jax.random.normal(ks[6], (E, H, I), jnp.float32) * sd(I), 'sh_gu_w': jax.random.normal(ks[7], (2 * SHI, H), jnp.float32) * sd(H), 'sh_down_w': jax.random.normal(ks[8], (H, SHI), jnp.float32) * sd(SHI)}
    _L0_ffn_all = _L0_ffn_setup()
    _L0_ffn_in = {k: v for k, v in _L0_ffn_all.items() if k in ('positions', 'ln1_w', 'ln2_w', 'q_w', 'kv_w', 'o_w', 'gate_w', 'w1', 'w2', 'sh_gu_w', 'sh_down_w')}
    del _L0_ffn_all
    return {'x': x, 'ctx_1024': ctx_1024, 'L0_attn_w_qkv': _L0_attn_in['w_qkv'], 'L0_attn_b_qkv': _L0_attn_in['b_qkv'], 'L0_attn_w_out': _L0_attn_in['w_out'], 'L0_attn_b_out': _L0_attn_in['b_out'], 'L0_xattn_Wq': _L0_xattn_in['Wq'], 'L0_xattn_bq': _L0_xattn_in['bq'], 'L0_xattn_Wk': _L0_xattn_in['Wk'], 'L0_xattn_bk': _L0_xattn_in['bk'], 'L0_ffn_positions': _L0_ffn_in['positions'], 'L0_ffn_ln1_w': _L0_ffn_in['ln1_w'], 'L0_ffn_ln2_w': _L0_ffn_in['ln2_w'], 'L0_ffn_q_w': _L0_ffn_in['q_w'], 'L0_ffn_kv_w': _L0_ffn_in['kv_w'], 'L0_ffn_o_w': _L0_ffn_in['o_w'], 'L0_ffn_gate_w': _L0_ffn_in['gate_w'], 'L0_ffn_w1': _L0_ffn_in['w1'], 'L0_ffn_w2': _L0_ffn_in['w2'], 'L0_ffn_sh_gu_w': _L0_ffn_in['sh_gu_w'], 'L0_ffn_sh_down_w': _L0_ffn_in['sh_down_w']}

def reference(x, ctx_1024, L0_attn_w_qkv, L0_attn_b_qkv, L0_attn_w_out, L0_attn_b_out, L0_xattn_Wq, L0_xattn_bq, L0_xattn_Wk, L0_xattn_bk, L0_ffn_positions, L0_ffn_ln1_w, L0_ffn_ln2_w, L0_ffn_q_w, L0_ffn_kv_w, L0_ffn_o_w, L0_ffn_gate_w, L0_ffn_w1, L0_ffn_w2, L0_ffn_sh_gu_w, L0_ffn_sh_down_w):
    import jax
    import jax.numpy as jnp

    def _L0_attn_ref(hidden_states, w_qkv, b_qkv, w_out, b_out):
        import jax, jax.numpy as jnp
        import numpy as np
        B, S, H = (4, 256, 256)
        Bc, Sc, Hc = hidden_states.shape
        scaling = jnp.sqrt(jnp.asarray(Hc, hidden_states.dtype))
        qkv = jnp.einsum('bsh,oh->bso', hidden_states, w_qkv) + b_qkv
        q, k, v = jnp.split(qkv, 3, axis=-1)
        scores = jnp.einsum('bqh,bkh->bqk', q, k) / scaling
        probs = jax.nn.softmax(scores, axis=-1)
        context = jnp.einsum('bqk,bkh->bqh', probs, v)
        out = jnp.einsum('bsh,oh->bso', context, w_out) + b_out
        return out

    def _L0_xattn_ref(teacher_logits, teacher_features, Wq, bq, Wk, bk):
        import jax, jax.numpy as jnp
        import numpy as np
        query = jnp.einsum('bnc,dc->bnd', teacher_features, Wq) + bq
        key = jnp.einsum('bnc,dc->bnd', teacher_features, Wk) + bk
        energy = jnp.einsum('bnd,bmd->bnm', query, key)
        attention = jax.nn.softmax(energy, axis=-1)
        x_m = jnp.einsum('bln,bmn->blm', teacher_logits, attention)
        return x_m

    def _L0_ffn_ref(hidden_states, positions, ln1_w, ln2_w, q_w, kv_w, o_w, gate_w, w1, w2, sh_gu_w, sh_down_w):
        import jax, jax.numpy as jnp
        import numpy as np
        H = 256
        NH = 16
        NOPE = 128
        ROPE = 64
        VD = 128
        QHD = NOPE + ROPE
        E = 16
        I = 176
        TOPK = 4
        NSH = 2
        SHI = I * NSH
        EPS = 1e-06
        B, S = (2, 128)

        def rmsnorm(x, w):
            return x * jax.lax.rsqrt(jnp.mean(x * x, axis=-1, keepdims=True) + EPS) * w
        b, s, h = hidden_states.shape
        x = rmsnorm(hidden_states, ln1_w)
        q = jnp.einsum('bsh,dh->bsd', x, q_w).reshape(b, s, NH, QHD)[..., :NOPE]
        kv = jnp.einsum('bsh,dh->bsd', x, kv_w)
        k = kv[..., :NH * NOPE].reshape(b, s, NH, NOPE)
        v = kv[..., NH * NOPE:NH * (NOPE + VD)].reshape(b, s, NH, VD)
        scale = QHD ** (-0.5)
        scores = jnp.einsum('bqnd,bknd->bnqk', q, k) * scale
        causal = jnp.tril(jnp.ones((s, s), bool))
        scores = jnp.where(causal, scores, -1000000000.0)
        p = jax.nn.softmax(scores, axis=-1)
        attn = jnp.einsum('bnqk,bknd->bqnd', p, v).reshape(b, s, NH * VD)
        attn_out = jnp.einsum('bsd,hd->bsh', attn, o_w)
        hid = hidden_states + attn_out
        x2 = rmsnorm(hid, ln2_w).reshape(-1, h)
        logits = x2 @ gate_w.T
        probs = jax.nn.softmax(logits, axis=-1)
        top_w, top_i = jax.lax.top_k(probs, TOPK)
        top_w = top_w / jnp.sum(top_w, axis=-1, keepdims=True)
        wfull = jnp.sum(jax.nn.one_hot(top_i, E, dtype=x2.dtype) * top_w[..., None], axis=1)
        gu = jnp.einsum('th,eih->tei', x2, w1)
        g, u = (gu[..., :I], gu[..., I:])
        act = jax.nn.silu(g) * u
        down = jnp.einsum('tei,ehi->teh', act, w2)
        routed = jnp.einsum('te,teh->th', wfull, down)
        sgu = x2 @ sh_gu_w.T
        sg, su = (sgu[..., :SHI], sgu[..., SHI:])
        shared = jax.nn.silu(sg) * su @ sh_down_w.T
        return hid + (routed + shared).reshape(b, s, h)
    x = _layernorm(x + _L0_attn_ref(x, L0_attn_w_qkv, L0_attn_b_qkv, L0_attn_w_out, L0_attn_b_out), axis=-1)
    x = _layernorm(x + _L0_xattn_ref(x, ctx_1024, L0_xattn_Wq, L0_xattn_bq, L0_xattn_Wk, L0_xattn_bk), axis=-1)
    x = _layernorm(x + _L0_ffn_ref(x, L0_ffn_positions, L0_ffn_ln1_w, L0_ffn_ln2_w, L0_ffn_q_w, L0_ffn_kv_w, L0_ffn_o_w, L0_ffn_gate_w, L0_ffn_w1, L0_ffn_w2, L0_ffn_sh_gu_w, L0_ffn_sh_down_w), axis=-1)
    return x

_drawn_inputs = setup_inputs


def setup_inputs(seed=0):
    import zlib

    import numpy as np

    out = dict(_drawn_inputs(seed))
    spreads = {'L0_attn_b_qkv': (0.0, 0.1),
     'L0_attn_b_out': (0.0, 0.1),
     'L0_xattn_bq': (0.0, 0.1),
     'L0_xattn_bk': (0.0, 0.1),
     'L0_ffn_ln1_w': (1.0, 0.2),
     'L0_ffn_ln2_w': (1.0, 0.2)}
    factors = {}
    for name, (base, spread) in spreads.items():
        noise = np.random.default_rng([zlib.crc32(name.encode()), seed]).standard_normal(out[name].shape)
        drawn = base * np.exp(spread * noise) if base else spread * noise
        out[name] = jnp.asarray(drawn.astype(out[name].dtype))
    for name, factor in factors.items():
        out[name] = (out[name] * factor).astype(out[name].dtype)
    return out
```

```python
from contextlib import ExitStack

import concourse.bass as bass
from concourse import mybir

F32 = mybir.dt.float32
F32R = mybir.dt.float32r
BF16 = mybir.dt.bfloat16
ALU = mybir.AluOpType
ACT = mybir.ActivationFunctionType
AX_X = mybir.AxisListType.X

P = 128
B, S, H = 4, 256, 256
T = B * S
HALF = T // 2
KC = H // P
NH, QHD, HD = 16, 192, 128
PAIRS = NH // 2
SP_ = 8
E, TOPK, I = 16, 4, 176
FF = E * I + 2 * I
NT = (FF + P - 1) // P
LN_EPS, RMS_EPS = 1e-5, 1e-6
SCALE = float(QHD) ** -0.5
MASK = -1e9 / SCALE


def program(nc, x, xT, ctxT, w_qkv, w_side, b_qkv, b_out, b_x, ln_w, w_heads_first, w_heads, w_last,
            w_moe, gateT, out):
    with ExitStack() as ctx:
        def sb(name, shape, dt=F32):
            return ctx.enter_context(nc.sbuf_tensor(name, shape, dt))

        def sem(name):
            return ctx.enter_context(nc.semaphore(name))

        def parts(name, shape):
            return sb(name + "_hi", shape, F32R), sb(name + "_lo", shape, F32R)

        XT = parts("XT", [P, KC, T])
        Q = parts("Q", [P, 2, T])
        K = parts("K", [P, 2, T])
        V = parts("V", [P, 2, 8, 256])
        AT = parts("AT", [P, 2, T])
        W = parts("W", [P, 2, 768])
        WS = parts("WS", [P, 768])
        PT = parts("PT", [P, 2, 512])
        CT = parts("CT", [P, 2, 512])
        hid = sb("hid", [P, 8, 256])
        x2 = sb("x2", [P, 8, 256])
        xb = sb("xb", [P, 8, 256])
        stage = sb("stage", [P, 8, 256])
        ex = sb("ex", [P, 6, 512])
        sm = sb("sm", [P, 2, 384])
        mask = sb("mask", [P, 256])
        ident = sb("ident", [P, P])
        identb = sb("identb", [P, P], BF16)
        bqkv = sb("bqkv", [P, 6])
        bxs = sb("bxs", [P, 2])
        lnw = sb("lnw", [P, 4])
        bo = sb("bo", [P, 256])
        zeros = sb("zeros", [1, 512], BF16)
        mh = sb("mh", [P, 2])
        mx = sb("mx", [P, 8, 2])
        nm = sb("nm", [P, 8, 2])
        sums = sb("sums", [P, 8, 2])
        rec = sb("rec", [P, 8, 2])
        stats = sb("stats", [P, 8, 6])
        mv = sb("mv", [P, 8, 2])
        veps = sb("veps", [P, 24])
        rstd = sb("rstd", [P, 24])
        msq = sb("msq", [P, 16])
        gate_raw = sb("gate_raw", [P, 2, E])
        gl = sb("gl", [P, 8, E + TOPK])
        gm = sb("gm", [P, 8])
        gs = sb("gs", [P, 8])
        gr = sb("gr", [P, 8])
        g8 = sb("g8", [P, 8, 8])
        grep = sb("grep", [P, 8, E + TOPK])
        gw = sb("gw", [P, 8, E])
        gt = sb("gt", [P, 8, E])
        wparts = sb("wparts", [P, 8, 96], BF16)
        wT = sb("wT", [96, T], BF16)
        sel = sb("sel", [96, NT * P], BF16)

        bank = [ctx.enter_context(nc.psum_tensor(f"bank{i}", [P, 512], F32)) for i in range(8)]

        def split3(pe, acc, lhs, rhs, first, last, **kw):
            for n, (a, b) in enumerate(((0, 0), (0, 1), (1, 0))):
                mm = pe.matmul(acc, lhs[a], rhs[b], start=first and n == 0, stop=last and n == 2, **kw)
            return mm

        def both(t, f):
            return f(t[0]), f(t[1])

        in_dma = [sem(f"in_dma{i}") for i in range(8)]
        const_dma, x_dma = sem("const_dma"), sem("x_dma")
        ident_ready, const_ready, xb_ready = sem("ident_ready"), sem("const_ready"), sem("xb_ready")
        in_hi, in_lo = sem("in_hi"), sem("in_lo")
        a_done, a_hi, a_lo = sem("a_done"), sem("a_hi"), sem("a_lo")
        fs_done, ft_done, fpv_done, fes_done = sem("fs_done"), sem("ft_done"), sem("fpv_done"), sem("fes_done")
        fout_done, fxt_done, fet_done = sem("fout_done"), sem("fxt_done"), sem("fet_done")
        fxm_done, fnt_done = sem("fxm_done"), sem("fnt_done")
        f_max, f_nm, f_exp, f_rec, f_norm = sem("f_max"), sem("f_nm"), sem("f_exp"), sem("f_rec"), sem("f_norm")
        e_max, e_nm, e_exp, e_rec, e_norm = sem("e_max"), sem("e_nm"), sem("e_exp"), sem("e_rec"), sem("e_norm")
        pt_hi, pt_lo, ct_hi, ct_lo = sem("pt_hi"), sem("pt_lo"), sem("ct_hi"), sem("ct_lo")
        x1t_hi, x1t_lo, et_hi, et_lo = sem("x1t_hi"), sem("x1t_lo"), sem("et_hi"), sem("et_lo")
        y1_ready, y1_stats, y1_var, y1_eps, y1_rstd = (sem(f"y1_{n}") for n in ("ready", "stats", "var", "eps", "rstd"))
        y2_ready, y2_stats, y2_var, y2_eps, y2_rstd = (sem(f"y2_{n}") for n in ("ready", "stats", "var", "eps", "rstd"))
        rms_eps, rms_rstd = sem("rms_eps"), sem("rms_rstd")
        pool_step, sel_ready, sel_dma = sem("pool_step"), sem("sel_ready"), sem("sel_dma")
        x1_ready, x2_ready, sq_ready, hid_copied = sem("x1_ready"), sem("x2_ready"), sem("sq_ready"), sem("hid_copied")
        xn_ready, xnt_hi, xnt_lo = sem("xn_ready"), sem("xnt_hi"), sem("xnt_lo")
        stage_dma = [sem(f"stage_dma{j}") for j in range(SP_)]
        w_hi, w_lo = sem("w_hi"), sem("w_lo")
        s_done, s_masked, s_exp, s_rec, s_norm = (
            sem("s_done"), sem("s_masked"), sem("s_exp"), sem("s_rec"), sem("s_norm"))
        t_done, t_hi, t_lo = sem("t_done"), sem("t_hi"), sem("t_lo")
        qk_done, qk_hi, qk_lo = sem("qk_done"), sem("qk_hi"), sem("qk_lo")
        v_done, v_hi, v_lo = sem("v_done"), sem("v_hi"), sem("v_lo")
        o_done, o_added = sem("o_done"), sem("o_added")
        pv_done, at_hi, at_lo = sem("pv_done"), sem("at_hi"), sem("at_lo")
        gate_dma, gate_hi, gate_lo = sem("gate_dma"), sem("gate_hi"), sem("gate_lo")
        h_sq, h_eps, h_rstd, h_norm = sem("h_sq"), sem("h_eps"), sem("h_rstd"), sem("h_norm")
        ht_done, ht_hi, ht_lo, gl_done = sem("ht_done"), sem("ht_hi"), sem("ht_lo"), sem("gl_done")
        r_max, r_sub, r_exp, r_step, r_parts, r_turned, wT_ready = (
            sem("r_max"), sem("r_sub"), sem("r_exp"), sem("r_step"), sem("r_parts"), sem("r_turned"), sem("wT_ready"))
        m_dma = [sem("m_dma0"), sem("m_dma1")]
        m_hi, m_lo = sem("m_hi"), sem("m_lo")
        g_done, u_done, b_done, d_done = sem("g_done"), sem("u_done"), sem("b_done"), sem("d_done")
        silu_ready, us_ready, act_ready, act_hi, act_lo = (
            sem("silu_ready"), sem("us_ready"), sem("act_ready"), sem("act_hi"), sem("act_lo"))
        hx_ready = sem("hx_ready")
        z_ready, z_stats, z_var, z_eps, z_rstd, z_out, out_dma = (
            sem("z_ready"), sem("z_stats"), sem("z_var"), sem("z_eps"), sem("z_rstd"), sem("z_out"), sem("out_dma"))

        block = ctx.enter_context(nc.Block())

        x_rows = x.rearrange("b (c p) h -> p (b c) h", p=P)
        out_rows = out.rearrange("b (c p) h -> b p c h", p=P)
        raw_xT = hid[:, :, :].rearrange("p (k t) h -> p k (t h)", k=KC)
        raw_ctx = x2[:, 0:4, :].rearrange("p t h -> p (t h)")
        raw_side = x2[:, 4:7, :].rearrange("p t h -> p (t h)")
        raw_moe = stage[:, 0:6, :].rearrange("p (s c) h -> p s (c h)", s=2)
        ctx_parts = both(V, lambda t: t[:, 1, 0:4, :].rearrange("p t h -> p (t h)"))
        xq_parts = both(V, lambda t: t[:, 1, 4:8, :].rearrange("p t h -> p (t h)"))
        xk_parts = both(XT, lambda t: t[:, 0, :])
        WV = both(W, lambda t: t[:, 0, 0:512].rearrange("p (k n) -> p k n", k=KC))
        WQ = both(W, lambda t: t[:, 0, 512:768].rearrange("p (k n) -> p k n", k=KC))
        WK = both(W, lambda t: t[:, 1, 0:256].rearrange("p (k n) -> p k n", k=KC))
        WO = both(W, lambda t: t[:, 1, 256:768].rearrange("p (h n) -> p h n", h=2))

        def qkv_at(t, part):
            return t[:, :, :].rearrange("p s n -> p (s n)")[:, part * 512:(part + 1) * 512]

        stage_flat = stage[:, :, :].rearrange("p s n -> p (s n)")
        inputs = (
            [(raw_xT[:, :, 0:HALF], both(XT, lambda t: t[:, :, 0:HALF]), xT[:, :, 0:HALF])]
            + [(stage_flat[:, n * 512:(n + 1) * 512], both(W, lambda t, n=n: qkv_at(t, n)), w_qkv[n, :, :])
               for n in range(3)]
            + [(raw_xT[:, :, HALF:T], both(XT, lambda t: t[:, :, HALF:T]), xT[:, :, HALF:T]),
               (raw_ctx, ctx_parts, ctxT[:, :]),
               (raw_side[:, 0:256], both(WS, lambda t: t[:, 0:256]), w_side[:, 0:256]),
               (raw_side[:, 256:768], both(WS, lambda t: t[:, 256:768]), w_side[:, 256:768])])
        IN_X0, IN_Q, IN_K, IN_V, IN_X1, IN_CTX, IN_SIDE, IN_OUT = range(1, 9)

        jobs = [(kind, c, half, max(need, IN_X1 if half else 0))
                for half in range(2)
                for kind, need in (("q", IN_Q), ("k", IN_K), ("v", IN_V)) for c in range(2)]
        jobs += [(kind, 0, half, IN_SIDE) for kind in ("xq", "xk") for half in range(2)]

        def job_target(kind, c, half):
            cols = slice(half * HALF, (half + 1) * HALF)
            if kind in "qk":
                return both(Q if kind == "q" else K, lambda t: t[:, c, cols])
            if kind == "v":
                r = 4 * half + 2 * c
                return both(V, lambda t: t[:, 0, r:r + 2, :].rearrange("p t h -> p (t h)"))
            return both(xq_parts if kind == "xq" else xk_parts, lambda t: t[:, cols])

        def job_bias(kind, c):
            return {"q": bqkv[:, c:c + 1], "k": bqkv[:, 2 + c:3 + c], "v": None,
                    "xq": bxs[:, 0:1], "xk": bxs[:, 1:2]}[kind]

        WAVES = [[(w - b, b) for b in range(B) if 0 <= w - b < 7] for w in range(7 + B - 1)]
        FS, FT, FPV, FES, FOUT, FXT, FET, FXM, FNT = 0, 1, 2, 3, 4, 5, 6, 7, 0

        def two(ap):
            return ap.rearrange("p (t h) -> p t h", t=2)

        FIRST_CHUNKS = 5
        BANK_QK, BANK_VO, BANK_PV, BANK_T, BANK_S = 0, 1, 2, 4, 6
        LAST = PAIRS - 1
        LAST_CHUNKS = (0, 5, 7)

        def chunks_done(g, j, last=False):
            if last:
                return FIRST_CHUNKS + SP_ * LAST + LAST_CHUNKS.index(j) + 1
            return FIRST_CHUNKS + SP_ * g + j + 1

        def chunk_target(j):
            return {0: both(WK, lambda t: t[:, :, :]), 4: both(WK, lambda t: t[:, :, :]),
                    2: both(WQ, lambda t: t[:, :, :]), 6: both(WQ, lambda t: t[:, :, :]),
                    1: both(WV, lambda t: t[:, 0, :]), 3: both(WV, lambda t: t[:, 1, :]),
                    5: both(WO, lambda t: t[:, 0, :]), 7: both(WO, lambda t: t[:, 1, :])}[j]

        def first_target(c):
            return chunk_target((2, 0, 1, 3, 2)[c])

        def over_pairs(eng, pair):
            pair(0, 0, True, False)
            with eng.Fori(0, (PAIRS - 2) // 2) as i:
                for n in range(2):
                    pair(2 * i + 1 + n, (1 + n) % 2, False, False)
            pair(LAST, LAST % 2, False, True)

        def mix_bank(s, n):
            return bank[4 + (3 * s + n) % 4]

        @block.sync
        def _(sp):
            for n, (raw, _, src) in enumerate(inputs):
                sp.dma_start(raw, src).then_inc(in_dma[n], 16)
                if n == 1:
                    sp.dma_start(bqkv[:, :], b_qkv).then_inc(const_dma, 16)
                    sp.dma_start(bxs[:, :], b_x).then_inc(const_dma, 16)
                    sp.dma_start(lnw[:, :], ln_w).then_inc(const_dma, 16)
            sp.dma_start(xb[:, :, :], x_rows).then_inc(x_dma, 16)
            sp.dma_start(bo[:, :], b_out.partition_broadcast(P)).then_inc(x_dma, 16)
            sp.dma_start(gate_raw[:, :, :], gateT).then_inc(gate_dma, 16)
            sp.wait_ge(in_lo, IN_V)
            for c in range(FIRST_CHUNKS):
                sp.dma_start(stage[:, c, :], w_heads_first[c, :, :]).then_inc(stage_dma[c], 16)

            def load(g, j, src):
                sp.dma_start(stage[:, j, :], src).then_inc(stage_dma[j], 16)

            for j in range(SP_):
                if j < FIRST_CHUNKS:
                    sp.wait_ge(w_lo, j + 1)
                load(0, j, w_heads[0, j, :, :])
            with sp.Fori(1, PAIRS - 1) as g:
                for j in range(SP_):
                    sp.wait_ge(w_lo, FIRST_CHUNKS + SP_ * (g - 1) + j + 1)
                    load(g, j, w_heads[bass.ds(g, 1), j, :, :].rearrange("g p n -> p (g n)"))
            for n, j in enumerate(LAST_CHUNKS):
                sp.wait_ge(w_lo, chunks_done(LAST - 1, j))
                load(LAST, j, w_last[n, :, :])

            sp.wait_ge(sel_ready, 1)
            for n in (32, 64):
                sp.dma_start(sel[n:n + 32, :], sel[0:32, :]).then_inc(sel_dma, 16)

            sp.wait_ge(w_lo, chunks_done(LAST, 7, True))
            for t in range(2):
                sp.dma_start(raw_moe[:, t, :], w_moe[t, :, :]).then_inc(m_dma[t], 16)
            with sp.Fori(1, (NT + 1) // 2) as i:
                for n in range(2):
                    sp.wait_ge(m_lo, 2 * i + n - 1)
                    sp.dma_start(raw_moe[:, n, :],
                                 w_moe[bass.ds(2 * i + n, 1), :, :].rearrange("g p n -> p (g n)"))\
                        .then_inc(m_dma[n], 16)
            for b in range(B):
                sp.wait_ge(z_out, b + 1)
                sp.dma_start(out_rows[b, :, :, :], xb[:, 2 * b:2 * b + 2, :]).then_inc(out_dma, 16)
            sp.wait_ge(out_dma, 16 * B)

        @block.tensor
        def _(pe):
            for n, (kind, c, half, need) in enumerate(jobs):
                pe.wait_ge(in_lo, need)
                if n >= 8:
                    pe.wait_ge(a_lo, n - 7)
                cols = slice(half * HALF, (half + 1) * HALF)
                if kind in "qk":
                    for k in range(KC):
                        at = (0 if kind == "q" else 512) + k * 256 + c * P
                        lhs = both(W, lambda t: t[:, :, :].rearrange("p s n -> p (s n)")[:, at:at + P])
                        mm = split3(pe, bank[n % 8][:, :], lhs, both(XT, lambda t: t[:, k, cols]),
                                    k == 0, k == KC - 1)
                elif kind == "v":
                    for r in range(2):
                        tok = (4 * half + 2 * c + r) * P
                        for k in range(KC):
                            at = 1024 + k * 256
                            mm = split3(pe, bank[n % 8][:, r * 256:r * 256 + 256],
                                        both(XT, lambda t: t[:, k, tok:tok + P]),
                                        both(W, lambda t: t[:, :, :].rearrange("p s n -> p (s n)")[:, at:at + 256]),
                                        k == 0, k == KC - 1)
                else:
                    at = 0 if kind == "xq" else P
                    mm = split3(pe, bank[n % 8][:, :], both(WS, lambda t: t[:, at:at + P]),
                                both(ctx_parts, lambda t: t[:, cols]), True, True)
                mm.then_inc(a_done, 1)
            pe.wait_ge(ident_ready, 2)
            pe.wait_ge(a_lo, len(jobs))

            def turn(dst, src):
                for n, s in enumerate(src):
                    mm = pe.transpose(dst[:, n * P:(n + 1) * P], s, ident[:, :])
                return mm

            def blocks(t, b):
                return [t(r)[:, c * P:(c + 1) * P] for c in range(2) for r in range(2)]

            for wave in WAVES:
                for st, b in wave:
                    tok = b * S
                    if st == 0:
                        if b:
                            pe.wait_ge(f_exp, b)
                        for r in range(2):
                            for k in range(KC):
                                mm = split3(pe, bank[FS][:, r * 256:r * 256 + 256],
                                            both(Q, lambda t: t[:, k, tok + r * P:tok + r * P + P]),
                                            both(K, lambda t: t[:, k, tok:tok + S]), k == 0, k == KC - 1)
                        mm.then_inc(fs_done, 1)
                    if st == 1:
                        pe.wait_ge(f_norm, b + 1)
                        if b:
                            pe.wait_ge(pt_lo, b)
                        turn(bank[FT], blocks(lambda r: ex[:, b % 2, r * 256:r * 256 + 256], b)).then_inc(ft_done, 1)
                    if st == 2:
                        pe.wait_ge(pt_lo, b + 1)
                        if b:
                            pe.wait_ge(ct_lo, b)
                            pe.wait_ge(e_exp, b)
                        for c in range(2):
                            for k in range(2):
                                mm = split3(pe, bank[FPV][:, c * 256:c * 256 + 256],
                                            both(V, lambda t: t[:, 0, 2 * b + k, c * P:c * P + P]),
                                            both(PT, lambda t: t[:, 0, k * 256:k * 256 + 256]), k == 0, k == 1)
                        mm.then_inc(fpv_done, 1)
                        for r in range(2):
                            mm = split3(pe, bank[FES][:, r * 256:r * 256 + 256],
                                        both(xq_parts, lambda t: t[:, tok + r * P:tok + r * P + P]),
                                        both(xk_parts, lambda t: t[:, tok:tok + S]), True, True)
                        mm.then_inc(fes_done, 1)
                    if st == 3:
                        pe.wait_ge(ct_lo, b + 1)
                        pe.wait_ge(in_lo, IN_OUT)
                        if b:
                            pe.wait_ge(y1_ready, b)
                        for r in range(2):
                            for k in range(KC):
                                mm = split3(pe, bank[FOUT][:, r * 256:r * 256 + 256],
                                            both(CT, lambda t: t[:, 0, k * 256 + r * P:k * 256 + r * P + P]),
                                            both(WS, lambda t: t[:, 256 + k * 256:512 + k * 256]),
                                            k == 0, k == KC - 1)
                        mm.then_inc(fout_done, 1)
                    if st == 4:
                        pe.wait_ge(x1_ready, b + 1)
                        if b:
                            pe.wait_ge(x1t_lo, b)
                        turn(bank[FXT], blocks(lambda r: hid[:, 2 * b + r, :], b)).then_inc(fxt_done, 1)
                        pe.wait_ge(e_norm, b + 1)
                        if b:
                            pe.wait_ge(et_lo, b)
                        turn(bank[FET], blocks(lambda r: ex[:, 2 + b, r * 256:r * 256 + 256], b)).then_inc(fet_done, 1)
                    if st == 5:
                        pe.wait_ge(x1t_lo, b + 1)
                        pe.wait_ge(et_lo, b + 1)
                        if b:
                            pe.wait_ge(y2_ready, b)
                        for r in range(2):
                            for k in range(2):
                                mm = split3(pe, bank[FXM][:, r * 256:r * 256 + 256],
                                            both(AT, lambda t: t[:, k, tok + r * P:tok + r * P + P]),
                                            both(PT, lambda t: t[:, 1, k * 256:k * 256 + 256]), k == 0, k == 1)
                        mm.then_inc(fxm_done, 1)
                    if st == 6:
                        pe.wait_ge(xn_ready, b + 1)
                        if b:
                            pe.wait_ge(xnt_lo, b)
                        turn(bank[FNT], blocks(lambda r: xb[:, 2 * b + r, :], b)).then_inc(fnt_done, 1)

            def project_qk(b, index, weights):
                pe.wait_ge(w_lo, weights)
                if not (isinstance(index, int) and index == 0):
                    pe.wait_ge(qk_lo, index)
                half = b % 2
                w = WQ if b < 2 else WK
                for k in range(KC):
                    mm = split3(pe, bank[BANK_QK][:, :], both(w, lambda t: t[:, k, :]),
                                both(XT, lambda t: t[:, k, half * HALF:half * HALF + HALF]), k == 0, k == KC - 1)
                mm.then_inc(qk_done, 1)

            def project_v(q):
                for r in range(2):
                    tok = (2 * q + r) * P
                    for k in range(KC):
                        mm = split3(pe, bank[BANK_VO][:, r * 256:r * 256 + 256],
                                    both(XT, lambda t: t[:, k, tok:tok + P]),
                                    both(WV, lambda t: t[:, k, :]), k == 0, k == KC - 1)
                mm.then_inc(v_done, 1)

            def project_o(q):
                for r in range(2):
                    tok = (2 * q + r) * P
                    for h in range(2):
                        mm = split3(pe, bank[BANK_VO][:, r * 256:r * 256 + 256],
                                    both(AT, lambda t: t[:, h, tok:tok + P]),
                                    both(WO, lambda t: t[:, h, :]), h == 0, h == 1)
                mm.then_inc(o_done, 1)

            def scores(m, j):
                tok, h, dst = (j % 4) * S, j // 4, bank[BANK_S + j % 2]
                q = both(Q, lambda t: t[:, h, tok:tok + S])
                k = both(K, lambda t: t[:, h, tok:tok + S])
                split3(pe, dst[:, 0:128], both(q, lambda t: t[:, 0:P]), both(k, lambda t: t[:, 0:P]), True, True)
                split3(pe, dst[:, 128:384], both(q, lambda t: t[:, P:S]), k, True, True).then_inc(s_done, 1)

            def turn_probs(m, j):
                pe.wait_ge(s_norm, m + 1)
                p = ex[:, j % 4, 0:384]
                turn(bank[BANK_T + j % 2], [p[:, n * P:(n + 1) * P] for n in range(3)]).then_inc(t_done, 1)

            def values(m, j, par):
                pe.wait_ge(t_lo, m + 1)
                b, h = j % 4, j // 4
                dst = bank[BANK_PV + (j // 2) % 2][:, (j % 2) * 256:(j % 2) * 256 + 256]
                v = both(V, lambda t: t[:, par, 2 * b:2 * b + 2, h * P:h * P + P])
                p = both(PT, lambda t: t[:, j % 2, :])
                split3(pe, dst, both(v, lambda t: t[:, 0, :]), both(p, lambda t: t[:, 0:256]), True, False)
                split3(pe, dst[:, 128:256], both(v, lambda t: t[:, 1, :]), both(p, lambda t: t[:, 256:384]),
                       False, True).then_inc(pv_done, 1)

            pe.wait_ge(xnt_lo, B)
            for b in range(4):
                project_qk(b, b, 1 if b < 2 else 2)
                if b == 0:
                    pe.wait_ge(w_lo, 4)
                else:
                    pe.wait_ge(v_lo, b)
                project_v(b)

            def pair(g, par, first, last):
                for j in range(SP_):
                    m = SP_ * g + j
                    if j % 4 == 0:
                        pe.wait_ge(qk_lo, SP_ * g + j + 4)
                    if not (first and j < 2):
                        pe.wait_ge(s_masked, m - 1)
                    scores(m, j)
                    if not (first and j < 2):
                        if not (first and j < 4):
                            pe.wait_ge(t_lo, m - 3)
                        turn_probs(m - 2, (j - 2) % 8)
                    if not (last and j >= 4):
                        done = {0: lambda: chunks_done(g - 1, 6) if not first else FIRST_CHUNKS,
                                2: lambda: chunks_done(g, 0, last), 4: lambda: chunks_done(g, 2),
                                6: lambda: chunks_done(g, 4)}[j // 2 * 2]()
                        project_qk(j % 4, SP_ * g + 4 + j, done)
                    if j < 4:
                        if not first:
                            if j == 0:
                                pe.wait_ge(w_lo, chunks_done(g - 1, 7))
                                pe.wait_ge(v_lo, 4 * g + 4)
                            else:
                                pe.wait_ge(o_added, 4 * (g - 1) + j)
                            if j % 2 == 0:
                                pe.wait_ge(at_lo, 4 * g - 1 + j // 2)
                            project_o(j)
                    elif not last:
                        if j == 4:
                            pe.wait_ge(w_lo, chunks_done(g, 3))
                            if not first:
                                pe.wait_ge(o_added, 4 * g)
                        else:
                            pe.wait_ge(v_lo, 4 * (g + 1) + j - 4)
                        project_v(j - 4)
                    if not (first and j < 2):
                        if j == 2:
                            pe.wait_ge(v_lo, 4 * g + 4)
                        if j % 2 == 0 and not (first and j < 6):
                            pe.wait_ge(at_lo, 4 * g + j // 2 - 2)
                        values(m - 2, (j - 2) % 8, par if j >= 2 else 1 - par)

            over_pairs(pe, pair)
            for j in (0, 1):
                m = SP_ * PAIRS + j
                pe.wait_ge(t_lo, m - 3)
                turn_probs(m - 2, 6 + j)
                if j == 0:
                    pe.wait_ge(at_lo, 4 * PAIRS - 2)
                values(m - 2, 6 + j, LAST % 2)
            pe.wait_ge(w_lo, chunks_done(LAST, 7, True))
            for q in range(4):
                pe.wait_ge(at_lo, 4 * PAIRS - 1 + q // 2)
                pe.wait_ge(o_added, 4 * LAST + q)
                project_o(q)

            for b in range(B):
                pe.wait_ge(h_norm, b + 1)
                if b:
                    pe.wait_ge(ht_lo, b)
                turn(bank[2], blocks(lambda r: xb[:, 2 * b + r, :], b)).then_inc(ht_done, 1)
            pe.wait_ge(ht_lo, B)
            pe.wait_ge(gate_lo, 1)
            for t in range(8):
                for k in range(KC):
                    mm = split3(pe, bank[3][:, t * E:(t + 1) * E], both(XT, lambda a: a[:, k, t * P:(t + 1) * P]),
                                both(WS, lambda a: a[:, k * E:(k + 1) * E]), k == 0, k == KC - 1)
            mm.then_inc(gl_done, 1)

            def product(s, c, n, half, slot, tile):
                back = 3 * c + n - 4
                if back >= 0:
                    reader, steps = ((act_ready, 2), (silu_ready, 1), (us_ready, 1))[n]
                    pe.wait_ge(reader, s - steps + 1)
                if n == 2:
                    at = slice(tile * P, (tile + 1) * P) if isinstance(tile, int) else bass.ds(tile * P, P)
                    pe.matmul(mix_bank(c, n)[:, :], sel[:, at], wT[:, half * HALF:half * HALF + HALF],
                              start=True, stop=True).then_inc(b_done, 1)
                    return
                for k in range(KC):
                    at = n * 256 + k * P
                    mm = split3(pe, mix_bank(c, n)[:, :], both(W, lambda a: a[:, slot, at:at + P]),
                                both(XT, lambda a: a[:, k, half * HALF:half * HALF + HALF]),
                                k == 0, k == KC - 1)
                mm.then_inc((g_done, u_done)[n], 1)

            def down(s, half, slot):
                pe.wait_ge(act_lo, s + 1)
                for r in range(4):
                    t = 4 * half + r
                    mm = split3(pe, bank[t // 2][:, (t % 2) * 256:(t % 2) * 256 + 256],
                                both(CT, lambda a: a[:, half, r * P:(r + 1) * P]),
                                both(W, lambda a: a[:, slot, 512:768]),
                                False, True, skip_group_check=True)
                mm.then_inc(d_done, 1)

            pe.wait_ge(m_lo, 1)
            product(0, 0, 0, 0, 0, 0)
            product(0, 0, 1, 0, 0, 0)
            product(1, 1, 0, 1, 0, 0)
            pe.wait_ge(r_parts, 1)
            for t in range(8):
                mm = pe.transpose(bank[3][:, :].bitcast(BF16)[0:96, t * P:(t + 1) * P], wparts[:, t, :], identb[:, :])
            mm.then_inc(r_turned, 1)
            pe.wait_ge(wT_ready, 1)
            pe.wait_ge(sel_dma, 32)
            product(0, 0, 2, 0, 0, 0)
            product(1, 1, 1, 1, 0, 0)
            product(1, 1, 2, 1, 0, 0)
            for n in range(4):
                pe.matmul(bank[n][:, :], zeros[0:1, 0:P], zeros[0:1, :], start=True, stop=True)
            down(0, 0, 0)
            with pe.Fori(0, (NT - 1) // 2) as i:
                for c in range(2, 6):
                    s, tile, half, slot = 4 * i + c, 2 * i + c // 2, c % 2, (c // 2) % 2
                    if half == 0:
                        pe.wait_ge(m_lo, tile + 1)
                    for n in range(3):
                        product(s, c, n, half, slot, tile)
                    down(s - 1, 1 - half, (slot + 1) % 2 if half == 0 else slot)
            down(2 * NT - 1, 1, (NT - 1) % 2)

        def front_order(eng, evac, split):
            for n in range(IN_V):
                split(n)
            for n in range(len(jobs)):
                evac(n)
                if n in (1, 3, 5, 7):
                    split(IN_V + (n - 1) // 2)

        @block.scalar
        def _(act):
            act.preload_act_table(ACT.Exp)

            def split(n):
                act.wait_ge(in_dma[n], 16)
                act.activation(inputs[n][1][0], inputs[n][0], ACT.Copy).then_inc(in_hi, 1)

            def evac(n):
                kind, c, half, _ = jobs[n]
                if n == 0:
                    act.wait_ge(const_dma, 48)
                act.wait_ge(a_done, n + 1)
                bias, dst = job_bias(kind, c), job_target(kind, c, half)[0]
                if bias is None:
                    act.activation(dst, bank[n % 8][:, :], ACT.Copy).then_inc(a_hi, 1)
                else:
                    act.activation(dst, bank[n % 8][:, :], ACT.Identity, bias=bias).then_inc(a_hi, 1)

            front_order(act, evac, split)

            def exps(dst, src, slot, scale, done):
                for r in range(2):
                    ins = act.activation(dst[:, r * 256:r * 256 + 256], src[:, r * 256:r * 256 + 256], ACT.Exp,
                                         bias=nm[:, slot, r:r + 1], scale=scale, accum_out=sums[:, slot, r:r + 1])
                ins.then_inc(done, 1)

            def w_split(j, count, dst):
                act.wait_ge(stage_dma[j], count)
                act.activation(dst[0], stage[:, j, :], ACT.Copy).then_inc(w_hi, 1)

            for w, wave in enumerate(WAVES):
                for st, b in wave:
                    tok = b * S
                    if st == 0:
                        act.wait_ge(f_nm, b + 1)
                        if b >= 2:
                            act.wait_ge(ft_done, b - 1)
                        exps(ex[:, b % 2, :], bank[FS], b, 1.0 / 16, f_exp)
                    if st == 1:
                        act.wait_ge(ft_done, b + 1)
                        act.activation(PT[0][:, 0, :], bank[FT][:, :], ACT.Copy).then_inc(pt_hi, 1)
                    if st == 2:
                        act.wait_ge(fpv_done, b + 1)
                        for c in range(2):
                            ins = act.activation(CT[0][:, 0, c * 256:c * 256 + 256],
                                                 bank[FPV][:, c * 256:c * 256 + 256],
                                                 ACT.Identity, bias=bqkv[:, 4 + c:5 + c])
                        ins.then_inc(ct_hi, 1)
                        act.wait_ge(e_nm, b + 1)
                        exps(ex[:, 2 + b, :], bank[FES], 4 + b, 1.0, e_exp)
                    if st == 4:
                        act.wait_ge(fxt_done, b + 1)
                        act.activation(AT[0][:, :, tok:tok + S], two(bank[FXT][:, :]), ACT.Copy).then_inc(x1t_hi, 1)
                        act.wait_ge(fet_done, b + 1)
                        act.activation(PT[0][:, 1, :], bank[FET][:, :], ACT.Copy).then_inc(et_hi, 1)
                    if st == 6:
                        act.wait_ge(fnt_done, b + 1)
                        for c in range(2):
                            ins = act.activation(XT[0][:, c, tok:tok + S], bank[FNT][:, c * 256:c * 256 + 256],
                                                 ACT.Copy, scale=lnw[:, c:c + 1])
                        ins.then_inc(xnt_hi, 1)
                for st, b in wave:
                    if st == 5:
                        act.wait_ge(x2_ready, b + 1)
                        act.activation(hid[:, 2 * b:2 * b + 2, :], x2[:, 2 * b:2 * b + 2, :], ACT.Copy)\
                            .then_inc(hid_copied, 1)
                if w == 2:
                    for c in range(FIRST_CHUNKS - 1):
                        w_split(c, 16, first_target(c))

            def qk_high(j, index):
                act.wait_ge(qk_done, index + 1)
                head, half = (j // 4 + 1) % 2, j % 2
                act.activation((Q if j % 4 < 2 else K)[0][:, head, half * HALF:half * HALF + HALF],
                               bank[BANK_QK][:, :], ACT.Copy).then_inc(qk_hi, 1)

            def v_high(q, par, index):
                act.wait_ge(v_done, index + 1)
                act.activation(V[0][:, par, 2 * q:2 * q + 2, :].rearrange("p t h -> p (t h)"),
                               bank[BANK_VO][:, :], ACT.Copy).then_inc(v_hi, 1)

            for b in range(4):
                qk_high(4 + b, b)
                v_high(b, 0, b)
                if b == 1:
                    w_split(FIRST_CHUNKS - 1, 16, first_target(FIRST_CHUNKS - 1))

            def probs_high(m, j):
                act.wait_ge(t_done, m - 1)
                act.activation(PT[0][:, j % 2, 0:384], bank[BANK_T + j % 2][:, 0:384], ACT.Copy).then_inc(t_hi, 1)

            def out_high(m, j):
                act.wait_ge(pv_done, m - 1)
                before = (j - 2) % SP_
                h, half = before // 4, before % 4 // 2
                act.activation(AT[0][:, h, half * HALF:half * HALF + HALF],
                               bank[BANK_PV + (before // 2) % 2][:, :], ACT.Copy).then_inc(at_hi, 1)

            def pair(g, par, first, last):
                for j in range(SP_):
                    m = SP_ * g + j
                    if not (first and j < 2):
                        probs_high(m, j)
                    act.wait_ge(s_masked, m + 1)
                    for at, n, r in ((0, 128, 0), (128, 256, 1)):
                        ins = act.activation(ex[:, j % 4, at:at + n], sm[:, j % 2, at:at + n], ACT.Exp,
                                             bias=nm[:, j, r:r + 1], scale=-1.0, accum_out=sums[:, j, r:r + 1])
                    ins.then_inc(s_exp, 1)
                    if not (last and j >= 4):
                        qk_high(j, SP_ * g + 4 + j)
                    if j >= 4 and not last:
                        v_high(j - 4, 1 - par, 4 * (g + 1) + j - 4)
                    if j % 2 and not (first and j < 2):
                        out_high(m, j)
                    if not last or j in LAST_CHUNKS:
                        if j in (0, 2, 4, 6):
                            act.wait_ge(qk_done, SP_ * g + 4 + j)
                        elif j in (1, 3):
                            act.wait_ge(v_done, 4 * (g + 1))
                        elif not first:
                            act.wait_ge(o_done, 4 * g)
                        w_split(j, 16 * (g + 1 + (j < FIRST_CHUNKS)), chunk_target(j))

            over_pairs(act, pair)
            for j in (0, 1):
                probs_high(SP_ * PAIRS + j, j)
            out_high(SP_ * PAIRS + 1, 1)

            def m_split(t, slot, count):
                act.wait_ge(m_dma[slot], count)
                act.activation(W[0][:, slot, :], raw_moe[:, slot, :], ACT.Copy).then_inc(m_hi, 1)

            act.wait_ge(gate_dma, 16)
            act.activation(WS[0][:, 0:2 * E], gate_raw[:, :, :].rearrange("p k e -> p (k e)"), ACT.Copy)\
                .then_inc(gate_hi, 1)
            m_split(0, 0, 16)
            for b in range(B):
                act.wait_ge(ht_done, b + 1)
                for c in range(2):
                    ins = act.activation(XT[0][:, c, b * S:b * S + S], bank[2][:, c * 256:c * 256 + 256],
                                         ACT.Copy, scale=lnw[:, 2 + c:3 + c])
                ins.then_inc(ht_hi, 1)
            act.wait_ge(r_sub, 1)
            act.activation(gl[:, :, 0:E], gw[:, :, :], ACT.Exp).then_inc(r_exp, 1)
            act.preload_act_table(ACT.Silu)

            def mix(s, c):
                half = c % 2
                act.wait_ge(g_done, s + 1)
                if c >= 2:
                    act.wait_ge(us_ready, s - 1)
                act.activation(ex[:, half, :], mix_bank(c, 0)[:, :], ACT.Silu).then_inc(silu_ready, 1)
                act.wait_ge(act_ready, s + 1)
                if c >= 2:
                    act.wait_ge(d_done, s - 1)
                act.activation(CT[0][:, half, :], ex[:, 4 + half, :], ACT.Copy).then_inc(act_hi, 1)

            mix(0, 0)
            m_split(1, 1, 16)
            mix(1, 1)
            with act.Fori(0, (NT - 1) // 2) as i:
                for c in range(2, 6):
                    s, tile = 4 * i + c, 2 * i + c // 2
                    if c % 2:
                        act.wait_ge(d_done, s - 1)
                        m_split(tile + 1, (c // 2 + 1) % 2, 16 * (i + 1 + (c // 2 + 1) // 2))
                    mix(s, c)

        @block.vector
        def _(dve):
            def low(dst, src, high, done):
                dve.tensor_tensor(dst, src, high.bitcast(F32), ALU.subtract).then_inc(done, 1)

            def split(n):
                dve.wait_ge(in_hi, n + 1)
                low(inputs[n][1][1], inputs[n][0], inputs[n][1][0], in_lo)

            def evac(n):
                kind, c, half, _ = jobs[n]
                dve.wait_ge(a_hi, n + 1)
                bias, (high, lo) = job_bias(kind, c), job_target(kind, c, half)
                if bias is None:
                    low(lo, bank[n % 8][:, :], high, a_lo)
                else:
                    dve.scalar_tensor_tensor(out=lo, in0=bank[n % 8][:, :], scalar=bias, in1=high.bitcast(F32),
                                             op0=ALU.add, op1=ALU.subtract).then_inc(a_lo, 1)

            front_order(dve, evac, split)
            dve.wait_ge(x_dma, 32)
            dve.tensor_tensor(xb[:, :, :], xb[:, :, :], bo[:, :].unsqueeze(1).to_broadcast([P, 8, 256]), ALU.add)\
               .then_inc(xb_ready, 1)

            def negmax(src, slot, scale, peak, done, count):
                dve.tensor_reduce(mx[:, slot, :], two(src), AX_X, ALU.max).then_inc(peak, 1)
                dve.wait_ge(peak, count)
                dve.tensor_scalar(nm[:, slot, :], mx[:, slot, :], -scale, None, ALU.mult).then_inc(done, 1)

            def normalise(dst, slot, inverted, done, count):
                dve.reciprocal(rec[:, slot, :], sums[:, slot, :]).then_inc(inverted, 1)
                dve.wait_ge(inverted, count)
                for r in range(2):
                    ins = dve.tensor_scalar(dst[:, r * 256:r * 256 + 256], dst[:, r * 256:r * 256 + 256],
                                            rec[:, slot, r:r + 1], None, ALU.mult)
                ins.then_inc(done, 1)

            def moments(src, b, added, counted, done):
                dve.wait_ge(added, b + 1)
                for r in range(2):
                    ins = dve.bn_stats(stats[:, 2 * b + r, :], src[:, 2 * b + r, :])
                ins.then_inc(counted, 1)
                dve.wait_ge(counted, b + 1)
                for r in range(2):
                    ins = dve.bn_aggr(mv[:, 2 * b + r, :], stats[:, 2 * b + r, :])
                ins.then_inc(done, 1)

            def centre(dst, src, b, at, done):
                for r in range(2):
                    t = 2 * b + r
                    ins = dve.tensor_scalar(dst[:, t, :], src[:, t, :], mv[:, t, 0:1], rstd[:, at + t:at + t + 1],
                                            ALU.subtract, ALU.mult)
                ins.then_inc(done, 1)

            def squares(src, b, done):
                for r in range(2):
                    t = 2 * b + r
                    ins = dve.tensor_tensor_reduce(out=xb[:, t, :], in0=src[:, t, :], in1=src[:, t, :], scale=1.0,
                                                   scalar=0.0, op0=ALU.mult, op1=ALU.add, accum_out=msq[:, t:t + 1])
                ins.then_inc(done, 1)

            def rms_rows(src, b, done):
                for r in range(2):
                    t = 2 * b + r
                    ins = dve.tensor_scalar(xb[:, t, :], src[:, t, :], rstd[:, 16 + t:17 + t], None, ALU.mult)
                ins.then_inc(done, 1)

            def weighted_low(b, turned, w, done):
                for c in range(2):
                    ins = dve.scalar_tensor_tensor(out=XT[1][:, c, b * S:b * S + S],
                                                   in0=turned[:, c * 256:c * 256 + 256],
                                                   scalar=lnw[:, w + c:w + c + 1],
                                                   in1=XT[0][:, c, b * S:b * S + S].bitcast(F32),
                                                   op0=ALU.mult, op1=ALU.subtract)
                ins.then_inc(done, 1)

            for wave in WAVES:
                for st, b in wave:
                    tok, rows = b * S, slice(2 * b, 2 * b + 2)
                    if st == 0:
                        dve.wait_ge(fs_done, b + 1)
                        negmax(bank[FS][:, :], b, 1.0 / 16, f_max, f_nm, b + 1)
                    if st == 1:
                        dve.wait_ge(pt_hi, b + 1)
                        low(PT[1][:, 0, :], bank[FT][:, :], PT[0][:, 0, :], pt_lo)
                    if st == 2:
                        dve.wait_ge(ct_hi, b + 1)
                        for c in range(2):
                            cols = slice(c * 256, c * 256 + 256)
                            ins = dve.scalar_tensor_tensor(out=CT[1][:, 0, cols], in0=bank[FPV][:, cols],
                                                           scalar=bqkv[:, 4 + c:5 + c],
                                                           in1=CT[0][:, 0, cols].bitcast(F32),
                                                           op0=ALU.add, op1=ALU.subtract)
                        ins.then_inc(ct_lo, 1)
                        dve.wait_ge(fes_done, b + 1)
                        negmax(bank[FES][:, :], 4 + b, 1.0, e_max, e_nm, b + 1)
                    if st == 3:
                        dve.wait_ge(fout_done, b + 1)
                        if b == 0:
                            dve.wait_ge(xb_ready, 1)
                        dve.tensor_tensor(xb[:, rows, :], two(bank[FOUT][:, :]), xb[:, rows, :], ALU.add)\
                           .then_inc(y1_ready, 1)
                        moments(xb, b, y1_ready, y1_stats, y1_var)
                    if st == 4:
                        dve.wait_ge(x1t_hi, b + 1)
                        low(AT[1][:, :, tok:tok + S], two(bank[FXT][:, :]), AT[0][:, :, tok:tok + S], x1t_lo)
                        dve.wait_ge(et_hi, b + 1)
                        low(PT[1][:, 1, :], bank[FET][:, :], PT[0][:, 1, :], et_lo)
                    if st == 5:
                        dve.wait_ge(fxm_done, b + 1)
                        dve.tensor_tensor(hid[:, rows, :], two(bank[FXM][:, :]), hid[:, rows, :], ALU.add)\
                           .then_inc(y2_ready, 1)
                        moments(hid, b, y2_ready, y2_stats, y2_var)
                    if st == 6:
                        dve.wait_ge(xnt_hi, b + 1)
                        weighted_low(b, bank[FNT], 0, xnt_lo)
                for st, b in wave:
                    if st == 0:
                        dve.wait_ge(f_exp, b + 1)
                        normalise(ex[:, b % 2, :], b, f_rec, f_norm, b + 1)
                    if st == 2:
                        dve.wait_ge(e_exp, b + 1)
                        normalise(ex[:, 2 + b, :], 4 + b, e_rec, e_norm, b + 1)
                    if st == 3:
                        dve.wait_ge(y1_rstd, b + 1)
                        centre(hid, xb, b, 0, x1_ready)
                    if st == 5:
                        dve.wait_ge(y2_rstd, b + 1)
                        centre(x2, hid, b, 8, x2_ready)
                        dve.wait_ge(x2_ready, b + 1)
                        squares(x2, b, sq_ready)
                for st, b in wave:
                    if st == 5:
                        dve.wait_ge(rms_rstd, b + 1)
                        rms_rows(x2, b, xn_ready)

            def qk_low(j, index):
                dve.wait_ge(qk_hi, index + 1)
                at = ((j // 4 + 1) % 2, slice(j % 2 * HALF, j % 2 * HALF + HALF))
                high, lo = both(Q if j % 4 < 2 else K, lambda t: t[:, at[0], at[1]])
                low(lo, bank[BANK_QK][:, :], high, qk_lo)

            def v_low(q, par, index):
                dve.wait_ge(v_hi, index + 1)
                high, lo = both(V, lambda t: t[:, par, 2 * q:2 * q + 2, :].rearrange("p t h -> p (t h)"))
                low(lo, bank[BANK_VO][:, :], high, v_lo)

            def probs_low(m, j):
                dve.wait_ge(t_hi, m - 1)
                low(PT[1][:, j % 2, 0:384], bank[BANK_T + j % 2][:, 0:384], PT[0][:, j % 2, 0:384], t_lo)

            def add_o(q, index):
                dve.wait_ge(o_done, index + 1)
                rows = slice(2 * q, 2 * q + 2)
                dve.tensor_tensor(hid[:, rows, :], two(bank[BANK_VO][:, :]), hid[:, rows, :], ALU.add)\
                   .then_inc(o_added, 1)

            def inverse_sums(j):
                dve.reciprocal(rec[:, j, :], sums[:, j, :]).then_inc(s_rec, 1)

            for b in range(4):
                qk_low(4 + b, b)
                v_low(b, 0, b)
            dve.wait_ge(hid_copied, B)

            def pair(g, par, first, last):
                for j in range(SP_):
                    m = SP_ * g + j
                    if first and j == 0:
                        dve.wait_ge(const_ready, 1)
                        dve.wait_ge(s_done, 1)
                    else:
                        dve.wait_ge(s_exp, m)
                        dve.wait_ge(s_done, m + 1)
                        inverse_sums((j - 1) % SP_)
                    for at, n, r in ((0, 128, 0), (128, 256, 1)):
                        ins = dve.tensor_tensor_reduce(out=sm[:, j % 2, at:at + n],
                                                       in0=bank[BANK_S + j % 2][:, at:at + n],
                                                       in1=mask[:, 256 - n:256], scale=-SCALE, scalar=3.0e38,
                                                       op0=ALU.add, op1=ALU.min, accum_out=nm[:, j, r:r + 1])
                    ins.then_inc(s_masked, 1)
                    if not (first and j < 2):
                        probs_low(m, j)
                    if not (last and j >= 4):
                        qk_low(j, SP_ * g + 4 + j)
                    if j < 4 and not first:
                        add_o(j, 4 * (g - 1) + j)
                    if j >= 4 and not last:
                        v_low(j - 4, 1 - par, 4 * (g + 1) + j - 4)
                    if j % 2 and not (first and j < 2):
                        before = (j - 2) % SP_
                        h, half = before // 4, before % 4 // 2
                        dve.wait_ge(at_hi, 4 * g + (j - 1) // 2)
                        high, lo = both(AT, lambda t: t[:, h, half * HALF:half * HALF + HALF])
                        low(lo, bank[BANK_PV + (before // 2) % 2][:, :], high, at_lo)

            over_pairs(dve, pair)
            dve.wait_ge(s_exp, SP_ * PAIRS)
            inverse_sums(SP_ - 1)
            for j in (0, 1):
                probs_low(SP_ * PAIRS + j, j)
            dve.wait_ge(at_hi, 4 * PAIRS)
            high, lo = both(AT, lambda t: t[:, 1, HALF:T])
            low(lo, bank[BANK_PV + 1][:, :], high, at_lo)

            dve.wait_ge(gate_hi, 1)
            low(WS[1][:, 0:2 * E], gate_raw[:, :, :].rearrange("p k e -> p (k e)"), WS[0][:, 0:2 * E], gate_lo)

            def m_low(t, slot):
                dve.wait_ge(m_hi, t + 1)
                low(W[1][:, slot, :], raw_moe[:, slot, :], W[0][:, slot, :], m_lo)

            for b in range(B):
                add_o(b, 4 * LAST + b)
                dve.wait_ge(o_added, 4 * LAST + b + 1)
                squares(hid, b, h_sq)
            for b in range(B):
                dve.wait_ge(h_rstd, b + 1)
                rms_rows(hid, b, h_norm)
            m_low(0, 0)
            for b in range(B):
                dve.wait_ge(ht_hi, b + 1)
                weighted_low(b, bank[2], 2, ht_lo)

            steps = [0]

            def link(ins):
                steps[0] += 1
                ins.then_inc(r_step, 1)
                dve.wait_ge(r_step, steps[0])

            def spread(a, n):
                return a[:, :].unsqueeze(2).to_broadcast([P, 8, n])

            probs = gl[:, :, 0:E]
            dve.wait_ge(gl_done, 1)
            dve.wait_ge(const_ready, 1)
            logits = bank[3][:, 0:8 * E].rearrange("p (t e) -> p t e", e=E)
            link(dve.tensor_reduce(gm[:, :], logits, AX_X, ALU.max))
            ins = dve.tensor_tensor(gw[:, :, :], logits, spread(gm, E), ALU.subtract)
            ins.then_inc(r_sub, 1)
            dve.wait_ge(r_exp, 1)
            link(dve.tensor_reduce(gs[:, :], probs, AX_X, ALU.add))
            link(dve.reciprocal(gr[:, :], gs[:, :]))
            link(dve.tensor_tensor(probs, probs, spread(gr, E), ALU.mult))
            for t in range(8):
                ins = dve.max(g8[:, t, :], gl[:, t, :])
            link(ins)
            link(dve.tensor_reduce(gs[:, :], g8[:, :, 0:TOPK], AX_X, ALU.add))
            link(dve.memset(g8[:, :, TOPK:8], -1.0))
            for t in range(8):
                ins = dve.match_replace(grep[:, t, :], g8[:, t, :], gl[:, t, :], 0.0)
            link(ins)
            link(dve.reciprocal(gr[:, :], gs[:, :]))
            link(dve.tensor_tensor(gw[:, :, :], probs, grep[:, :, 0:E], ALU.subtract))
            link(dve.tensor_tensor(gw[:, :, :], gw[:, :, :], spread(gr, E), ALU.mult))
            link(dve.tensor_copy(wparts[:, :, 0:E], gw[:, :, :]))
            link(dve.tensor_tensor(gt[:, :, :], gw[:, :, :], wparts[:, :, 0:E], ALU.subtract))
            link(dve.tensor_copy(wparts[:, :, 32:32 + E], gt[:, :, :]))
            link(dve.tensor_tensor(gt[:, :, :], gt[:, :, :], wparts[:, :, 32:32 + E], ALU.subtract))
            dve.tensor_copy(wparts[:, :, 64:64 + E], gt[:, :, :]).then_inc(r_parts, 1)
            dve.wait_ge(r_turned, 1)
            dve.tensor_copy(wT[:, :], bank[3][:, :].bitcast(BF16)[0:96, :]).then_inc(wT_ready, 1)

            def mix(s, c, tile=None):
                half = c % 2
                dve.wait_ge(silu_ready, s + 1)
                dve.wait_ge(u_done, s + 1)
                dve.tensor_tensor(ex[:, 2 + half, :], mix_bank(c, 1)[:, :], ex[:, half, :], ALU.mult)\
                   .then_inc(us_ready, 1)
                if tile is not None:
                    m_low(tile, tile_slot(c))
                dve.wait_ge(us_ready, s + 1)
                dve.wait_ge(b_done, s + 1)
                dve.tensor_tensor(ex[:, 4 + half, :], mix_bank(c, 2)[:, :], ex[:, 2 + half, :], ALU.mult)\
                   .then_inc(act_ready, 1)
                dve.wait_ge(act_hi, s + 1)
                low(CT[1][:, half, :], ex[:, 4 + half, :], CT[0][:, half, :], act_lo)

            def tile_slot(c):
                return (c // 2 + 1) % 2

            mix(0, 0)
            mix(1, 1, 1)
            with dve.Fori(0, (NT - 1) // 2) as i:
                for c in range(2, 6):
                    mix(4 * i + c, c, 2 * i + c // 2 + 1 if c % 2 else None)

            for b in range(B):
                rows = slice(2 * b, 2 * b + 2)
                dve.wait_ge(hx_ready, 1)
                dve.wait_ge(d_done, 2 * NT - 1 + b // 2)
                dve.tensor_tensor(hid[:, rows, :], two(bank[b][:, :]), x2[:, rows, :], ALU.add).then_inc(z_ready, 1)
                moments(hid, b, z_ready, z_stats, z_var)
            for b in range(B):
                dve.wait_ge(z_rstd, b + 1)
                centre(xb, hid, b, 0, z_out)

        @block.gpsimd
        def _(pool):
            pool.memset(ident[:, :], 0.0).then_inc(pool_step, 1)
            pool.memset(identb[:, :], 0.0).then_inc(pool_step, 1)
            pool.memset(mask[:, :], 0.0).then_inc(pool_step, 1)
            pool.memset(sel[0:32, :], 1.0).then_inc(pool_step, 1)
            pool.memset(mh[:, :], -0.5).then_inc(pool_step, 1)
            pool.memset(zeros[:, :], 0.0).then_inc(pool_step, 1)
            pool.memset(wparts[:, :, :], 0.0).then_inc(pool_step, 1)
            pool.memset(gl[:, :, :], -1.0).then_inc(pool_step, 1)
            pool.wait_ge(pool_step, 8)
            for m in (ident, identb):
                pool.affine_select(out=m[:, :], in_=m[:, :], compare_op=ALU.not_equal, fill=1.0, base=0,
                                   pattern=[[-1, P]], channel_multiplier=1).then_inc(ident_ready, 1)
            pool.affine_select(out=mask[:, 128:256], in_=mask[:, 128:256], compare_op=ALU.is_ge, fill=MASK, base=0,
                               pattern=[[-1, P]], channel_multiplier=1)
            pool.memset(wparts[:, :, E:E + 1], 1.0).then_inc(const_ready, 1)
            pool.affine_select(out=sel[0:32, 0:E * I], in_=sel[0:32, 0:E * I], compare_op=ALU.is_ge, fill=0.0,
                               base=0, pattern=[[1, E * I]], channel_multiplier=-I).then_inc(pool_step, 1)
            pool.wait_ge(pool_step, 9)
            pool.affine_select(out=sel[0:32, 0:E * I], in_=sel[0:32, 0:E * I], compare_op=ALU.is_ge, fill=0.0,
                               base=I - 1, pattern=[[-1, E * I]], channel_multiplier=I)
            pool.affine_select(out=sel[0:32, E * I:], in_=sel[0:32, E * I:], compare_op=ALU.is_equal, fill=0.0,
                               base=-E, pattern=[[0, NT * P - E * I]], channel_multiplier=1).then_inc(sel_ready, 1)

            def inverse_root(src, at, n, scale, eps, eps_done, done, count):
                pool.tensor_scalar(veps[:, at:at + n], src, scale, eps, ALU.mult, ALU.add).then_inc(eps_done, 1)
                pool.wait_ge(eps_done, count)
                pool.tensor_tensor(rstd[:, at:at + n], veps[:, at:at + n], mh[:, 0:n], ALU.pow).then_inc(done, 1)

            def w_low(j, count, dst):
                pool.wait_ge(w_hi, count)
                pool.tensor_tensor(dst[1], stage[:, j, :], dst[0].bitcast(F32), ALU.subtract).then_inc(w_lo, 1)

            for w, wave in enumerate(WAVES):
                for st, b in wave:
                    var = mv[:, 2 * b:2 * b + 2, 1]
                    if st == 3:
                        pool.wait_ge(y1_var, b + 1)
                        inverse_root(var, 2 * b, 2, 1.0, LN_EPS, y1_eps, y1_rstd, b + 1)
                    if st == 5:
                        pool.wait_ge(y2_var, b + 1)
                        inverse_root(var, 8 + 2 * b, 2, 1.0, LN_EPS, y2_eps, y2_rstd, b + 1)
                for st, b in wave:
                    if st == 5:
                        pool.wait_ge(sq_ready, b + 1)
                        inverse_root(msq[:, 2 * b:2 * b + 2], 16 + 2 * b, 2, 1.0 / H, RMS_EPS, rms_eps, rms_rstd, b + 1)
                if w == 2:
                    for c in range(FIRST_CHUNKS - 1):
                        w_low(c, c + 1, first_target(c))
            w_low(FIRST_CHUNKS - 1, FIRST_CHUNKS, first_target(FIRST_CHUNKS - 1))

            def pair(g, par, first, last):
                for j in range(SP_):
                    pool.wait_ge(s_rec, SP_ * g + j + 1)
                    for at, n, r in ((0, 128, 0), (128, 256, 1)):
                        ins = pool.tensor_tensor(ex[:, j % 4, at:at + n], ex[:, j % 4, at:at + n],
                                                 rec[:, j, r:r + 1].to_broadcast([P, n]), ALU.mult)
                    ins.then_inc(s_norm, 1)
                    if not last or j in LAST_CHUNKS:
                        w_low(j, chunks_done(g, j, last), chunk_target(j))

            over_pairs(pool, pair)
            for b in range(B):
                pool.wait_ge(h_sq, b + 1)
                inverse_root(msq[:, 2 * b:2 * b + 2], 16 + 2 * b, 2, 1.0 / H, RMS_EPS, h_eps, h_rstd, b + 1)
            pool.tensor_tensor(x2[:, :, :], hid[:, :, :], x2[:, :, :], ALU.add).then_inc(hx_ready, 1)
            for b in range(B):
                pool.wait_ge(z_var, b + 1)
                inverse_root(mv[:, 2 * b:2 * b + 2, 1], 2 * b, 2, 1.0, LN_EPS, z_eps, z_rstd, b + 1)


def kernel(**inputs):
    import numpy as np
    import concourse.bacc as bacc
    from concourse.bass_utils import run_bass_kernel_spmd

    a = {k: np.asarray(v) for k, v in inputs.items()}
    f32 = np.float32

    def chunks(w):
        return w.reshape(-1, P, w.shape[-1]).transpose(1, 0, 2)

    xT = chunks(a["x"].reshape(T, H).T)
    ctxT = a["ctx_1024"].reshape(T, P).T
    w_qkv = np.stack([chunks(a["L0_attn_w_qkv"][n * H:(n + 1) * H].T).reshape(P, 512) for n in range(3)])
    w_side = np.concatenate([a["L0_xattn_Wq"].T, a["L0_xattn_Wk"].T,
                             chunks(a["L0_attn_w_out"].T).reshape(P, 512)], axis=1)
    b_qkv = a["L0_attn_b_qkv"].reshape(6, P).T
    b_x = np.stack([a["L0_xattn_bq"], a["L0_xattn_bk"]], axis=1)
    ln_w = np.concatenate([a["L0_ffn_ln1_w"].reshape(2, P).T, a["L0_ffn_ln2_w"].reshape(2, P).T], axis=1)

    q = a["L0_ffn_q_w"].reshape(NH, QHD, H)[:, :HD]
    kv = a["L0_ffn_kv_w"]
    k = kv[:NH * HD].reshape(NH, HD, H)
    v = kv[NH * HD:2 * NH * HD].reshape(PAIRS, 2 * HD, H)
    o = a["L0_ffn_o_w"].reshape(H, NH, HD)

    def q_of(n):
        return chunks(q[n].T).reshape(P, 256)

    def k_of(n):
        return chunks(k[n].T).reshape(P, 256)

    def v_of(g, c):
        return v[g].T[c * P:(c + 1) * P]

    def o_of(n):
        return o[:, n].T

    w_first = np.stack([q_of(0), k_of(0), v_of(0, 0), v_of(0, 1), q_of(1)])
    w_heads = np.stack([np.stack([k_of(2 * g + 1), v_of(g + 1, 0), q_of(2 * g + 2), v_of(g + 1, 1),
                                  k_of(2 * g + 2), o_of(2 * g), q_of(2 * g + 3), o_of(2 * g + 1)])
                        for g in range(PAIRS - 1)])
    w_last = np.stack([k_of(NH - 1), o_of(NH - 2), o_of(NH - 1)])

    w1, sh = a["L0_ffn_w1"], a["L0_ffn_sh_gu_w"]
    tiles = NT + 1
    g = np.zeros((tiles * P, H), f32)
    u = np.zeros((tiles * P, H), f32)
    d = np.zeros((tiles * P, H), f32)
    g[:E * I] = w1[:, :I].reshape(E * I, H)
    u[:E * I] = w1[:, I:].reshape(E * I, H)
    d[:E * I] = a["L0_ffn_w2"].transpose(0, 2, 1).reshape(E * I, H)
    g[E * I:FF] = sh[:2 * I]
    u[E * I:FF] = sh[2 * I:]
    d[E * I:FF] = a["L0_ffn_sh_down_w"].T

    def gu_tiles(w):
        return w.reshape(tiles, P, KC, P).transpose(0, 3, 2, 1).reshape(tiles, P, 256)

    w_moe = np.concatenate([gu_tiles(g), gu_tiles(u), d.reshape(tiles, P, H)], axis=2)
    gateT = chunks(a["L0_ffn_gate_w"].T)

    nc = bacc.Bacc("TRN2", target_bir_lowering=False, num_devices=1)
    given = dict(x=a["x"], xT=xT, ctxT=ctxT, w_qkv=w_qkv, w_side=w_side, b_qkv=b_qkv,
                 b_out=a["L0_attn_b_out"], b_x=b_x, ln_w=ln_w, w_heads_first=w_first, w_heads=w_heads,
                 w_last=w_last, w_moe=w_moe, gateT=gateT)
    given = {n: np.ascontiguousarray(w) for n, w in given.items()}
    args = {n: nc.dram_tensor(n, w.shape, mybir.dt.from_np(w.dtype), kind="ExternalInput").ap()
            for n, w in given.items()}
    out = nc.dram_tensor("out", (B, S, H), F32, kind="ExternalOutput").ap()
    program(nc, *args.values(), out)
    return run_bass_kernel_spmd(nc, [given], core_ids=[0]).results[0]["out"]
```

```python
from contextlib import ExitStack

import concourse.bass as bass
from concourse import mybir

F32 = mybir.dt.float32
F32R = mybir.dt.float32r
BF16 = mybir.dt.bfloat16
ALU = mybir.AluOpType
ACT = mybir.ActivationFunctionType
AX_X = mybir.AxisListType.X

P = 128
B, S, H = 4, 256, 256
T = B * S
HALF = T // 2
KC = H // P
NH, QHD, HD = 16, 192, 128
PAIRS = NH // 2
SP_ = 8
E, TOPK, I = 16, 4, 176
FF = E * I + 2 * I
NT = (FF + P - 1) // P
LN_EPS, RMS_EPS = 1e-5, 1e-6
SCALE = float(QHD) ** -0.5
MASK = -1e9 / SCALE


def program(nc, x, xT, ctxT, w_qkv, w_side, b_qkv, b_out, b_x, ln_w, w_heads_first, w_heads, w_last,
            w_moe, gateT, out):
    with ExitStack() as ctx:
        def sb(name, shape, dt=F32):
            return ctx.enter_context(nc.sbuf_tensor(name, shape, dt))

        def sem(name):
            return ctx.enter_context(nc.semaphore(name))

        def parts(name, shape):
            return sb(name + "_hi", shape, F32R), sb(name + "_lo", shape, F32R)

        XT = parts("XT", [P, KC, T])
        Q = parts("Q", [P, 2, T])
        K = parts("K", [P, 2, T])
        V = parts("V", [P, 2, 8, 256])
        AT = parts("AT", [P, 2, T])
        W = parts("W", [P, 2, 768])
        WS = parts("WS", [P, 768])
        PT = parts("PT", [P, 2, 512])
        CT = parts("CT", [P, 2, 512])
        hid = sb("hid", [P, 8, 256])
        x2 = sb("x2", [P, 8, 256])
        xb = sb("xb", [P, 8, 256])
        stage = sb("stage", [P, 8, 256])
        ex = sb("ex", [P, 8, 512])
        sm = sb("sm", [P, 2, 384])
        mask = sb("mask", [P, 256])
        ident = sb("ident", [P, P])
        identb = sb("identb", [P, P], BF16)
        bqkv = sb("bqkv", [P, 6])
        bxs = sb("bxs", [P, 2])
        lnw = sb("lnw", [P, 4])
        bo = sb("bo", [P, 256])
        zeros = sb("zeros", [1, 512], BF16)
        mh = sb("mh", [P, 2])
        mx = sb("mx", [P, 8, 2])
        nm = sb("nm", [P, 8, 2])
        sums = sb("sums", [P, 8, 2])
        rec = sb("rec", [P, 8, 2])
        c_nm = sb("c_nm", [P, 8, 2])
        c_sums = sb("c_sums", [P, 8, 2])
        c_rec = sb("c_rec", [P, 8, 2])
        stats = sb("stats", [P, 8, 6])
        mv = sb("mv", [P, 8, 2])
        veps = sb("veps", [P, 24])
        rstd = sb("rstd", [P, 24])
        msq = sb("msq", [P, 16])
        shift = sb("shift", [P, 8])
        gate_raw = sb("gate_raw", [P, 2, E])
        gl = sb("gl", [P, 8, E + TOPK])
        gm = sb("gm", [P, 8])
        gs = sb("gs", [P, 8])
        gr = sb("gr", [P, 8])
        g8 = sb("g8", [P, 8, 8])
        grep = sb("grep", [P, 8, E + TOPK])
        gw = sb("gw", [P, 8, E])
        gt = sb("gt", [P, 8, E])
        wparts = sb("wparts", [P, 8, 96], BF16)
        wT = sb("wT", [96, T], BF16)
        sel = sb("sel", [96, NT * P], BF16)

        bank = [ctx.enter_context(nc.psum_tensor(f"bank{i}", [P, 512], F32)) for i in range(8)]

        def split3(pe, acc, lhs, rhs, first, last, **kw):
            for n, (a, b) in enumerate(((0, 0), (0, 1), (1, 0))):
                mm = pe.matmul(acc, lhs[a], rhs[b], start=first and n == 0, stop=last and n == 2, **kw)
            return mm

        def both(t, f):
            return f(t[0]), f(t[1])

        in_dma = [sem(f"in_dma{i}") for i in range(8)]
        const_dma, x_dma = sem("const_dma"), sem("x_dma")
        ident_ready, const_ready, xb_ready = sem("ident_ready"), sem("const_ready"), sem("xb_ready")
        in_hi, in_lo = sem("in_hi"), sem("in_lo")
        a_done, a_hi, a_lo = sem("a_done"), sem("a_hi"), sem("a_lo")
        fs_done, ft_done, fpv_done, fes_done = sem("fs_done"), sem("ft_done"), sem("fpv_done"), sem("fes_done")
        fout_done, fxt_done, fet_done = sem("fout_done"), sem("fxt_done"), sem("fet_done")
        fxm_done, fnt_done = sem("fxm_done"), sem("fnt_done")
        f_max, f_nm, f_exp, f_rec, f_norm = sem("f_max"), sem("f_nm"), sem("f_exp"), sem("f_rec"), sem("f_norm")
        e_max, e_nm, e_exp, e_rec, e_norm = sem("e_max"), sem("e_nm"), sem("e_exp"), sem("e_rec"), sem("e_norm")
        pt_hi, pt_lo, ct_hi, ct_lo = sem("pt_hi"), sem("pt_lo"), sem("ct_hi"), sem("ct_lo")
        x1t_hi, x1t_lo, et_hi, et_lo = sem("x1t_hi"), sem("x1t_lo"), sem("et_hi"), sem("et_lo")
        y1_ready, y1_stats, y1_var, y1_eps, y1_rstd = (sem(f"y1_{n}") for n in ("ready", "stats", "var", "eps", "rstd"))
        y2_ready, y2_stats, y2_var, y2_eps, y2_rstd = (sem(f"y2_{n}") for n in ("ready", "stats", "var", "eps", "rstd"))
        rms_eps, rms_rstd = sem("rms_eps"), sem("rms_rstd")
        pool_step, sel_ready, sel_dma = sem("pool_step"), sem("sel_ready"), sem("sel_dma")
        x1_ready, x2_ready, sq_ready, hid_copied = sem("x1_ready"), sem("x2_ready"), sem("sq_ready"), sem("hid_copied")
        xn_ready, xnt_hi, xnt_lo = sem("xn_ready"), sem("xnt_hi"), sem("xnt_lo")
        stage_dma = [sem(f"stage_dma{j}") for j in range(SP_)]
        w_hi, w_lo = sem("w_hi"), sem("w_lo")
        s_done, s_masked, s_exp, s_rec, s_norm = (
            sem("s_done"), sem("s_masked"), sem("s_exp"), sem("s_rec"), sem("s_norm"))
        t_done, t_hi, t_lo = sem("t_done"), sem("t_hi"), sem("t_lo")
        qk_done, qk_hi, qk_lo = sem("qk_done"), sem("qk_hi"), sem("qk_lo")
        v_done, v_hi, v_lo = sem("v_done"), sem("v_hi"), sem("v_lo")
        o_done, o_added = sem("o_done"), sem("o_added")
        pv_done, at_hi, at_lo = sem("pv_done"), sem("at_hi"), sem("at_lo")
        gate_dma, gate_hi, gate_lo = sem("gate_dma"), sem("gate_hi"), sem("gate_lo")
        h_sq, h_eps, h_rstd, h_norm = sem("h_sq"), sem("h_eps"), sem("h_rstd"), sem("h_norm")
        ht_done, ht_hi, ht_lo, gl_done = sem("ht_done"), sem("ht_hi"), sem("ht_lo"), sem("gl_done")
        r_max, r_sub, r_exp, r_step, r_parts, r_turned, wT_ready = (
            sem("r_max"), sem("r_sub"), sem("r_exp"), sem("r_step"), sem("r_parts"), sem("r_turned"), sem("wT_ready"))
        m_dma = [sem("m_dma0"), sem("m_dma1")]
        m_hi, m_lo = sem("m_hi"), sem("m_lo")
        g_done, u_done, b_done, d_done = sem("g_done"), sem("u_done"), sem("b_done"), sem("d_done")
        silu_ready, us_ready, act_ready, act_hi, act_lo = (
            sem("silu_ready"), sem("us_ready"), sem("act_ready"), sem("act_hi"), sem("act_lo"))
        hx_ready = sem("hx_ready")
        d_last, z_shift = sem("d_last"), sem("z_shift")
        z_out_late = sem("z_out_late")
        lt_done, lt_copied = sem("lt_done"), sem("lt_copied")
        z_ready, z_stats, z_var, z_eps, z_rstd, z_out, out_dma = (
            sem("z_ready"), sem("z_stats"), sem("z_var"), sem("z_eps"), sem("z_rstd"), sem("z_out"), sem("out_dma"))

        block = ctx.enter_context(nc.Block())

        x_rows = x.rearrange("b (c p) h -> p (b c) h", p=P)
        out_rows = out.rearrange("b (c p) h -> b p c h", p=P)
        raw_xT = hid[:, :, :].rearrange("p (k t) h -> p k (t h)", k=KC)
        raw_ctx = x2[:, 0:4, :].rearrange("p t h -> p (t h)")
        raw_side = x2[:, 4:7, :].rearrange("p t h -> p (t h)")
        raw_moe = stage[:, 0:6, :].rearrange("p (s c) h -> p s (c h)", s=2)
        ctx_parts = both(V, lambda t: t[:, 1, 0:4, :].rearrange("p t h -> p (t h)"))
        xq_parts = both(V, lambda t: t[:, 1, 4:8, :].rearrange("p t h -> p (t h)"))
        xk_parts = both(XT, lambda t: t[:, 0, :])
        WV = both(W, lambda t: t[:, 0, 0:512].rearrange("p (k n) -> p k n", k=KC))
        WQ = both(W, lambda t: t[:, 0, 512:768].rearrange("p (k n) -> p k n", k=KC))
        WK = both(W, lambda t: t[:, 1, 0:256].rearrange("p (k n) -> p k n", k=KC))
        WO = both(W, lambda t: t[:, 1, 256:768].rearrange("p (h n) -> p h n", h=2))

        def qkv_at(t, part):
            return t[:, :, :].rearrange("p s n -> p (s n)")[:, part * 512:(part + 1) * 512]

        stage_flat = stage[:, :, :].rearrange("p s n -> p (s n)")
        inputs = (
            [(raw_xT[:, :, 0:HALF], both(XT, lambda t: t[:, :, 0:HALF]), xT[:, :, 0:HALF])]
            + [(stage_flat[:, n * 512:(n + 1) * 512], both(W, lambda t, n=n: qkv_at(t, n)), w_qkv[n, :, :])
               for n in range(3)]
            + [(raw_ctx, ctx_parts, ctxT[:, :]),
               (raw_side[:, 0:256], both(WS, lambda t: t[:, 0:256]), w_side[:, 0:256]),
               (raw_xT[:, :, HALF:T], both(XT, lambda t: t[:, :, HALF:T]), xT[:, :, HALF:T]),
               (raw_side[:, 256:768], both(WS, lambda t: t[:, 256:768]), w_side[:, 256:768])])
        IN_X0, IN_Q, IN_K, IN_V, IN_CTX, IN_SIDE, IN_X1, IN_OUT = range(1, 9)

        jobs = [(kind, c, half, max(need, IN_X1 if half else 0))
                for half in range(2)
                for kind, need, count in (("q", IN_Q, 2), ("k", IN_K, 2), ("v", IN_V, 2),
                                          ("xq", IN_SIDE, 1), ("xk", IN_SIDE, 1))
                for c in range(count)]

        def jobs_until(kind, half):
            return max(n + 1 for n, job in enumerate(jobs) if job[0] == kind and job[2] == half)

        def job_target(kind, c, half):
            cols = slice(half * HALF, (half + 1) * HALF)
            if kind in "qk":
                return both(Q if kind == "q" else K, lambda t: t[:, c, cols])
            if kind == "v":
                r = 4 * half + 2 * c
                return both(V, lambda t: t[:, 0, r:r + 2, :].rearrange("p t h -> p (t h)"))
            return both(xq_parts if kind == "xq" else xk_parts, lambda t: t[:, cols])

        def job_bias(kind, c):
            return {"q": bqkv[:, c:c + 1], "k": bqkv[:, 2 + c:3 + c], "v": None,
                    "xq": bxs[:, 0:1], "xk": bxs[:, 1:2]}[kind]

        FRONT = """
            input 0, input 1, input 2, input 3, input 4, job 0, input 5, job 1, job 2, split 0, input 6, job 3,
            split 1, input 7, split 2, job 4, split 3, split 4, job 5, scores 0, job 6, split 5, job 7, peak 0,
            split 6, exps 0, norm 0, job 8, split 7, job 9, scores 1, split 8, peak 1, turn 0, pt 0, split 9,
            cross 0, job 10, exps 1, norm 1, context 0, cross_peak 0, job 11, split 10, ct 0, split 11, turn 1,
            job 12, cross_exps 0, project 0, x_bias 0, pt 1, cross_norm 0, y1 0, split 12, job 13, split 13,
            context 1, scores 2, y1_root 0, x1 0, cross_turn 0, x1_turn 0, peak 2, ct 1, cross 1, cross_pt 0,
            exps 2, cross_peak 1, x1t 0, cross_exps 1, project 1, norm 2, y1 1, cross_norm 1, mix 0, y2 0, turn 2,
            scores 3, y1_root 1, pt 2, peak 3, cross_turn 1, y2_root 0, context 2, weights 0, x1 1, x2 0,
            cross_pt 1, weights 1, exps 3, ct 2, x1_turn 1, x1t 1, squares 0, rms 0, job 14, split 14, job 15,
            mix 1, split 15, xn 0, xn_turn 0, norm 3, turn 3, project 2, y2 1, xnt 0, pt 3, keep 0, y2_root 1,
            cross 2, weights 2, weights 3, x2 1, cross_peak 2, squares 1, y1 2, rms 1, cross_exps 2, context 3,
            y1_root 2, ct 3, xn 1, cross_norm 2, v 0, weights 4, x1 2, xn_turn 1, xnt 1, project 3, cross_turn 2,
            weights 5, y1 3, cross_pt 2, x1_turn 2, x1t 2, cross 3, qk 0, y1_root 3, cross_peak 3, qk_split 0,
            mix 2, qk 1, x1 3, cross_exps 3, x1_turn 3, cross_norm 3, y2 2, qk_split 1, x1t 3, cross_turn 3,
            cross_pt 3, y2_root 2, head_scores 0, head_mask 0, x2 2, head_scores 1, mix 3, head_exps 0, head_mask 1,
            head_inverse 0, qk 2, squares 2, head_norm 0, rms 2, y2 3, v_split 0, head_turn 0, y2_root 3,
            qk_split 2, x2 3, xn 2, xn_turn 2, head_exps 1, head_probs 0, qk 3, v 1, squares 3, xnt 2,
            head_values 0, head_inverse 1, qk_split 3, rms 3, xn 3, v_split 1, xn_turn 3, head_norm 1, keep 1,
            xnt 3, head_scores 2, v 2, v_split 2, head_mask 2, qk 4, head_turn 1, v 3, qk_split 4, head_exps 2,
            keep 2, head_inverse 2, qk 5, head_norm 2, head_probs 1, head_scores 3, qk_split 5, weights 6,
            head_turn 2, head_mask 3, head_values 1, head_probs 2, head_exps 3, qk 6, head_inverse 3, head_scores 4,
            head_norm 3, qk_split 6, head_scores 5, head_mask 4, weights 7, v_split 3, qk 7, weights 8, head_exps 4,
            head_turn 3, head_mask 5, v 4, qk_split 7, head_inverse 4, qk 8, qk_split 8, head_values 2,
            head_scores 6, weights 9, head_norm 4, head_mask 6, v_split 4, head_exps 5, weights 10, head_scores 7,
            qk 9, head_probs 3, weights 11, qk_split 9, v 5, head_attn 0, head_inverse 5, weights 12, head_turn 4,
            v_split 5, head_values 3, head_probs 4, head_exps 6, qk 10, head_inverse 6, v 6, head_norm 5,
            head_attn 1, qk_split 10, head_mask 7, head_values 4, head_turn 5, v_split 6, head_probs 5, head_exps 7,
            qk 11, v 7, keep 3, qk_split 11, head_values 5, v_split 7, head_norm 6, head_attn 2
        """
        FRONT = [(part.split()[0], int(part.split()[1])) for part in FRONT.split(",")]

        def before(at, kind):
            return sum(k == kind for k, _ in FRONT[:at])

        def before_with(at, kind, parity):
            return max((n + 1 for k, n in FRONT[:at] if k == kind and n % 2 == parity), default=0)

        FIRST_STEPS = ((0, 0), (0, 1), (1, 0), (1, 1), (0, 2), (0, 3), (1, 2), (1, 3))
        PIECES = tuple((h, qk, half, need) for half in range(2)
                       for h, qk, need in ((0, "q", 1), (0, "k", 2), (1, "q", 5), (1, "k", 6)))
        PIECES += tuple((0, qk, half, need) for qk, need in (("q", 8), ("k", 10)) for half in range(2))

        FJ, FS, FT, FPV, FES, FET = (5, 6, 7), 0, 1, 2, 3, 4
        FOUT, FXT, FXM, FNT = FS, FT, FPV, FES

        def chain_ex(b):
            return ex[:, 6 + b % 2, :]

        def two(ap):
            return ap.rearrange("p (t h) -> p t h", t=2)

        FIRST_CHUNKS = 5
        BANK_QK, BANK_VO, BANK_PV, BANK_T, BANK_S = 5, 6, (7, 4), (0, 1), (2, 3)
        LAST = PAIRS - 1
        LAST_CHUNKS = (0, 5, 7)

        def chunks_done(g, j, last=False):
            if last:
                return FIRST_CHUNKS + SP_ * LAST + LAST_CHUNKS.index(j) + 1
            return FIRST_CHUNKS + SP_ * g + j + 1

        def chunk_target(j):
            return {0: both(WK, lambda t: t[:, :, :]), 4: both(WK, lambda t: t[:, :, :]),
                    2: both(WQ, lambda t: t[:, :, :]), 6: both(WQ, lambda t: t[:, :, :]),
                    1: both(WV, lambda t: t[:, 0, :]), 3: both(WV, lambda t: t[:, 1, :]),
                    5: both(WO, lambda t: t[:, 0, :]), 7: both(WO, lambda t: t[:, 1, :])}[j]

        FIRST_PLACES = (2, 0, 1, 3, 7, 5, 1, 2, 3, 4, 5, 6, 7)
        FIRST_SLOTS = (0, 1, 2, 3, 4, 0, 1, 2, 3, 4, 5, 6, 7)

        def first_target(c):
            return chunk_target(FIRST_PLACES[c])

        TAIL = """
            vbusy 0, abusy 0, inverse 59, scores 60, o_weights 0, norm 59, turn 58, mask 60, o_weights 1, scores 61,
            mask 61, probs 58, gate 0, exps 60, inverse 60, scores 62, mask 62, turn 59, scores 63, exps 61,
            inverse 61, probs 59, norm 60, norm 61, exps 62, values 58, turn 60, mask 63, values 59, inverse 62,
            probs 60, exps 63, turn 61, inverse 63, norm 62, probs 61, norm 63, values 60, attn 59, turn 62,
            values 61, turn 63, attn 60, probs 62, out 0, attn 61, values 62, add 0, probs 63, out 1, attn 62,
            values 63, squares 0, rms 0, add 1, out 2, attn 63, xn 0, squares 1, add 2, out 3, squares 2, rms 1,
            xn 1, add 3, xn_turn 0, xnt 0, rms 2, xn_turn 1, logits 0, xn 2, squares 3, xnt 1, rms 3, xn 3,
            xn_turn 2, logits_copy 0, logits 1, xn_turn 3, xnt 2, logits_turn 0, logits_copy 1, logits_turn 1,
            xnt 3, logits 2, logits_copy 2, tile 0, logits 3, logits_turn 2, logits_copy 3, logits_turn 3, g 0, u 0,
            router 0, silu 0, g 1, u 1, silu 1, hx 0, weights_turn 0
        """
        TAIL = [(part.split()[0], int(part.split()[1])) for part in TAIL.split(",")]
        M = SP_ * PAIRS
        HEAD_STEPS = 4
        M0 = M - HEAD_STEPS
        LATE_PV = {M0 - 2: 4, M0 - 1: 4, M0: 7, M0 + 1: 5, M0 + 2: 4, M0 + 3: 7}
        LATE_OUT, LATE_TURN, LATE_LOGITS_T, LATE_LOGITS, LATE_WT = (6, 3), (0, 1), 2, 6, 3

        def logits_T(n):
            return (bank[LATE_LOGITS_T][0:E, n % 2 * 256:n % 2 * 256 + 256],
                    ex[0:E, 4 + n // 2, n % 2 * 256:n % 2 * 256 + 256])

        def at_count(m):
            return m // 2 + 1 if m < M0 else M0 // 2 + m - M0 + 1

        def late_out(t, m):
            if m < M0:
                return t[:, 0, HALF:T]
            return t[:, 1, (m - M0) * S:(m - M0 + 1) * S]

        def late_pv(m):
            return bank[LATE_PV[m]][:, 0:512 if m < M0 else 256]

        def over_pairs(eng, pair):
            with eng.Fori(0, (PAIRS - 2) // 2) as i:
                for n in range(2):
                    pair(2 * i + 1 + n, (1 + n) % 2, False, False)
            pair(LAST, LAST % 2, False, True)

        def mix_bank(s, n):
            return bank[4 + (3 * s + n) % 4]

        @block.sync
        def _(sp):
            for n, (raw, _, src) in enumerate(inputs):
                sp.dma_start(raw, src).then_inc(in_dma[n], 16)
                if n == 1:
                    sp.dma_start(bqkv[:, :], b_qkv).then_inc(const_dma, 16)
                    sp.dma_start(bxs[:, :], b_x).then_inc(const_dma, 16)
                    sp.dma_start(lnw[:, :], ln_w).then_inc(const_dma, 16)
            sp.dma_start(xb[:, :, :], x_rows).then_inc(x_dma, 16)
            sp.dma_start(bo[:, :], b_out.partition_broadcast(P)).then_inc(x_dma, 16)
            sp.dma_start(gate_raw[:, :, :], gateT).then_inc(gate_dma, 16)
            sp.wait_ge(in_lo, IN_V)
            for c in range(FIRST_CHUNKS):
                sp.dma_start(stage[:, c, :], w_heads_first[c, :, :]).then_inc(stage_dma[c], 16)

            def load(g, j, src):
                sp.dma_start(stage[:, j, :], src).then_inc(stage_dma[j], 16)

            for j in range(SP_):
                if j < FIRST_CHUNKS:
                    sp.wait_ge(w_lo, j + 1)
                load(0, j, w_heads[0, j, :, :])
            with sp.Fori(1, PAIRS - 1) as g:
                for j in range(SP_):
                    sp.wait_ge(w_lo, FIRST_CHUNKS + SP_ * (g - 1) + j + 1)
                    load(g, j, w_heads[bass.ds(g, 1), j, :, :].rearrange("g p n -> p (g n)"))
            for n, j in enumerate(LAST_CHUNKS):
                sp.wait_ge(w_lo, chunks_done(LAST - 1, j))
                load(LAST, j, w_last[n, :, :])

            sp.wait_ge(sel_ready, 1)
            for n in (32, 64):
                sp.dma_start(sel[n:n + 32, :], sel[0:32, :]).then_inc(sel_dma, 16)

            for t in range(2):
                sp.wait_ge(w_lo, chunks_done(LAST, (0, 5)[t], True))
                sp.dma_start(raw_moe[:, t, :], w_moe[t, :, :]).then_inc(m_dma[t], 16)
            with sp.Fori(1, (NT + 1) // 2) as i:
                for n in range(2):
                    sp.wait_ge(m_lo, 2 * i + n - 1)
                    sp.dma_start(raw_moe[:, n, :],
                                 w_moe[bass.ds(2 * i + n, 1), :, :].rearrange("g p n -> p (g n)"))\
                        .then_inc(m_dma[n], 16)
            for b in range(B):
                if b < 2:
                    sp.wait_ge(z_out, b + 1)
                else:
                    sp.wait_ge(z_out_late, b - 1)
                sp.dma_start(out_rows[b, :, :, :], xb[:, 2 * b:2 * b + 2, :]).then_inc(out_dma, 16)
            sp.wait_ge(out_dma, 16 * B)

        @block.tensor
        def _(pe):
            def turn(dst, src):
                for n, s in enumerate(src):
                    mm = pe.transpose(dst[:, n * P:(n + 1) * P], s, ident[:, :])
                return mm

            def blocks(t):
                return [t(r)[:, c * P:(c + 1) * P] for c in range(2) for r in range(2)]

            def flat(t):
                return t[:, :, :].rearrange("p s n -> p (s n)")

            def first_product(n):
                kind, c, half, need = jobs[n]
                dst = bank[FJ[n % 3]]
                pe.wait_ge(in_lo, need)
                if n >= 3:
                    pe.wait_ge(a_lo, n - 2)
                cols = slice(half * HALF, (half + 1) * HALF)
                if kind in "qk":
                    for k in range(KC):
                        at = (0 if kind == "q" else 512) + k * 256 + c * P
                        mm = split3(pe, dst[:, :], both(W, lambda t: flat(t)[:, at:at + P]),
                                    both(XT, lambda t: t[:, k, cols]), k == 0, k == KC - 1)
                elif kind == "v":
                    for r in range(2):
                        tok = (4 * half + 2 * c + r) * P
                        for k in range(KC):
                            at = 1024 + k * 256
                            mm = split3(pe, dst[:, r * 256:r * 256 + 256], both(XT, lambda t: t[:, k, tok:tok + P]),
                                        both(W, lambda t: flat(t)[:, at:at + 256]), k == 0, k == KC - 1)
                else:
                    at = 0 if kind == "xq" else P
                    mm = split3(pe, dst[:, :], both(WS, lambda t: t[:, at:at + P]),
                                both(ctx_parts, lambda t: t[:, cols]), True, True)
                mm.then_inc(a_done, 1)

            def rows_of(count, dst, lhs, rhs):
                for r in range(2):
                    for k in range(count):
                        mm = split3(pe, dst[:, r * 256:r * 256 + 256], both(lhs[0], lambda t: lhs[1](t, r, k)),
                                    both(rhs[0], lambda t: rhs[1](t, k)), k == 0, k == count - 1)
                return mm

            def free(at, kind, sem_, own=""):
                if before(at, kind):
                    pe.wait_ge(sem_, before(at, kind))

            def free_of_heads(at, kind, parity, sem_):
                if before_with(at, kind, parity):
                    pe.wait_ge(sem_, before_with(at, kind, parity))

            def front_step(at, kind, b):
                tok = b * S
                if kind == "job":
                    first_product(b)
                if kind == "scores":
                    pe.wait_ge(a_lo, jobs_until("k", b // 2))
                    free(at, "scores", f_exp)
                    free(at, "project", y1_ready)
                    free_of_heads(at, "head_turn", 0, t_lo)
                    rows_of(KC, bank[FS], (Q, lambda t, r, k: t[:, k, tok + r * P:tok + r * P + P]),
                            (K, lambda t, k: t[:, k, tok:tok + S])).then_inc(fs_done, 1)
                if kind == "turn":
                    pe.wait_ge(f_norm, b + 1)
                    pe.wait_ge(ident_ready, 2)
                    free(at, "turn", pt_lo)
                    free(at, "x1_turn", x1t_lo)
                    free_of_heads(at, "head_turn", 1, t_lo)
                    turn(bank[FT], blocks(lambda r: chain_ex(b)[:, r * 256:r * 256 + 256])).then_inc(ft_done, 1)
                if kind == "context":
                    pe.wait_ge(pt_lo, b + 1)
                    pe.wait_ge(a_lo, jobs_until("v", b // 2))
                    free(at, "context", ct_lo)
                    free(at, "mix", y2_ready)
                    free_of_heads(at, "head_scores", 0, s_masked)
                    rows_of(2, bank[FPV], (V, lambda t, c, k: t[:, 0, 2 * b + k, c * P:c * P + P]),
                            (PT, lambda t, k: t[:, 0, k * 256:k * 256 + 256])).then_inc(fpv_done, 1)
                if kind == "cross":
                    pe.wait_ge(a_lo, jobs_until("xk", b // 2))
                    free(at, "cross", e_exp)
                    free(at, "xn_turn", xnt_lo)
                    free_of_heads(at, "head_scores", 1, s_masked)
                    rows_of(1, bank[FES], (xq_parts, lambda t, r, k: t[:, tok + r * P:tok + r * P + P]),
                            (xk_parts, lambda t, k: t[:, tok:tok + S])).then_inc(fes_done, 1)
                if kind == "project":
                    pe.wait_ge(ct_lo, b + 1)
                    pe.wait_ge(in_lo, IN_OUT)
                    free(at, "scores", f_exp)
                    free(at, "project", y1_ready)
                    free_of_heads(at, "head_turn", 0, t_lo)
                    rows_of(KC, bank[FOUT], (CT, lambda t, r, k: t[:, 0, k * 256 + r * P:k * 256 + r * P + P]),
                            (WS, lambda t, k: t[:, 256 + k * 256:512 + k * 256])).then_inc(fout_done, 1)
                if kind == "x1_turn":
                    pe.wait_ge(x1_ready, b + 1)
                    free(at, "turn", pt_lo)
                    free(at, "x1_turn", x1t_lo)
                    free_of_heads(at, "head_turn", 1, t_lo)
                    turn(bank[FXT], blocks(lambda r: hid[:, 2 * b + r, :])).then_inc(fxt_done, 1)
                if kind == "cross_turn":
                    pe.wait_ge(e_norm, b + 1)
                    free(at, "cross_turn", et_lo)
                    if before(at, "head_values") > 2:
                        pe.wait_ge(at_lo, 2)
                    turn(bank[FET], blocks(lambda r: ex[:, 2 + b, r * 256:r * 256 + 256])).then_inc(fet_done, 1)
                if kind == "mix":
                    pe.wait_ge(x1t_lo, b + 1)
                    pe.wait_ge(et_lo, b + 1)
                    free(at, "context", ct_lo)
                    free(at, "mix", y2_ready)
                    free_of_heads(at, "head_scores", 0, s_masked)
                    rows_of(2, bank[FXM], (AT, lambda t, r, k: t[:, k, tok + r * P:tok + r * P + P]),
                            (PT, lambda t, k: t[:, 1, k * 256:k * 256 + 256])).then_inc(fxm_done, 1)
                if kind == "xn_turn":
                    pe.wait_ge(xn_ready, b + 1)
                    free(at, "cross", e_exp)
                    free(at, "xn_turn", xnt_lo)
                    free_of_heads(at, "head_scores", 1, s_masked)
                    turn(bank[FNT], blocks(lambda r: xb[:, 2 * b + r, :])).then_inc(fnt_done, 1)
                if kind == "qk":
                    h, qk, half, need = PIECES[b]
                    pe.wait_ge(xnt_lo, 2 * half + 2)
                    pe.wait_ge(a_lo, len(jobs))
                    second = both(WO, lambda t: t[:, "kq".index(qk), :].rearrange("p (k n) -> p k n", k=KC))
                    project_piece(second if h else WQ if qk == "q" else WK, half, b, need)
                if kind == "v":
                    pe.wait_ge(xnt_lo, b % 4 + 1)
                    pe.wait_ge(w_lo, 4 if b < 4 else 9)
                    pe.wait_ge(a_lo, len(jobs))
                    if b:
                        pe.wait_ge(v_lo, b)
                    project_v(b % 4)
                if kind == "head_scores":
                    h, q = FIRST_STEPS[b]
                    pe.wait_ge(qk_lo, 4 * (q // 2) + 2 * h + 2)
                    if b % 2 == 0:
                        free(at, "context", ct_lo)
                        free(at, "mix", y2_ready)
                    else:
                        free(at, "cross", e_exp)
                        free(at, "xn_turn", xnt_lo)
                    if b >= 2:
                        pe.wait_ge(s_masked, b - 1)
                    scores(b, 4 * h + q, BANK_S[b % 2])
                if kind == "head_turn":
                    if b % 2 == 0:
                        free(at, "scores", f_exp)
                        free(at, "project", y1_ready)
                    else:
                        free(at, "turn", pt_lo)
                        free(at, "x1_turn", x1t_lo)
                    if b >= 2:
                        pe.wait_ge(t_lo, b - 1)
                    turn_probs(b, b)
                if kind == "head_values":
                    h, q = FIRST_STEPS[b]
                    pe.wait_ge(v_lo, q + 1)
                    if b == 2:
                        free(at, "cross_turn", et_lo)
                    elif b == 4:
                        pe.wait_ge(at_lo, 1)
                    values(b, b, 0, None, h, q)

            def project_qk(b, index, weights):
                project_piece(WQ if b < 2 else WK, b % 2, index, weights)

            def project_piece(w, half, index, weights):
                pe.wait_ge(w_lo, weights)
                if not (isinstance(index, int) and index == 0):
                    pe.wait_ge(qk_lo, index)
                for k in range(KC):
                    mm = split3(pe, bank[BANK_QK][:, :], both(w, lambda t: t[:, k, :]),
                                both(XT, lambda t: t[:, k, half * HALF:half * HALF + HALF]), k == 0, k == KC - 1)
                mm.then_inc(qk_done, 1)

            def project_v(q):
                for r in range(2):
                    tok = (2 * q + r) * P
                    for k in range(KC):
                        mm = split3(pe, bank[BANK_VO][:, r * 256:r * 256 + 256],
                                    both(XT, lambda t: t[:, k, tok:tok + P]),
                                    both(WV, lambda t: t[:, k, :]), k == 0, k == KC - 1)
                mm.then_inc(v_done, 1)

            def project_o(q, dst=BANK_VO):
                for r in range(2):
                    tok = (2 * q + r) * P
                    for h in range(2):
                        mm = split3(pe, bank[dst][:, r * 256:r * 256 + 256],
                                    both(AT, lambda t: t[:, h, tok:tok + P]),
                                    both(WO, lambda t: t[:, h, :]), h == 0, h == 1)
                mm.then_inc(o_done, 1)

            def scores(m, j, to=None):
                tok, h, dst = (j % 4) * S, j // 4, bank[BANK_S[j % 2] if to is None else to]
                q = both(Q, lambda t: t[:, h, tok:tok + S])
                k = both(K, lambda t: t[:, h, tok:tok + S])
                split3(pe, dst[:, 0:128], both(q, lambda t: t[:, 0:P]), both(k, lambda t: t[:, 0:P]), True, True)
                split3(pe, dst[:, 128:384], both(q, lambda t: t[:, P:S]), k, True, True).then_inc(s_done, 1)

            def turn_probs(m, j):
                pe.wait_ge(s_norm, m + 1)
                p = ex[:, j % 4, 0:384]
                turn(bank[BANK_T[j % 2]], [p[:, n * P:(n + 1) * P] for n in range(3)]).then_inc(t_done, 1)

            def values(m, j, par, dst=None, h=None, b=None):
                pe.wait_ge(t_lo, m + 1)
                if b is None:
                    b, h = j % 4, j // 4
                if dst is None:
                    dst = bank[BANK_PV[(j // 2) % 2]][:, (j % 2) * 256:(j % 2) * 256 + 256]
                v = both(V, lambda t: t[:, par, 2 * b:2 * b + 2, h * P:h * P + P])
                p = both(PT, lambda t: t[:, j % 2, :])
                split3(pe, dst, both(v, lambda t: t[:, 0, :]), both(p, lambda t: t[:, 0:256]), True, False)
                split3(pe, dst[:, 128:256], both(v, lambda t: t[:, 1, :]), both(p, lambda t: t[:, 256:384]),
                       False, True).then_inc(pv_done, 1)

            for at, (kind, b) in enumerate(FRONT):
                front_step(at, kind, b)

            def pair(g, par, first, last):
                for j in range(HEAD_STEPS if last else SP_):
                    m = SP_ * g + j
                    if j % 4 == 0:
                        pe.wait_ge(qk_lo, SP_ * g + j + 4)
                    if not (first and j < 2):
                        pe.wait_ge(s_masked, m - 1)
                    scores(m, j)
                    if not (first and j < 2):
                        if not (first and j < 4):
                            pe.wait_ge(t_lo, m - 3)
                        turn_probs(m - 2, (j - 2) % 8)
                    done = {0: lambda: chunks_done(g - 1, 6) if not first else FIRST_CHUNKS,
                            2: lambda: chunks_done(g, 0, last), 4: lambda: chunks_done(g, 2),
                            6: lambda: chunks_done(g, 4)}[j // 2 * 2]()
                    project_qk(j % 4, SP_ * g + 4 + j, done)
                    if j < 4:
                        if not first:
                            if j == 0:
                                pe.wait_ge(w_lo, chunks_done(g - 1, 7))
                                pe.wait_ge(v_lo, 4 * g + 4)
                            else:
                                pe.wait_ge(o_added, 4 * (g - 1) + j)
                            if j % 2 == 0:
                                pe.wait_ge(at_lo, 4 * g - 1 + j // 2)
                            project_o(j)
                    else:
                        if j == 4:
                            pe.wait_ge(w_lo, chunks_done(g, 3))
                            if not first:
                                pe.wait_ge(o_added, 4 * g)
                        else:
                            pe.wait_ge(v_lo, 4 * (g + 1) + j - 4)
                        project_v(j - 4)
                    if not (first and j < 2):
                        if j == 2:
                            pe.wait_ge(v_lo, 4 * g + 4)
                        if j % 2 == 0 and not (first and j < 6):
                            pe.wait_ge(at_lo, 4 * g + j // 2 - 2)
                        values(m - 2, (j - 2) % 8, par if j >= 2 else 1 - par)

            def product(s, c, n, half, slot, tile):
                back = 3 * c + n - 4
                if back >= 0:
                    reader, steps = ((act_ready, 2), (silu_ready, 1), (us_ready, 1))[n]
                    pe.wait_ge(reader, s - steps + 1)
                if n == 2:
                    at = slice(tile * P, (tile + 1) * P) if isinstance(tile, int) else bass.ds(tile * P, P)
                    pe.matmul(mix_bank(c, n)[:, :], sel[:, at], wT[:, half * HALF:half * HALF + HALF],
                              start=True, stop=True).then_inc(b_done, 1)
                    return
                for k in range(KC):
                    at = n * 256 + k * P
                    mm = split3(pe, mix_bank(c, n)[:, :], both(W, lambda a: a[:, slot, at:at + P]),
                                both(XT, lambda a: a[:, k, half * HALF:half * HALF + HALF]),
                                k == 0, k == KC - 1)
                mm.then_inc((g_done, u_done)[n], 1)

            def down(s, half, slot, last=False):
                pe.wait_ge(act_lo, s + 1)
                for r in range(4):
                    t = 4 * half + r
                    mm = split3(pe, bank[t // 2][:, (t % 2) * 256:(t % 2) * 256 + 256],
                                both(CT, lambda a: a[:, half, r * P:(r + 1) * P]),
                                both(W, lambda a: a[:, slot, 512:768]),
                                False, True, skip_group_check=True)
                    if last and r % 2:
                        mm.then_inc(d_last, 1)
                if not last:
                    mm.then_inc(d_done, 1)

            over_pairs(pe, pair)

            def tail_step(kind, n):
                if kind == "scores":
                    if n == M0:
                        pe.wait_ge(qk_lo, M)
                    pe.wait_ge(s_masked, n - 1)
                    scores(n, n % SP_)
                if kind == "turn":
                    pe.wait_ge(t_lo, n - 1)
                    turn_probs(n, n % SP_)
                if kind == "values":
                    if n != M0 - 1:
                        if n == M0 + 1:
                            pe.wait_ge(qk_lo, M)
                        else:
                            pe.wait_ge(at_lo, at_count(n - 3))
                    at = n % 2 * 256 if n < M0 else 0
                    values(n, n % SP_, LAST % 2, bank[LATE_PV[n]][:, at:at + 256])
                if kind == "out":
                    pe.wait_ge(at_lo, at_count(M0 + n))
                    pe.wait_ge(w_lo, chunks_done(LAST, 7, True))
                    if n == 1:
                        pe.wait_ge(s_masked, M)
                    else:
                        pe.wait_ge(o_added, 4 * LAST + max(n - 1, 0))
                    project_o(n, LATE_OUT[n % 2])
                if kind == "xn_turn":
                    pe.wait_ge(h_norm, n + 1)
                    if n < 2:
                        pe.wait_ge(t_lo, M - 1 + n)
                    else:
                        pe.wait_ge(ht_lo, n - 1)
                    turn(bank[LATE_TURN[n % 2]], blocks(lambda r: xb[:, 2 * n + r, :])).then_inc(ht_done, 1)
                if kind == "logits":
                    pe.wait_ge(ht_lo, n + 1)
                    if n == 0:
                        pe.wait_ge(gate_lo, 1)
                        pe.wait_ge(s_masked, M - 1)
                    if n:
                        pe.wait_ge(lt_copied, n)
                    for k in range(KC):
                        mm = split3(pe, logits_T(n)[0], both(WS, lambda a: a[:, k * E:(k + 1) * E]),
                                    both(XT, lambda a: a[:, k, n * S:(n + 1) * S]), k == 0, k == KC - 1)
                    mm.then_inc(lt_done, 1)
                if kind == "logits_turn":
                    pe.wait_ge(lt_copied, n + 1)
                    if n == 0:
                        pe.wait_ge(o_added, 4 * LAST + 3)
                    for r in range(2):
                        t = 2 * n + r
                        mm = pe.transpose(bank[LATE_LOGITS][:, t * E:(t + 1) * E],
                                          logits_T(n)[1][:, r * P:(r + 1) * P], ident[0:E, 0:E])
                    mm.then_inc(gl_done, 1)
                if kind in "gu":
                    pe.wait_ge(m_lo, 1)
                    pe.wait_ge(ht_lo, 2 * n + 2)
                    pe.wait_ge(at_lo, at_count(M - 1))
                    product(n, n, "gu".index(kind), n, 0, 0)
                if kind == "weights_turn":
                    pe.wait_ge(r_parts, 1)
                    pe.wait_ge(o_added, 4 * PAIRS)
                    for t in range(8):
                        mm = pe.transpose(bank[LATE_WT][:, :].bitcast(BF16)[0:96, t * P:(t + 1) * P],
                                          wparts[:, t, :], identb[:, :])
                    mm.then_inc(r_turned, 1)

            for kind, n in TAIL:
                tail_step(kind, n)

            pe.wait_ge(wT_ready, 1)
            pe.wait_ge(sel_dma, 32)
            product(0, 0, 2, 0, 0, 0)
            product(1, 1, 2, 1, 0, 0)
            for n in range(4):
                pe.matmul(bank[n][:, :], zeros[0:1, 0:P], zeros[0:1, :], start=True, stop=True)
            down(0, 0, 0)
            with pe.Fori(0, (NT - 1) // 2) as i:
                for c in range(2, 6):
                    s, tile, half, slot = 4 * i + c, 2 * i + c // 2, c % 2, (c // 2) % 2
                    if half == 0:
                        pe.wait_ge(m_lo, tile + 1)
                    for n in range(3):
                        product(s, c, n, half, slot, tile)
                    down(s - 1, 1 - half, (slot + 1) % 2 if half == 0 else slot)
            down(2 * NT - 1, 1, (NT - 1) % 2, True)

        @block.scalar
        def _(act):
            act.preload_act_table(ACT.Exp)

            def split(n):
                act.wait_ge(in_dma[n], 16)
                act.activation(inputs[n][1][0], inputs[n][0], ACT.Copy).then_inc(in_hi, 1)

            def evac(n):
                kind, c, half, _ = jobs[n]
                if n == 0:
                    act.wait_ge(const_dma, 48)
                act.wait_ge(a_done, n + 1)
                bias, dst = job_bias(kind, c), job_target(kind, c, half)[0]
                if bias is None:
                    act.activation(dst, bank[FJ[n % 3]][:, :], ACT.Copy).then_inc(a_hi, 1)
                else:
                    act.activation(dst, bank[FJ[n % 3]][:, :], ACT.Identity, bias=bias).then_inc(a_hi, 1)

            def exps(dst, src, slot, scale, done):
                for r in range(2):
                    ins = act.activation(dst[:, r * 256:r * 256 + 256], src[:, r * 256:r * 256 + 256], ACT.Exp,
                                         bias=c_nm[:, slot, r:r + 1], scale=scale,
                                         accum_out=c_sums[:, slot, r:r + 1])
                ins.then_inc(done, 1)

            def w_split(j, count, dst):
                act.wait_ge(stage_dma[j], count)
                act.activation(dst[0], stage[:, j, :], ACT.Copy).then_inc(w_hi, 1)

            def front_step(kind, b):
                tok = b * S
                if kind == "input":
                    split(b)
                if kind == "split":
                    evac(b)
                if kind == "exps":
                    act.wait_ge(f_nm, b + 1)
                    if b >= 2:
                        act.wait_ge(ft_done, b - 1)
                    exps(chain_ex(b), bank[FS], b, 1.0 / 16, f_exp)
                if kind == "norm":
                    act.wait_ge(f_rec, b + 1)
                    for r in range(2):
                        p = chain_ex(b)[:, r * 256:r * 256 + 256]
                        ins = act.activation(p, p, ACT.Copy, scale=c_rec[:, b, r:r + 1])
                    ins.then_inc(f_norm, 1)
                if kind == "pt":
                    act.wait_ge(ft_done, b + 1)
                    act.activation(PT[0][:, 0, :], bank[FT][:, :], ACT.Copy).then_inc(pt_hi, 1)
                if kind == "ct":
                    act.wait_ge(fpv_done, b + 1)
                    for c in range(2):
                        ins = act.activation(CT[0][:, 0, c * 256:c * 256 + 256], bank[FPV][:, c * 256:c * 256 + 256],
                                             ACT.Identity, bias=bqkv[:, 4 + c:5 + c])
                    ins.then_inc(ct_hi, 1)
                if kind == "cross_exps":
                    act.wait_ge(e_nm, b + 1)
                    exps(ex[:, 2 + b, :], bank[FES], 4 + b, 1.0, e_exp)
                if kind == "x1t":
                    act.wait_ge(fxt_done, b + 1)
                    act.activation(AT[0][:, :, tok:tok + S], two(bank[FXT][:, :]), ACT.Copy).then_inc(x1t_hi, 1)
                if kind == "cross_pt":
                    act.wait_ge(fet_done, b + 1)
                    act.activation(PT[0][:, 1, :], bank[FET][:, :], ACT.Copy).then_inc(et_hi, 1)
                if kind == "squares":
                    act.wait_ge(x2_ready, b + 1)
                    squares(x2, b, sq_ready)
                if kind == "xn":
                    act.wait_ge(rms_rstd, b + 1)
                    for t in (2 * b, 2 * b + 1):
                        ins = act.activation(xb[:, t, :], x2[:, t, :], ACT.Copy, scale=rstd[:, 16 + t:17 + t])
                    ins.then_inc(xn_ready, 1)
                if kind == "xnt":
                    act.wait_ge(fnt_done, b + 1)
                    for c in range(2):
                        ins = act.activation(XT[0][:, c, tok:tok + S], bank[FNT][:, c * 256:c * 256 + 256],
                                             ACT.Copy, scale=lnw[:, c:c + 1])
                    ins.then_inc(xnt_hi, 1)
                if kind == "weights":
                    for sem_, count in {6: ((v_done, 4),), 7: ((qk_done, 5),), 9: ((qk_done, 6),),
                                        10: ((qk_done, 8),), 11: ((qk_done, 10),)}.get(b, ()):
                        act.wait_ge(sem_, count)
                    w_split(FIRST_SLOTS[b], 16 * (1 + (b >= 5 and FIRST_SLOTS[b] < FIRST_CHUNKS)), first_target(b))
                if kind == "qk_split":
                    h, qk, half, _ = PIECES[b]
                    piece_high(Q if qk == "q" else K, h, half, b)
                if kind == "v_split":
                    v_high(b % 4, b // 4, b)
                if kind == "head_exps":
                    if b >= 4:
                        act.wait_ge(t_done, b - 3)
                    act.wait_ge(s_masked, b + 1)
                    exp_scores(b)
                if kind == "head_probs":
                    probs_high(b + 2, b)
                if kind == "head_attn":
                    piece_out(2 * b + 2, b % 2, b // 2, b % 2)

            def squares(src, b, done):
                for r in range(2):
                    t = 2 * b + r
                    ins = act.activation(xb[:, t, :], src[:, t, :], ACT.Square, accum_out=msq[:, t:t + 1])
                ins.then_inc(done, 1)

            def qk_high(j, index):
                piece_high(Q if j % 4 < 2 else K, (j // 4 + 1) % 2, j % 2, index)

            def piece_high(dst, head, half, index):
                act.wait_ge(qk_done, index + 1)
                act.activation(dst[0][:, head, half * HALF:half * HALF + HALF],
                               bank[BANK_QK][:, :], ACT.Copy).then_inc(qk_hi, 1)

            def v_high(q, par, index):
                act.wait_ge(v_done, index + 1)
                act.activation(V[0][:, par, 2 * q:2 * q + 2, :].rearrange("p t h -> p (t h)"),
                               bank[BANK_VO][:, :], ACT.Copy).then_inc(v_hi, 1)

            def probs_high(m, j):
                act.wait_ge(t_done, m - 1)
                act.activation(PT[0][:, j % 2, 0:384], bank[BANK_T[j % 2]][:, 0:384], ACT.Copy).then_inc(t_hi, 1)

            def out_high(m, j):
                before = (j - 2) % SP_
                piece_out(m - 1, before // 4, before % 4 // 2, (before // 2) % 2)

            def piece_out(count, h, half, n):
                act.wait_ge(pv_done, count)
                act.activation(AT[0][:, h, half * HALF:half * HALF + HALF],
                               bank[BANK_PV[n]][:, :], ACT.Copy).then_inc(at_hi, 1)

            def exp_scores(j):
                for at, n, r in ((0, 128, 0), (128, 256, 1)):
                    ins = act.activation(ex[:, j % 4, at:at + n], sm[:, j % 2, at:at + n], ACT.Exp,
                                         bias=nm[:, j, r:r + 1], scale=-1.0, accum_out=sums[:, j, r:r + 1])
                ins.then_inc(s_exp, 1)

            for kind, b in FRONT:
                front_step(kind, b)

            def pair(g, par, first, last):
                for j in range(HEAD_STEPS if last else SP_):
                    m = SP_ * g + j
                    if not (first and j < 2):
                        probs_high(m, j)
                    act.wait_ge(s_masked, m + 1)
                    exp_scores(j)
                    qk_high(j, SP_ * g + 4 + j)
                    if j >= 4:
                        v_high(j - 4, 1 - par, 4 * (g + 1) + j - 4)
                    if j % 2 and not (first and j < 2):
                        out_high(m, j)
                    if not last or j in LAST_CHUNKS:
                        if j in (0, 2, 4, 6):
                            act.wait_ge(qk_done, SP_ * g + 4 + j)
                        elif j in (1, 3):
                            act.wait_ge(v_done, 4 * (g + 1))
                        elif not first:
                            act.wait_ge(o_done, 4 * g)
                        w_split(j, 16 * (g + 1 + (j < FIRST_CHUNKS)), chunk_target(j))

            over_pairs(act, pair)
            def m_split(t, slot, count):
                act.wait_ge(m_dma[slot], count)
                act.activation(W[0][:, slot, :], raw_moe[:, slot, :], ACT.Copy).then_inc(m_hi, 1)

            def tail_step(kind, n):
                if kind == "exps":
                    act.wait_ge(s_masked, n + 1)
                    exp_scores(n % SP_)
                if kind == "probs":
                    probs_high(n + 2, n % SP_)
                if kind == "attn":
                    act.wait_ge(pv_done, n + 1)
                    act.activation(late_out(AT[0], n), late_pv(n), ACT.Copy).then_inc(at_hi, 1)
                if kind == "o_weights":
                    j = (5, 7)[n]
                    act.wait_ge(o_done, 4 * LAST)
                    w_split(j, 16 * (LAST + 1), chunk_target(j))
                if kind == "gate":
                    act.wait_ge(gate_dma, 16)
                    act.activation(WS[0][:, 0:2 * E], gate_raw[:, :, :].rearrange("p k e -> p (k e)"), ACT.Copy)\
                        .then_inc(gate_hi, 1)
                if kind == "tile":
                    m_split(0, 0, 16)
                if kind == "squares":
                    act.wait_ge(o_added, 4 * LAST + n + 1)
                    squares(hid, n, h_sq)
                if kind == "xnt":
                    act.wait_ge(ht_done, n + 1)
                    for c in range(2):
                        ins = act.activation(XT[0][:, c, n * S:n * S + S],
                                             bank[LATE_TURN[n % 2]][:, c * 256:c * 256 + 256],
                                             ACT.Copy, scale=lnw[:, 2 + c:3 + c])
                    ins.then_inc(ht_hi, 1)
                if kind == "logits_copy":
                    act.wait_ge(lt_done, n + 1)
                    act.activation(logits_T(n)[1], logits_T(n)[0], ACT.Copy).then_inc(lt_copied, 1)
                if kind == "router":
                    act.wait_ge(r_sub, 1)
                    act.activation(gl[:, :, 0:E], gw[:, :, :], ACT.Exp).then_inc(r_exp, 1)
                    act.preload_act_table(ACT.Silu)

            for kind, n in TAIL:
                tail_step(kind, n)

            def silu(s, c):
                act.wait_ge(g_done, s + 1)
                if c >= 2:
                    act.wait_ge(us_ready, s - 1)
                act.activation(ex[:, c % 2, :], mix_bank(c, 0)[:, :], ACT.Silu).then_inc(silu_ready, 1)

            def activations_high(s, c):
                half = c % 2
                act.wait_ge(act_ready, s + 1)
                if c >= 2:
                    act.wait_ge(d_done, s - 1)
                act.activation(CT[0][:, half, :], ex[:, 4 + half, :], ACT.Copy).then_inc(act_hi, 1)

            silu(0, 0)
            silu(1, 1)
            activations_high(0, 0)
            m_split(1, 1, 16)
            activations_high(1, 1)
            with act.Fori(0, (NT - 1) // 2) as i:
                for c in range(2, 6):
                    s, tile = 4 * i + c, 2 * i + c // 2
                    if c % 2:
                        act.wait_ge(d_done, s - 1)
                        m_split(tile + 1, (c // 2 + 1) % 2, 16 * (i + 1 + (c // 2 + 1) // 2))
                    silu(s, c)
                    activations_high(s, c)

            for b in range(2):
                act.wait_ge(z_shift, b + 1)
                for t in (2 * b, 2 * b + 1):
                    ins = act.activation(xb[:, t, :], hid[:, t, :], ACT.Identity, bias=shift[:, t:t + 1],
                                         scale=rstd[:, t:t + 1])
                ins.then_inc(z_out, 1)

        @block.vector
        def _(dve):
            def low(dst, src, high, done):
                dve.tensor_tensor(dst, src, high.bitcast(F32), ALU.subtract).then_inc(done, 1)

            def split(n):
                dve.wait_ge(in_hi, n + 1)
                low(inputs[n][1][1], inputs[n][0], inputs[n][1][0], in_lo)

            def evac(n):
                kind, c, half, _ = jobs[n]
                dve.wait_ge(a_hi, n + 1)
                bias, (high, lo) = job_bias(kind, c), job_target(kind, c, half)
                if bias is None:
                    low(lo, bank[FJ[n % 3]][:, :], high, a_lo)
                else:
                    dve.scalar_tensor_tensor(out=lo, in0=bank[FJ[n % 3]][:, :], scalar=bias, in1=high.bitcast(F32),
                                             op0=ALU.add, op1=ALU.subtract).then_inc(a_lo, 1)

            def negmax(src, slot, scale, peak, done, count):
                dve.tensor_reduce(mx[:, slot, :], two(src), AX_X, ALU.max).then_inc(peak, 1)
                dve.wait_ge(peak, count)
                dve.tensor_scalar(c_nm[:, slot, :], mx[:, slot, :], -scale, None, ALU.mult).then_inc(done, 1)

            def moments(src, b, added, counted, done):
                dve.wait_ge(added, b + 1)
                for r in range(2):
                    ins = dve.bn_stats(stats[:, 2 * b + r, :], src[:, 2 * b + r, :])
                ins.then_inc(counted, 1)
                dve.wait_ge(counted, b + 1)
                for r in range(2):
                    ins = dve.bn_aggr(mv[:, 2 * b + r, :], stats[:, 2 * b + r, :])
                ins.then_inc(done, 1)

            def centre(dst, src, b, at, done):
                for r in range(2):
                    t = 2 * b + r
                    ins = dve.tensor_scalar(dst[:, t, :], src[:, t, :], mv[:, t, 0:1], rstd[:, at + t:at + t + 1],
                                            ALU.subtract, ALU.mult)
                ins.then_inc(done, 1)

            def rms_rows(src, b, done):
                for r in range(2):
                    t = 2 * b + r
                    ins = dve.tensor_scalar(xb[:, t, :], src[:, t, :], rstd[:, 16 + t:17 + t], None, ALU.mult)
                ins.then_inc(done, 1)

            def weighted_low(b, turned, w, done):
                for c in range(2):
                    ins = dve.scalar_tensor_tensor(out=XT[1][:, c, b * S:b * S + S],
                                                   in0=turned[:, c * 256:c * 256 + 256],
                                                   scalar=lnw[:, w + c:w + c + 1],
                                                   in1=XT[0][:, c, b * S:b * S + S].bitcast(F32),
                                                   op0=ALU.mult, op1=ALU.subtract)
                ins.then_inc(done, 1)

            def front_step(kind, b):
                tok, rows = b * S, slice(2 * b, 2 * b + 2)
                if kind == "input":
                    split(b)
                if kind == "split":
                    evac(b)
                if kind == "peak":
                    dve.wait_ge(fs_done, b + 1)
                    negmax(bank[FS][:, :], b, 1.0 / 16, f_max, f_nm, b + 1)
                if kind == "norm":
                    dve.wait_ge(f_exp, b + 1)
                    dve.reciprocal(c_rec[:, b, :], c_sums[:, b, :]).then_inc(f_rec, 1)
                if kind == "pt":
                    dve.wait_ge(pt_hi, b + 1)
                    low(PT[1][:, 0, :], bank[FT][:, :], PT[0][:, 0, :], pt_lo)
                if kind == "ct":
                    dve.wait_ge(ct_hi, b + 1)
                    for c in range(2):
                        cols = slice(c * 256, c * 256 + 256)
                        ins = dve.scalar_tensor_tensor(out=CT[1][:, 0, cols], in0=bank[FPV][:, cols],
                                                       scalar=bqkv[:, 4 + c:5 + c],
                                                       in1=CT[0][:, 0, cols].bitcast(F32),
                                                       op0=ALU.add, op1=ALU.subtract)
                    ins.then_inc(ct_lo, 1)
                if kind == "cross_peak":
                    dve.wait_ge(fes_done, b + 1)
                    negmax(bank[FES][:, :], 4 + b, 1.0, e_max, e_nm, b + 1)
                if kind == "cross_norm":
                    dve.wait_ge(e_exp, b + 1)
                    dve.reciprocal(c_rec[:, 4 + b, :], c_sums[:, 4 + b, :]).then_inc(e_rec, 1)
                if kind == "y1":
                    dve.wait_ge(fout_done, b + 1)
                    if b == 0:
                        dve.wait_ge(xb_ready, 1)
                    dve.tensor_tensor(xb[:, rows, :], two(bank[FOUT][:, :]), xb[:, rows, :], ALU.add)\
                       .then_inc(y1_ready, 1)
                    moments(xb, b, y1_ready, y1_stats, y1_var)
                if kind == "x1":
                    dve.wait_ge(y1_rstd, b + 1)
                    centre(hid, xb, b, 0, x1_ready)
                if kind == "x1t":
                    dve.wait_ge(x1t_hi, b + 1)
                    low(AT[1][:, :, tok:tok + S], two(bank[FXT][:, :]), AT[0][:, :, tok:tok + S], x1t_lo)
                if kind == "cross_pt":
                    dve.wait_ge(et_hi, b + 1)
                    low(PT[1][:, 1, :], bank[FET][:, :], PT[0][:, 1, :], et_lo)
                if kind == "y2":
                    dve.wait_ge(fxm_done, b + 1)
                    dve.tensor_tensor(hid[:, rows, :], two(bank[FXM][:, :]), hid[:, rows, :], ALU.add)\
                       .then_inc(y2_ready, 1)
                    moments(hid, b, y2_ready, y2_stats, y2_var)
                if kind == "x2":
                    dve.wait_ge(y2_rstd, b + 1)
                    centre(x2, hid, b, 8, x2_ready)
                if kind == "xnt":
                    dve.wait_ge(xnt_hi, b + 1)
                    weighted_low(b, bank[FNT], 0, xnt_lo)
                if kind == "qk_split":
                    h, qk, half, _ = PIECES[b]
                    piece_low(Q if qk == "q" else K, h, half, b)
                if kind == "v_split":
                    v_low(b % 4, b // 4, b)
                if kind == "head_mask":
                    if b == 0:
                        dve.wait_ge(const_ready, 1)
                    if b >= 2:
                        dve.wait_ge(s_exp, b - 1)
                    dve.wait_ge(s_done, b + 1)
                    mask_scores(b)
                if kind == "head_inverse":
                    dve.wait_ge(s_exp, b + 1)
                    inverse_sums(b)
                if kind == "head_probs":
                    probs_low(b + 2, b)
                if kind == "head_attn":
                    dve.wait_ge(at_hi, b + 1)
                    high, lo = both(AT, lambda t: t[:, b % 2, b // 2 * HALF:b // 2 * HALF + HALF])
                    low(lo, bank[BANK_PV[b % 2]][:, :], high, at_lo)

            def qk_low(j, index):
                piece_low(Q if j % 4 < 2 else K, (j // 4 + 1) % 2, j % 2, index)

            def piece_low(dst, head, half, index):
                dve.wait_ge(qk_hi, index + 1)
                high, lo = both(dst, lambda t: t[:, head, half * HALF:half * HALF + HALF])
                low(lo, bank[BANK_QK][:, :], high, qk_lo)

            def v_low(q, par, index):
                dve.wait_ge(v_hi, index + 1)
                high, lo = both(V, lambda t: t[:, par, 2 * q:2 * q + 2, :].rearrange("p t h -> p (t h)"))
                low(lo, bank[BANK_VO][:, :], high, v_lo)

            def probs_low(m, j):
                dve.wait_ge(t_hi, m - 1)
                low(PT[1][:, j % 2, 0:384], bank[BANK_T[j % 2]][:, 0:384], PT[0][:, j % 2, 0:384], t_lo)

            def add_o(q, index, src=BANK_VO):
                dve.wait_ge(o_done, index + 1)
                rows = slice(2 * q, 2 * q + 2)
                dve.tensor_tensor(hid[:, rows, :], two(bank[src][:, :]), hid[:, rows, :], ALU.add)\
                   .then_inc(o_added, 1)

            def inverse_sums(j):
                dve.reciprocal(rec[:, j, :], sums[:, j, :]).then_inc(s_rec, 1)

            def mask_scores(j):
                for at, n, r in ((0, 128, 0), (128, 256, 1)):
                    ins = dve.tensor_tensor_reduce(out=sm[:, j % 2, at:at + n],
                                                   in0=bank[BANK_S[j % 2]][:, at:at + n],
                                                   in1=mask[:, 256 - n:256], scale=-SCALE, scalar=3.0e38,
                                                   op0=ALU.add, op1=ALU.min, accum_out=nm[:, j, r:r + 1])
                ins.then_inc(s_masked, 1)

            for kind, b in FRONT:
                front_step(kind, b)
            dve.wait_ge(hid_copied, B)

            def pair(g, par, first, last):
                for j in range(HEAD_STEPS if last else SP_):
                    m = SP_ * g + j
                    if first and j == 0:
                        dve.wait_ge(const_ready, 1)
                        dve.wait_ge(s_done, 1)
                    else:
                        dve.wait_ge(s_exp, m)
                        dve.wait_ge(s_done, m + 1)
                        inverse_sums((j - 1) % SP_)
                    mask_scores(j)
                    if not (first and j < 2):
                        probs_low(m, j)
                    qk_low(j, SP_ * g + 4 + j)
                    if j < 4 and not first:
                        add_o(j, 4 * (g - 1) + j)
                    if j >= 4:
                        v_low(j - 4, 1 - par, 4 * (g + 1) + j - 4)
                    if j % 2 and not (first and j < 2):
                        before = (j - 2) % SP_
                        h, half = before // 4, before % 4 // 2
                        dve.wait_ge(at_hi, 4 * g + (j - 1) // 2)
                        high, lo = both(AT, lambda t: t[:, h, half * HALF:half * HALF + HALF])
                        low(lo, bank[BANK_PV[(before // 2) % 2]][:, :], high, at_lo)

            over_pairs(dve, pair)

            def m_low(t, slot):
                dve.wait_ge(m_hi, t + 1)
                low(W[1][:, slot, :], raw_moe[:, slot, :], W[0][:, slot, :], m_lo)

            steps = [0]

            def link(ins):
                steps[0] += 1
                ins.then_inc(r_step, 1)
                dve.wait_ge(r_step, steps[0])

            def spread(a, n):
                return a[:, :].unsqueeze(2).to_broadcast([P, 8, n])

            def router():
                probs = gl[:, :, 0:E]
                dve.wait_ge(gl_done, B)
                dve.wait_ge(const_ready, 1)
                logits = bank[LATE_LOGITS][:, 0:8 * E].rearrange("p (t e) -> p t e", e=E)
                link(dve.tensor_reduce(gm[:, :], logits, AX_X, ALU.max))
                ins = dve.tensor_tensor(gw[:, :, :], logits, spread(gm, E), ALU.subtract)
                ins.then_inc(r_sub, 1)
                dve.wait_ge(r_exp, 1)
                link(dve.tensor_reduce(gs[:, :], probs, AX_X, ALU.add))
                link(dve.reciprocal(gr[:, :], gs[:, :]))
                link(dve.tensor_tensor(probs, probs, spread(gr, E), ALU.mult))
                for t in range(8):
                    ins = dve.max(g8[:, t, :], gl[:, t, :])
                link(ins)
                link(dve.tensor_reduce(gs[:, :], g8[:, :, 0:TOPK], AX_X, ALU.add))
                link(dve.memset(g8[:, :, TOPK:8], -1.0))
                for t in range(8):
                    ins = dve.match_replace(grep[:, t, :], g8[:, t, :], gl[:, t, :], 0.0)
                link(ins)
                link(dve.reciprocal(gr[:, :], gs[:, :]))
                link(dve.tensor_tensor(gw[:, :, :], probs, grep[:, :, 0:E], ALU.subtract))
                link(dve.tensor_tensor(gw[:, :, :], gw[:, :, :], spread(gr, E), ALU.mult))
                link(dve.tensor_copy(wparts[:, :, 0:E], gw[:, :, :]))
                link(dve.tensor_tensor(gt[:, :, :], gw[:, :, :], wparts[:, :, 0:E], ALU.subtract))
                link(dve.tensor_copy(wparts[:, :, 32:32 + E], gt[:, :, :]))
                link(dve.tensor_tensor(gt[:, :, :], gt[:, :, :], wparts[:, :, 32:32 + E], ALU.subtract))
                dve.tensor_copy(wparts[:, :, 64:64 + E], gt[:, :, :]).then_inc(r_parts, 1)

            def tail_step(kind, n):
                if kind == "inverse":
                    dve.wait_ge(s_exp, n + 1)
                    inverse_sums(n % SP_)
                if kind == "mask":
                    dve.wait_ge(s_exp, n - 1)
                    dve.wait_ge(s_done, n + 1)
                    mask_scores(n % SP_)
                if kind == "probs":
                    probs_low(n + 2, n % SP_)
                if kind == "attn":
                    dve.wait_ge(at_hi, at_count(n))
                    low(late_out(AT[1], n), late_pv(n), late_out(AT[0], n), at_lo)
                if kind == "gate":
                    dve.wait_ge(gate_hi, 1)
                    low(WS[1][:, 0:2 * E], gate_raw[:, :, :].rearrange("p k e -> p (k e)"), WS[0][:, 0:2 * E],
                        gate_lo)
                if kind == "tile":
                    m_low(0, 0)
                if kind == "add":
                    add_o(n, 4 * LAST + n, LATE_OUT[n % 2])
                if kind == "xn":
                    dve.wait_ge(h_rstd, n + 1)
                    rms_rows(hid, n, h_norm)
                if kind == "xnt":
                    dve.wait_ge(ht_hi, n + 1)
                    weighted_low(n, bank[LATE_TURN[n % 2]], 2, ht_lo)
                if kind == "router":
                    router()
                if kind == "weights_turn":
                    dve.wait_ge(r_turned, 1)
                    dve.tensor_copy(wT[:, :], bank[LATE_WT][:, :].bitcast(BF16)[0:96, :]).then_inc(wT_ready, 1)

            for kind, n in TAIL:
                tail_step(kind, n)

            def mix(s, c, tile=None):
                half = c % 2
                if tile is not None:
                    m_low(tile, tile_slot(c))
                dve.wait_ge(silu_ready, s + 1)
                dve.wait_ge(u_done, s + 1)
                dve.tensor_tensor(ex[:, 2 + half, :], mix_bank(c, 1)[:, :], ex[:, half, :], ALU.mult)\
                   .then_inc(us_ready, 1)
                dve.wait_ge(us_ready, s + 1)
                dve.wait_ge(b_done, s + 1)
                dve.tensor_tensor(ex[:, 4 + half, :], mix_bank(c, 2)[:, :], ex[:, 2 + half, :], ALU.mult)\
                   .then_inc(act_ready, 1)
                dve.wait_ge(act_hi, s + 1)
                low(CT[1][:, half, :], ex[:, 4 + half, :], CT[0][:, half, :], act_lo)

            def tile_slot(c):
                return (c // 2 + 1) % 2

            mix(0, 0)
            mix(1, 1, 1)
            with dve.Fori(0, (NT - 1) // 2) as i:
                for c in range(2, 6):
                    mix(4 * i + c, c, 2 * i + c // 2 + 1 if c % 2 else None)

            for b in range(B):
                rows = slice(2 * b, 2 * b + 2)
                dve.wait_ge(hx_ready, 1)
                if b < 2:
                    dve.wait_ge(d_done, 2 * NT - 1)
                else:
                    dve.wait_ge(d_last, b - 1)
                dve.tensor_tensor(hid[:, rows, :], two(bank[b][:, :]), x2[:, rows, :], ALU.add).then_inc(z_ready, 1)
                moments(hid, b, z_ready, z_stats, z_var)
            for b in (2, 3):
                dve.wait_ge(z_rstd, b + 1)
                centre(xb, hid, b, 0, z_out_late)

        @block.gpsimd
        def _(pool):
            pool.memset(ident[:, :], 0.0).then_inc(pool_step, 1)
            pool.memset(identb[:, :], 0.0).then_inc(pool_step, 1)
            pool.memset(mask[:, :], 0.0).then_inc(pool_step, 1)
            pool.memset(sel[0:32, :], 1.0).then_inc(pool_step, 1)
            pool.memset(mh[:, :], -0.5).then_inc(pool_step, 1)
            pool.memset(zeros[:, :], 0.0).then_inc(pool_step, 1)
            pool.memset(wparts[:, :, :], 0.0).then_inc(pool_step, 1)
            pool.memset(gl[:, :, :], -1.0).then_inc(pool_step, 1)
            pool.wait_ge(pool_step, 8)
            for m in (ident, identb):
                pool.affine_select(out=m[:, :], in_=m[:, :], compare_op=ALU.not_equal, fill=1.0, base=0,
                                   pattern=[[-1, P]], channel_multiplier=1).then_inc(ident_ready, 1)
            pool.affine_select(out=mask[:, 128:256], in_=mask[:, 128:256], compare_op=ALU.is_ge, fill=MASK, base=0,
                               pattern=[[-1, P]], channel_multiplier=1)
            pool.memset(wparts[:, :, E:E + 1], 1.0).then_inc(const_ready, 1)
            pool.affine_select(out=sel[0:32, 0:E * I], in_=sel[0:32, 0:E * I], compare_op=ALU.is_ge, fill=0.0,
                               base=0, pattern=[[1, E * I]], channel_multiplier=-I).then_inc(pool_step, 1)
            pool.wait_ge(pool_step, 9)
            pool.affine_select(out=sel[0:32, 0:E * I], in_=sel[0:32, 0:E * I], compare_op=ALU.is_ge, fill=0.0,
                               base=I - 1, pattern=[[-1, E * I]], channel_multiplier=I)
            pool.affine_select(out=sel[0:32, E * I:], in_=sel[0:32, E * I:], compare_op=ALU.is_equal, fill=0.0,
                               base=-E, pattern=[[0, NT * P - E * I]], channel_multiplier=1).then_inc(sel_ready, 1)

            def inverse_root(src, at, n, scale, eps, eps_done, done, count):
                pool.tensor_scalar(veps[:, at:at + n], src, scale, eps, ALU.mult, ALU.add).then_inc(eps_done, 1)
                pool.wait_ge(eps_done, count)
                pool.tensor_tensor(rstd[:, at:at + n], veps[:, at:at + n], mh[:, 0:n], ALU.pow).then_inc(done, 1)

            def w_low(j, count, dst):
                pool.wait_ge(w_hi, count)
                pool.tensor_tensor(dst[1], stage[:, j, :], dst[0].bitcast(F32), ALU.subtract).then_inc(w_lo, 1)

            def normalise(m, j):
                pool.wait_ge(s_rec, m + 1)
                for at, n, r in ((0, 128, 0), (128, 256, 1)):
                    ins = pool.tensor_tensor(ex[:, j % 4, at:at + n], ex[:, j % 4, at:at + n],
                                             rec[:, j, r:r + 1].to_broadcast([P, n]), ALU.mult)
                ins.then_inc(s_norm, 1)

            for kind, b in FRONT:
                rows = slice(2 * b, 2 * b + 2)
                if kind == "x_bias":
                    pool.wait_ge(x_dma, 32)
                    pool.tensor_tensor(xb[:, :, :], xb[:, :, :], bo[:, :].unsqueeze(1).to_broadcast([P, 8, 256]),
                                       ALU.add).then_inc(xb_ready, 1)
                if kind == "y1_root":
                    pool.wait_ge(y1_var, b + 1)
                    inverse_root(mv[:, rows, 1], 2 * b, 2, 1.0, LN_EPS, y1_eps, y1_rstd, b + 1)
                if kind == "cross_norm":
                    pool.wait_ge(e_rec, b + 1)
                    for r in range(2):
                        p = ex[:, 2 + b, r * 256:r * 256 + 256]
                        ins = pool.tensor_tensor(p, p, c_rec[:, 4 + b, r:r + 1].to_broadcast([P, 256]), ALU.mult)
                    ins.then_inc(e_norm, 1)
                if kind == "y2_root":
                    pool.wait_ge(y2_var, b + 1)
                    inverse_root(mv[:, rows, 1], 8 + 2 * b, 2, 1.0, LN_EPS, y2_eps, y2_rstd, b + 1)
                if kind == "rms":
                    pool.wait_ge(sq_ready, b + 1)
                    inverse_root(msq[:, rows], 16 + 2 * b, 2, 1.0 / H, RMS_EPS, rms_eps, rms_rstd, b + 1)
                if kind == "keep":
                    pool.wait_ge(x2_ready, b + 1)
                    pool.tensor_copy(hid[:, rows, :], x2[:, rows, :]).then_inc(hid_copied, 1)
                if kind == "weights":
                    w_low(FIRST_SLOTS[b], b + 1, first_target(b))
                if kind == "head_norm":
                    normalise(b, b)

            def pair(g, par, first, last):
                for j in range(HEAD_STEPS - 1 if last else SP_):
                    if not last or j in LAST_CHUNKS:
                        w_low(j, chunks_done(g, j, last), chunk_target(j))
                    normalise(SP_ * g + j, j)

            def tail_step(kind, n):
                if kind == "norm":
                    normalise(n, n % SP_)
                if kind == "o_weights":
                    j = (5, 7)[n]
                    w_low(j, chunks_done(LAST, j, True), chunk_target(j))
                if kind == "rms":
                    pool.wait_ge(h_sq, n + 1)
                    inverse_root(msq[:, 2 * n:2 * n + 2], 16 + 2 * n, 2, 1.0 / H, RMS_EPS, h_eps, h_rstd, n + 1)
                if kind == "hx":
                    pool.tensor_tensor(x2[:, :, :], hid[:, :, :], x2[:, :, :], ALU.add).then_inc(hx_ready, 1)

            normalise(SP_ - 1, SP_ - 1)
            over_pairs(pool, pair)
            for kind, n in TAIL:
                tail_step(kind, n)
            for b in range(B):
                pool.wait_ge(z_var, b + 1)
                rows = slice(2 * b, 2 * b + 2)
                if b < 2:
                    pool.tensor_scalar(shift[:, rows], mv[:, rows, 0], -1.0, None, ALU.mult)
                inverse_root(mv[:, rows, 1], 2 * b, 2, 1.0, LN_EPS, z_eps, z_rstd, b + 1)
                if b < 2:
                    pool.wait_ge(z_rstd, b + 1)
                    pool.tensor_tensor(shift[:, rows], shift[:, rows], rstd[:, rows], ALU.mult).then_inc(z_shift, 1)


def kernel(**inputs):
    import numpy as np
    import concourse.bacc as bacc
    from concourse.bass_utils import run_bass_kernel_spmd

    a = {k: np.asarray(v) for k, v in inputs.items()}
    f32 = np.float32

    def chunks(w):
        return w.reshape(-1, P, w.shape[-1]).transpose(1, 0, 2)

    xT = chunks(a["x"].reshape(T, H).T)
    ctxT = a["ctx_1024"].reshape(T, P).T
    w_qkv = np.stack([chunks(a["L0_attn_w_qkv"][n * H:(n + 1) * H].T).reshape(P, 512) for n in range(3)])
    w_side = np.concatenate([a["L0_xattn_Wq"].T, a["L0_xattn_Wk"].T,
                             chunks(a["L0_attn_w_out"].T).reshape(P, 512)], axis=1)
    b_qkv = a["L0_attn_b_qkv"].reshape(6, P).T
    b_x = np.stack([a["L0_xattn_bq"], a["L0_xattn_bk"]], axis=1)
    ln_w = np.concatenate([a["L0_ffn_ln1_w"].reshape(2, P).T, a["L0_ffn_ln2_w"].reshape(2, P).T], axis=1)

    q = a["L0_ffn_q_w"].reshape(NH, QHD, H)[:, :HD]
    kv = a["L0_ffn_kv_w"]
    k = kv[:NH * HD].reshape(NH, HD, H)
    v = kv[NH * HD:2 * NH * HD].reshape(PAIRS, 2 * HD, H)
    o = a["L0_ffn_o_w"].reshape(H, NH, HD)

    def q_of(n):
        return chunks(q[n].T).reshape(P, 256)

    def k_of(n):
        return chunks(k[n].T).reshape(P, 256)

    def v_of(g, c):
        return v[g].T[c * P:(c + 1) * P]

    def o_of(n):
        return o[:, n].T

    w_first = np.stack([q_of(0), k_of(0), v_of(0, 0), v_of(0, 1), q_of(1)])
    w_heads = np.stack([np.stack([k_of(2 * g + 1), v_of(g + 1, 0), q_of(2 * g + 2), v_of(g + 1, 1),
                                  k_of(2 * g + 2), o_of(2 * g), q_of(2 * g + 3), o_of(2 * g + 1)])
                        for g in range(PAIRS - 1)])
    w_last = np.stack([k_of(NH - 1), o_of(NH - 2), o_of(NH - 1)])

    w1, sh = a["L0_ffn_w1"], a["L0_ffn_sh_gu_w"]
    tiles = NT + 1
    g = np.zeros((tiles * P, H), f32)
    u = np.zeros((tiles * P, H), f32)
    d = np.zeros((tiles * P, H), f32)
    g[:E * I] = w1[:, :I].reshape(E * I, H)
    u[:E * I] = w1[:, I:].reshape(E * I, H)
    d[:E * I] = a["L0_ffn_w2"].transpose(0, 2, 1).reshape(E * I, H)
    g[E * I:FF] = sh[:2 * I]
    u[E * I:FF] = sh[2 * I:]
    d[E * I:FF] = a["L0_ffn_sh_down_w"].T

    def gu_tiles(w):
        return w.reshape(tiles, P, KC, P).transpose(0, 3, 2, 1).reshape(tiles, P, 256)

    w_moe = np.concatenate([gu_tiles(g), gu_tiles(u), d.reshape(tiles, P, H)], axis=2)
    gateT = chunks(a["L0_ffn_gate_w"].T)

    nc = bacc.Bacc("TRN2", target_bir_lowering=False, num_devices=1)
    given = dict(x=a["x"], xT=xT, ctxT=ctxT, w_qkv=w_qkv, w_side=w_side, b_qkv=b_qkv,
                 b_out=a["L0_attn_b_out"], b_x=b_x, ln_w=ln_w, w_heads_first=w_first, w_heads=w_heads,
                 w_last=w_last, w_moe=w_moe, gateT=gateT)
    given = {n: np.ascontiguousarray(w) for n, w in given.items()}
    args = {n: nc.dram_tensor(n, w.shape, mybir.dt.from_np(w.dtype), kind="ExternalInput").ap()
            for n, w in given.items()}
    out = nc.dram_tensor("out", (B, S, H), F32, kind="ExternalOutput").ap()
    program(nc, *args.values(), out)
    return run_bass_kernel_spmd(nc, [given], core_ids=[0]).results[0]["out"]
```

```python
from contextlib import ExitStack

import concourse.bass as bass
from concourse import mybir

F32 = mybir.dt.float32
F32R = mybir.dt.float32r
BF16 = mybir.dt.bfloat16
ALU = mybir.AluOpType
ACT = mybir.ActivationFunctionType
AX_X = mybir.AxisListType.X

P = 128
B, S, H = 4, 256, 256
T = B * S
HALF = T // 2
KC = H // P
NH, QHD, HD = 16, 192, 128
PAIRS = NH // 2
SP_ = 8
E, TOPK, I = 16, 4, 176
FF = E * I + 2 * I
NT = (FF + P - 1) // P
LN_EPS, RMS_EPS = 1e-5, 1e-6
SCALE = float(QHD) ** -0.5
MASK = -1e9 / SCALE


def program(nc, x, xT, ctxT, w_qkv, w_side, b_qkv, b_out, b_x, ln_w, w_heads_first, w_heads, w_last,
            w_moe, gateT, out):
    with ExitStack() as ctx:
        def sb(name, shape, dt=F32):
            return ctx.enter_context(nc.sbuf_tensor(name, shape, dt))

        def sem(name):
            return ctx.enter_context(nc.semaphore(name))

        def parts(name, shape):
            return sb(name + "_hi", shape, F32R), sb(name + "_lo", shape, F32R)

        XT = parts("XT", [P, KC, T])
        Q = parts("Q", [P, 2, T])
        K = parts("K", [P, 2, T])
        V = parts("V", [P, 2, 8, 256])
        AT = parts("AT", [P, 2, T])
        W = parts("W", [P, 2, 768])
        WS = parts("WS", [P, 768])
        PT = parts("PT", [P, 2, 512])
        CT = parts("CT", [P, 2, 512])
        hid = sb("hid", [P, 8, 256])
        x2 = sb("x2", [P, 8, 256])
        xb = sb("xb", [P, 8, 256])
        stage = sb("stage", [P, 8, 256])
        ex = sb("ex", [P, 8, 512])
        sm = sb("sm", [P, 2, 384])
        mask = sb("mask", [P, 256])
        ident = sb("ident", [P, P])
        identb = sb("identb", [P, P], BF16)
        bqkv = sb("bqkv", [P, 6])
        bxs = sb("bxs", [P, 2])
        lnw = sb("lnw", [P, 4])
        bo = sb("bo", [P, 256])
        zeros = sb("zeros", [1, 512], BF16)
        mh = sb("mh", [P, 2])
        mx = sb("mx", [P, 8, 2])
        nm = sb("nm", [P, 8, 2])
        sums = sb("sums", [P, 8, 2])
        rec = sb("rec", [P, 8, 2])
        c_nm = sb("c_nm", [P, 8, 2])
        c_sums = sb("c_sums", [P, 8, 2])
        c_rec = sb("c_rec", [P, 8, 2])
        stats = sb("stats", [P, 8, 6])
        mv = sb("mv", [P, 8, 2])
        veps = sb("veps", [P, 24])
        rstd = sb("rstd", [P, 24])
        msq = sb("msq", [P, 16])
        shift = sb("shift", [P, 8])
        gate_raw = sb("gate_raw", [P, 2, E])
        gl = sb("gl", [P, 8, E + TOPK])
        gm = sb("gm", [P, 8])
        gs = sb("gs", [P, 8])
        gr = sb("gr", [P, 8])
        g8 = sb("g8", [P, 8, 8])
        grep = sb("grep", [P, 8, E + TOPK])
        gw = sb("gw", [P, 8, E])
        gt = sb("gt", [P, 8, E])
        wparts = sb("wparts", [P, 8, 96], BF16)
        wT = sb("wT", [96, T], BF16)
        sel = sb("sel", [96, NT * P], BF16)

        bank = [ctx.enter_context(nc.psum_tensor(f"bank{i}", [P, 512], F32)) for i in range(8)]

        def split3(pe, acc, lhs, rhs, first, last, **kw):
            for n, (a, b) in enumerate(((0, 0), (0, 1), (1, 0))):
                mm = pe.matmul(acc, lhs[a], rhs[b], start=first and n == 0, stop=last and n == 2, **kw)
            return mm

        def both(t, f):
            return f(t[0]), f(t[1])

        in_dma = [sem(f"in_dma{i}") for i in range(9)]
        const_dma, x_dma = sem("const_dma"), sem("x_dma")
        ident_ready, const_ready, xb_ready = sem("ident_ready"), sem("const_ready"), sem("xb_ready")
        in_hi, in_lo, wq_lo = sem("in_hi"), sem("in_lo"), sem("wq_lo")
        a_done, a_hi, a_lo = sem("a_done"), sem("a_hi"), sem("a_lo")
        fs_done, ft_done, fpv_done, fes_done = sem("fs_done"), sem("ft_done"), sem("fpv_done"), sem("fes_done")
        fout_done, fxt_done, fet_done = sem("fout_done"), sem("fxt_done"), sem("fet_done")
        fxm_done, fnt_done = sem("fxm_done"), sem("fnt_done")
        f_max, f_nm, f_exp, f_rec, f_norm = sem("f_max"), sem("f_nm"), sem("f_exp"), sem("f_rec"), sem("f_norm")
        e_max, e_nm, e_exp, e_rec, e_norm = sem("e_max"), sem("e_nm"), sem("e_exp"), sem("e_rec"), sem("e_norm")
        pt_hi, pt_lo, ct_hi, ct_lo = sem("pt_hi"), sem("pt_lo"), sem("ct_hi"), sem("ct_lo")
        x1t_hi, x1t_lo, et_hi, et_lo = sem("x1t_hi"), sem("x1t_lo"), sem("et_hi"), sem("et_lo")
        y1_ready, y1_stats, y1_var, y1_eps, y1_rstd = (
            sem("y1_ready"), sem("y1_stats"), sem("y1_var"), sem("y1_eps"), sem("y1_rstd"))
        y2_ready, y2_stats, y2_var, y2_eps, y2_rstd = (
            sem("y2_ready"), sem("y2_stats"), sem("y2_var"), sem("y2_eps"), sem("y2_rstd"))
        rms_eps, rms_rstd = sem("rms_eps"), sem("rms_rstd")
        pool_step, sel_ready, sel_dma = sem("pool_step"), sem("sel_ready"), sem("sel_dma")
        x1_ready, x2_ready, sq_ready, hid_copied = (
            sem("x1_ready"), sem("x2_ready"), sem("sq_ready"), sem("hid_copied"))
        xn_ready, xnt_hi, xnt_lo = sem("xn_ready"), sem("xnt_hi"), sem("xnt_lo")
        stage_dma = [sem(f"stage_dma{j}") for j in range(SP_)]
        w_hi, w_lo = sem("w_hi"), sem("w_lo")
        s_done, s_masked, s_exp, s_rec, s_norm = (
            sem("s_done"), sem("s_masked"), sem("s_exp"), sem("s_rec"), sem("s_norm"))
        t_done, t_hi, t_lo = sem("t_done"), sem("t_hi"), sem("t_lo")
        qk_done, qk_hi, qk_lo = sem("qk_done"), sem("qk_hi"), sem("qk_lo")
        v_done, v_hi, v_lo = sem("v_done"), sem("v_hi"), sem("v_lo")
        o_done, o_added = sem("o_done"), sem("o_added")
        pv_done, at_hi, at_lo = sem("pv_done"), sem("at_hi"), sem("at_lo")
        gate_dma, gate_hi, gate_lo = sem("gate_dma"), sem("gate_hi"), sem("gate_lo")
        h_sq, h_eps, h_rstd, h_norm = sem("h_sq"), sem("h_eps"), sem("h_rstd"), sem("h_norm")
        ht_done, ht_hi, ht_lo, gl_done = sem("ht_done"), sem("ht_hi"), sem("ht_lo"), sem("gl_done")
        r_sub, r_exp, r_step, r_parts, r_turned, wT_ready = (
            sem("r_sub"), sem("r_exp"), sem("r_step"), sem("r_parts"), sem("r_turned"), sem("wT_ready"))
        m_dma = [sem("m_dma0"), sem("m_dma1")]
        m_hi, m_lo = sem("m_hi"), sem("m_lo")
        g_done, u_done, b_done, d_done = sem("g_done"), sem("u_done"), sem("b_done"), sem("d_done")
        silu_ready, us_ready, act_ready, act_hi, act_lo = (
            sem("silu_ready"), sem("us_ready"), sem("act_ready"), sem("act_hi"), sem("act_lo"))
        hx_ready = sem("hx_ready")
        d_last, z_shift = sem("d_last"), sem("z_shift")
        z_out_late, z_summed, z_mean, z_squared = (
            sem("z_out_late"), sem("z_summed"), sem("z_mean"), sem("z_squared"))
        lt_done, lt_copied = sem("lt_done"), sem("lt_copied")
        z_ready, z_stats, z_var, z_eps, z_rstd, z_out, out_dma = (
            sem("z_ready"), sem("z_stats"), sem("z_var"), sem("z_eps"), sem("z_rstd"), sem("z_out"), sem("out_dma"))

        block = ctx.enter_context(nc.Block())

        x_rows = x.rearrange("b (c p) h -> p (b c) h", p=P)
        out_rows = out.rearrange("b (c p) h -> b p c h", p=P)
        raw_xT = hid[:, :, :].rearrange("p (k t) h -> p k (t h)", k=KC)
        raw_ctx = x2[:, 0:4, :].rearrange("p t h -> p (t h)")
        raw_side = x2[:, 4:7, :].rearrange("p t h -> p (t h)")
        raw_moe = stage[:, 0:6, :].rearrange("p (s c) h -> p s (c h)", s=2)
        ctx_parts = both(V, lambda t: t[:, 1, 0:4, :].rearrange("p t h -> p (t h)"))
        xq_parts = both(V, lambda t: t[:, 1, 4:8, :].rearrange("p t h -> p (t h)"))
        xk_parts = both(XT, lambda t: t[:, 0, :])
        WV = both(W, lambda t: t[:, 0, 0:512].rearrange("p (k n) -> p k n", k=KC))
        WQ = both(W, lambda t: t[:, 0, 512:768].rearrange("p (k n) -> p k n", k=KC))
        WK = both(W, lambda t: t[:, 1, 0:256].rearrange("p (k n) -> p k n", k=KC))
        WO = both(W, lambda t: t[:, 1, 256:768].rearrange("p (h n) -> p h n", h=2))

        def qkv_at(t, part):
            return t[:, :, :].rearrange("p s n -> p (s n)")[:, part * 512:(part + 1) * 512]

        stage_flat = stage[:, :, :].rearrange("p s n -> p (s n)")
        def w_input(n):
            return (stage_flat[:, n * 512:(n + 1) * 512], both(W, lambda t: qkv_at(t, n)), w_qkv[n, :, :])

        inputs = (
            [w_input(0)]
            + [(raw_xT[:, k, 0:HALF], both(XT, lambda t, k=k: t[:, k, 0:HALF]), xT[:, k, 0:HALF])
               for k in range(KC)]
            + [w_input(1), w_input(2),
               (raw_ctx, ctx_parts, ctxT[:, :]),
               (raw_side[:, 0:256], both(WS, lambda t: t[:, 0:256]), w_side[:, 0:256]),
               (raw_xT[:, :, HALF:T], both(XT, lambda t: t[:, :, HALF:T]), xT[:, :, HALF:T]),
               (raw_side[:, 256:768], both(WS, lambda t: t[:, 256:768]), w_side[:, 256:768])])
        IN_X0, IN_X0B, IN_K, IN_V, IN_CTX, IN_SIDE, IN_X1, IN_OUT = range(1, 9)

        jobs = [(kind, c, half, max(need, IN_X1 if half else 0))
                for half in range(2)
                for kind, need, count in (("q", IN_X0B, 2), ("k", IN_K, 2), ("v", IN_V, 2),
                                          ("xq", IN_SIDE, 1), ("xk", IN_SIDE, 1))
                for c in range(count)]

        def jobs_until(kind, half):
            return max(n + 1 for n, job in enumerate(jobs) if job[0] == kind and job[2] == half)

        def job_target(kind, c, half):
            cols = slice(half * HALF, (half + 1) * HALF)
            if kind in "qk":
                return both(Q if kind == "q" else K, lambda t: t[:, c, cols])
            if kind == "v":
                r = 4 * half + 2 * c
                return both(V, lambda t: t[:, 0, r:r + 2, :].rearrange("p t h -> p (t h)"))
            return both(xq_parts if kind == "xq" else xk_parts, lambda t: t[:, cols])

        def job_bias(kind, c):
            return {"q": bqkv[:, c:c + 1], "k": bqkv[:, 2 + c:3 + c], "v": None,
                    "xq": bxs[:, 0:1], "xk": bxs[:, 1:2]}[kind]

        FRONT = """
            input 0, input 1, input 2, input 3, job 0, input 4, sel 0, input 5, job 1, input 6, split 0, job 2,
            job 3, input 7, split 1, split 2, split 3, job 4, input 8, split 4, job 5, split 5, job 6, x_bias 0,
            job 7, split 6, split 7, scores 0, job 8, peak 0, cross 0, job 9, exps 0, norm 0, scores 1, turn 0,
            cross_peak 0, split 8, sel 1, cross_exps 0, job 10, cross 1, peak 1, pt 0, cross_norm 0, context 0,
            cross_turn 0, exps 1, norm 1, turn 1, cross_peak 1, split 9, ct 0, split 10, job 11, pt 1, split 11,
            project 0, y1 0, context 1, scores 2, y1_root 0, cross_pt 0, peak 2, job 12, x1 0, job 13, ct 1,
            cross_exps 1, exps 2, split 12, x1_turn 0, split 13, job 14, scores 3, x1t 0, mix 0, split 14, norm 2,
            peak 3, cross_norm 1, y2 0, turn 2, exps 3, pt 2, job 15, split 15, y2_root 0, project 1, weights 0,
            context 2, norm 3, x2 0, y1 1, ct 2, cross 2, y1_root 1, squares 0, turn 3, cross_peak 2, pt 3, x1 1,
            rms 0, cross_turn 1, project 2, cross_pt 1, context 3, weights 1, y1 2, weights 2, x1_turn 1, xn 0,
            cross_exps 2, ct 3, y1_root 2, x1t 1, cross_norm 2, xn_turn 0, xnt 0, x1 2, mix 1, y2 1, cross 3,
            x1_turn 2, cross_turn 2, project 3, weights 3, y2_root 1, cross_peak 3, cross_pt 2, v 0, keep 0, x2 1,
            x1t 2, mix 2, squares 1, rms 1, y1 3, y1_root 3, cross_exps 3, cross_norm 3, y2 2, y2_root 2, xn 1,
            x1 3, xn_turn 1, xnt 1, cross_turn 3, x2 2, weights 4, x1_turn 3, qk 0, cross_pt 3, x1t 3, v_split 0,
            squares 2, qk_split 0, keep 1, mix 3, y2 3, rms 2, qk 1, xn 2, xn_turn 2, weights 5, y2_root 3,
            qk_split 1, x2 3, v 1, qk 2, xnt 2, head_scores 0, head_scores 1, v_split 1, squares 3, rms 3,
            qk_split 2, xn 3, qk 3, head_mask 0, head_exps 0, head_mask 1, head_inverse 0, qk_split 3, xn_turn 3,
            head_norm 0, v 2, xnt 3, head_scores 2, head_exps 1, head_turn 0, head_inverse 1, qk 4, v_split 2,
            qk_split 4, head_norm 1, head_probs 0, v 3, head_turn 1, head_probs 1, head_mask 2, weights 6, qk 5,
            head_values 0, weights 7, qk_split 5, head_scores 3, head_exps 2, weights 8, head_inverse 2,
            head_mask 3, head_values 1, qk 6, keep 2, v_split 3, sel 2, head_scores 4, v 4, qk_split 6, head_mask 4,
            head_exps 3, qk 7, head_inverse 3, v_split 4, head_norm 2, head_exps 4, head_scores 5, qk_split 7,
            head_mask 5, v 5, qk 8, weights 9, v_split 5, head_norm 3, qk_split 8, head_scores 6, head_turn 2,
            head_mask 6, v 6, weights 10, head_probs 2, head_inverse 4, qk 9, head_exps 5, head_turn 3,
            head_inverse 5, keep 3, head_attn 0, head_norm 4, v_split 6, qk_split 9, head_norm 5, weights 11,
            head_values 2, head_scores 7, head_probs 3, head_turn 4, head_exps 6, qk 10, weights 12, head_values 3,
            head_inverse 6, head_norm 6, head_mask 7, head_probs 4, head_turn 5, v 7, qk_split 10, qk 11,
            head_exps 7, head_probs 5, v_split 7, qk_split 11, head_values 4, head_attn 1, head_values 5,
            head_attn 2
        """
        FRONT = [(part.split()[0], int(part.split()[1])) for part in FRONT.split(",")]

        def before(at, kind):
            return sum(k == kind for k, _ in FRONT[:at])

        def before_with(at, kind, parity):
            return max((n + 1 for k, n in FRONT[:at] if k == kind and n % 2 == parity), default=0)

        FIRST_STEPS = ((0, 0), (0, 1), (1, 0), (1, 1), (0, 2), (0, 3), (1, 2), (1, 3))
        PIECES = tuple((h, qk, half, need) for half in range(2)
                       for h, qk, need in ((0, "q", 1), (0, "k", 2), (1, "q", 5), (1, "k", 6)))
        PIECES += tuple((0, qk, half, need) for qk, need in (("q", 8), ("k", 10)) for half in range(2))

        FJ, FS, FT, FPV, FES, FET = (5, 6, 7), 0, 1, 2, 3, 4
        FOUT, FXT, FXM, FNT = FS, FT, FPV, FES

        def chain_ex(b):
            return ex[:, 6 + b % 2, :]

        def two(ap):
            return ap.rearrange("p (t h) -> p t h", t=2)

        FIRST_CHUNKS = 5
        BANK_QK, BANK_VO, BANK_PV, BANK_T, BANK_S = 5, 6, (7, 4), (0, 1), (2, 3)
        LAST = PAIRS - 1
        LAST_CHUNKS = (0, 5, 7)

        def chunks_done(g, j, last=False):
            if last:
                return FIRST_CHUNKS + SP_ * LAST + LAST_CHUNKS.index(j) + 1
            return FIRST_CHUNKS + SP_ * g + j + 1

        def chunk_target(j):
            return {0: both(WK, lambda t: t[:, :, :]), 4: both(WK, lambda t: t[:, :, :]),
                    2: both(WQ, lambda t: t[:, :, :]), 6: both(WQ, lambda t: t[:, :, :]),
                    1: both(WV, lambda t: t[:, 0, :]), 3: both(WV, lambda t: t[:, 1, :]),
                    5: both(WO, lambda t: t[:, 0, :]), 7: both(WO, lambda t: t[:, 1, :])}[j]

        FIRST_PLACES = (2, 0, 1, 3, 7, 5, 1, 2, 3, 4, 5, 6, 7)
        FIRST_SLOTS = (0, 1, 2, 3, 4, 0, 1, 2, 3, 4, 5, 6, 7)

        def first_target(c):
            return chunk_target(FIRST_PLACES[c])

        TAIL = """
            gate 0, scores 60, turn 58, o_weights 0, inverse 59, scores 61, norm 59, mask 60, scores 62, mask 61,
            probs 58, o_weights 1, turn 59, values 58, exps 60, inverse 60, exps 61, mask 62, norm 60, inverse 61,
            scores 63, probs 59, turn 60, mask 63, exps 62, inverse 62, probs 60, exps 63, inverse 63, norm 61,
            values 59, turn 61, values 60, norm 62, norm 63, probs 61, attn 59, turn 62, values 61, attn 60,
            turn 63, probs 62, attn 61, out 0, tile 0, probs 63, values 62, add 0, attn 62, out 1, squares 0,
            values 63, add 1, out 2, rms 0, attn 63, xn 0, squares 1, add 2, out 3, rms 1, xn 1, squares 2,
            xn_turn 0, add 3, rms 2, xnt 0, xn_turn 1, logits 0, xn 2, squares 3, xnt 1, xn_turn 2, logits_copy 0,
            rms 3, xn 3, logits 1, xn_turn 3, logits_turn 0, xnt 2, logits_copy 1, logits 2, logits_turn 1, xnt 3,
            logits_copy 2, logits 3, logits_copy 3, logits_turn 2, logits_turn 3, router 0, tile 1, g 0, hx 0, u 0,
            g 1, u 1, weights_turn 0
        """
        TAIL = [(part.split()[0], int(part.split()[1])) for part in TAIL.split(",")]
        M = SP_ * PAIRS
        HEAD_STEPS = 4
        M0 = M - HEAD_STEPS
        LATE_PV = {M0 - 2: 4, M0 - 1: 4, M0: 7, M0 + 1: 5, M0 + 2: 4, M0 + 3: 7}
        LATE_OUT, LATE_TURN, LATE_LOGITS_T, LATE_LOGITS, LATE_WT = (6, 3), (0, 1), 2, 6, (3, 2)

        def logits_T(n):
            return (bank[LATE_LOGITS_T][0:E, n % 2 * 256:n % 2 * 256 + 256],
                    ex[0:E, 4 + n // 2, n % 2 * 256:n % 2 * 256 + 256])

        def at_count(m):
            return m // 2 + 1 if m < M0 else M0 // 2 + m - M0 + 1

        def late_out(t, m):
            if m < M0:
                return t[:, 0, HALF:T]
            return t[:, 1, (m - M0) * S:(m - M0 + 1) * S]

        def late_pv(m):
            return bank[LATE_PV[m]][:, 0:512 if m < M0 else 256]

        def over_pairs(eng, pair):
            with eng.Fori(0, (PAIRS - 2) // 2) as i:
                for n in range(2):
                    pair(2 * i + 1 + n, (1 + n) % 2, False)
            pair(LAST, LAST % 2, True)

        def mix_bank(s, n):
            return bank[4 + (3 * s + n) % 4]

        @block.sync
        def _(sp):
            for n, (raw, _, src) in enumerate(inputs):
                sp.dma_start(raw, src).then_inc(in_dma[n], 16)
                if n == 4:
                    sp.dma_start(bqkv[:, :], b_qkv).then_inc(const_dma, 16)
                    sp.dma_start(bxs[:, :], b_x).then_inc(const_dma, 16)
                    sp.dma_start(lnw[:, :], ln_w).then_inc(const_dma, 16)
            sp.dma_start(xb[:, :, :], x_rows).then_inc(x_dma, 16)
            sp.dma_start(bo[:, :], b_out.partition_broadcast(P)).then_inc(x_dma, 16)
            sp.dma_start(gate_raw[:, :, :], gateT).then_inc(gate_dma, 16)
            sp.wait_ge(wq_lo, 1)
            sp.wait_ge(in_lo, IN_V)
            for c in range(FIRST_CHUNKS):
                sp.dma_start(stage[:, c, :], w_heads_first[c, :, :]).then_inc(stage_dma[c], 16)

            def load(g, j, src):
                sp.dma_start(stage[:, j, :], src).then_inc(stage_dma[j], 16)

            for j in range(SP_):
                if j < FIRST_CHUNKS:
                    sp.wait_ge(w_lo, j + 1)
                load(0, j, w_heads[0, j, :, :])
            with sp.Fori(1, PAIRS - 1) as g:
                for j in range(SP_):
                    sp.wait_ge(w_lo, FIRST_CHUNKS + SP_ * (g - 1) + j + 1)
                    load(g, j, w_heads[bass.ds(g, 1), j, :, :].rearrange("g p n -> p (g n)"))
            for n, j in enumerate(LAST_CHUNKS):
                sp.wait_ge(w_lo, chunks_done(LAST - 1, j))
                load(LAST, j, w_last[n, :, :])

            sp.wait_ge(sel_ready, 1)
            for n in (32, 64):
                sp.dma_start(sel[n:n + 32, :], sel[0:32, :]).then_inc(sel_dma, 16)

            for t in range(2):
                sp.wait_ge(w_lo, chunks_done(LAST, (0, 5)[t], True))
                sp.dma_start(raw_moe[:, t, :], w_moe[t, :, :]).then_inc(m_dma[t], 16)
            with sp.Fori(1, (NT + 1) // 2) as i:
                for n in range(2):
                    sp.wait_ge(m_lo, 2 * i + n - 1)
                    sp.dma_start(raw_moe[:, n, :],
                                 w_moe[bass.ds(2 * i + n, 1), :, :].rearrange("g p n -> p (g n)"))\
                        .then_inc(m_dma[n], 16)
            for b in range(B):
                if b < 2:
                    sp.wait_ge(z_out, b + 1)
                else:
                    sp.wait_ge(z_out_late, b - 1)
                sp.dma_start(out_rows[b, :, :, :], xb[:, 2 * b:2 * b + 2, :]).then_inc(out_dma, 16)
            sp.wait_ge(out_dma, 16 * B)

        @block.tensor
        def _(pe):
            def zero(n):
                pe.matmul(bank[n][:, :], zeros[0:1, 0:P], zeros[0:1, :], start=True, stop=True)

            def turn(dst, src):
                for n, s in enumerate(src):
                    mm = pe.transpose(dst[:, n * P:(n + 1) * P], s, ident[:, :])
                return mm

            def blocks(t):
                return [t(r)[:, c * P:(c + 1) * P] for c in range(2) for r in range(2)]

            def flat(t):
                return t[:, :, :].rearrange("p s n -> p (s n)")

            def first_product(n):
                kind, c, half, need = jobs[n]
                dst = bank[FJ[n % 3]]
                if n == 0:
                    pe.wait_ge(wq_lo, 1)
                    pe.wait_ge(in_lo, IN_X0)
                else:
                    pe.wait_ge(in_lo, need)
                if n >= 3:
                    pe.wait_ge(a_lo, n - 2)
                cols = slice(half * HALF, (half + 1) * HALF)
                if kind in "qk":
                    for k in range(KC):
                        if n == 0 and k == 1:
                            pe.wait_ge(in_lo, need)
                        at = (0 if kind == "q" else 512) + k * 256 + c * P
                        mm = split3(pe, dst[:, :], both(W, lambda t: flat(t)[:, at:at + P]),
                                    both(XT, lambda t: t[:, k, cols]), k == 0, k == KC - 1)
                elif kind == "v":
                    for r in range(2):
                        tok = (4 * half + 2 * c + r) * P
                        for k in range(KC):
                            at = 1024 + k * 256
                            mm = split3(pe, dst[:, r * 256:r * 256 + 256], both(XT, lambda t: t[:, k, tok:tok + P]),
                                        both(W, lambda t: flat(t)[:, at:at + 256]), k == 0, k == KC - 1)
                else:
                    at = 0 if kind == "xq" else P
                    mm = split3(pe, dst[:, :], both(WS, lambda t: t[:, at:at + P]),
                                both(ctx_parts, lambda t: t[:, cols]), True, True)
                mm.then_inc(a_done, 1)

            def rows_of(count, dst, lhs, rhs):
                for r in range(2):
                    for k in range(count):
                        mm = split3(pe, dst[:, r * 256:r * 256 + 256], both(lhs[0], lambda t: lhs[1](t, r, k)),
                                    both(rhs[0], lambda t: rhs[1](t, k)), k == 0, k == count - 1)
                return mm

            def free(at, kind, sem_):
                if before(at, kind):
                    pe.wait_ge(sem_, before(at, kind))

            def free_of_heads(at, kind, parity, sem_):
                if before_with(at, kind, parity):
                    pe.wait_ge(sem_, before_with(at, kind, parity))

            def front_step(at, kind, b):
                tok = b * S
                if kind == "job":
                    first_product(b)
                if kind == "scores":
                    pe.wait_ge(a_lo, jobs_until("k", b // 2))
                    free(at, "scores", f_exp)
                    free(at, "project", y1_ready)
                    free_of_heads(at, "head_turn", 0, t_lo)
                    rows_of(KC, bank[FS], (Q, lambda t, r, k: t[:, k, tok + r * P:tok + r * P + P]),
                            (K, lambda t, k: t[:, k, tok:tok + S])).then_inc(fs_done, 1)
                if kind == "turn":
                    pe.wait_ge(f_norm, b + 1)
                    pe.wait_ge(ident_ready, 2)
                    free(at, "turn", pt_lo)
                    free(at, "x1_turn", x1t_lo)
                    free_of_heads(at, "head_turn", 1, t_lo)
                    turn(bank[FT], blocks(lambda r: chain_ex(b)[:, r * 256:r * 256 + 256])).then_inc(ft_done, 1)
                if kind == "context":
                    pe.wait_ge(pt_lo, b + 1)
                    pe.wait_ge(a_lo, jobs_until("v", b // 2))
                    free(at, "context", ct_lo)
                    free(at, "mix", y2_ready)
                    free_of_heads(at, "head_scores", 0, s_masked)
                    rows_of(2, bank[FPV], (V, lambda t, c, k: t[:, 0, 2 * b + k, c * P:c * P + P]),
                            (PT, lambda t, k: t[:, 0, k * 256:k * 256 + 256])).then_inc(fpv_done, 1)
                if kind == "cross":
                    pe.wait_ge(a_lo, jobs_until("xk", b // 2))
                    free(at, "cross", e_exp)
                    free(at, "xn_turn", xnt_lo)
                    free_of_heads(at, "head_scores", 1, s_masked)
                    rows_of(1, bank[FES], (xq_parts, lambda t, r, k: t[:, tok + r * P:tok + r * P + P]),
                            (xk_parts, lambda t, k: t[:, tok:tok + S])).then_inc(fes_done, 1)
                if kind == "project":
                    pe.wait_ge(ct_lo, b + 1)
                    pe.wait_ge(in_lo, IN_OUT)
                    free(at, "scores", f_exp)
                    free(at, "project", y1_ready)
                    free_of_heads(at, "head_turn", 0, t_lo)
                    rows_of(KC, bank[FOUT], (CT, lambda t, r, k: t[:, 0, k * 256 + r * P:k * 256 + r * P + P]),
                            (WS, lambda t, k: t[:, 256 + k * 256:512 + k * 256])).then_inc(fout_done, 1)
                if kind == "x1_turn":
                    pe.wait_ge(x1_ready, b + 1)
                    free(at, "turn", pt_lo)
                    free(at, "x1_turn", x1t_lo)
                    free_of_heads(at, "head_turn", 1, t_lo)
                    turn(bank[FXT], blocks(lambda r: hid[:, 2 * b + r, :])).then_inc(fxt_done, 1)
                if kind == "cross_turn":
                    pe.wait_ge(e_norm, b + 1)
                    free(at, "cross_turn", et_lo)
                    if before(at, "head_values") > 2:
                        pe.wait_ge(at_lo, 2)
                    turn(bank[FET], blocks(lambda r: ex[:, 2 + b, r * 256:r * 256 + 256])).then_inc(fet_done, 1)
                if kind == "mix":
                    pe.wait_ge(x1t_lo, b + 1)
                    pe.wait_ge(et_lo, b + 1)
                    free(at, "context", ct_lo)
                    free(at, "mix", y2_ready)
                    free_of_heads(at, "head_scores", 0, s_masked)
                    rows_of(2, bank[FXM], (AT, lambda t, r, k: t[:, k, tok + r * P:tok + r * P + P]),
                            (PT, lambda t, k: t[:, 1, k * 256:k * 256 + 256])).then_inc(fxm_done, 1)
                if kind == "xn_turn":
                    pe.wait_ge(xn_ready, b + 1)
                    free(at, "cross", e_exp)
                    free(at, "xn_turn", xnt_lo)
                    free_of_heads(at, "head_scores", 1, s_masked)
                    turn(bank[FNT], blocks(lambda r: xb[:, 2 * b + r, :])).then_inc(fnt_done, 1)
                if kind == "qk":
                    h, qk, half, need = PIECES[b]
                    pe.wait_ge(xnt_lo, 2 * half + 2)
                    pe.wait_ge(a_lo, len(jobs))
                    second = both(WO, lambda t: t[:, "kq".index(qk), :].rearrange("p (k n) -> p k n", k=KC))
                    project_piece(second if h else WQ if qk == "q" else WK, half, b, need)
                if kind == "v":
                    pe.wait_ge(xnt_lo, b % 4 + 1)
                    pe.wait_ge(w_lo, 4 if b < 4 else 9)
                    pe.wait_ge(a_lo, len(jobs))
                    if b:
                        pe.wait_ge(v_lo, b)
                    project_v(b % 4)
                if kind == "head_scores":
                    h, q = FIRST_STEPS[b]
                    pe.wait_ge(qk_lo, 4 * (q // 2) + 2 * h + 2)
                    if b % 2 == 0:
                        free(at, "context", ct_lo)
                        free(at, "mix", y2_ready)
                    else:
                        free(at, "cross", e_exp)
                        free(at, "xn_turn", xnt_lo)
                    if b >= 2:
                        pe.wait_ge(s_masked, b - 1)
                    scores(b, 4 * h + q, BANK_S[b % 2])
                if kind == "head_turn":
                    if b % 2 == 0:
                        free(at, "scores", f_exp)
                        free(at, "project", y1_ready)
                    else:
                        free(at, "turn", pt_lo)
                        free(at, "x1_turn", x1t_lo)
                    if b >= 2:
                        pe.wait_ge(t_lo, b - 1)
                    turn_probs(b, b)
                if kind == "head_values":
                    h, q = FIRST_STEPS[b]
                    pe.wait_ge(v_lo, q + 1)
                    if b == 2:
                        free(at, "cross_turn", et_lo)
                    elif b == 4:
                        pe.wait_ge(at_lo, 1)
                    values(b, b, 0, None, h, q)

            def project_qk(b, index, weights):
                project_piece(WQ if b < 2 else WK, b % 2, index, weights)

            def project_piece(w, half, index, weights):
                pe.wait_ge(w_lo, weights)
                if not (isinstance(index, int) and index == 0):
                    pe.wait_ge(qk_lo, index)
                for k in range(KC):
                    mm = split3(pe, bank[BANK_QK][:, :], both(w, lambda t: t[:, k, :]),
                                both(XT, lambda t: t[:, k, half * HALF:half * HALF + HALF]), k == 0, k == KC - 1)
                mm.then_inc(qk_done, 1)

            def project_v(q):
                for r in range(2):
                    tok = (2 * q + r) * P
                    for k in range(KC):
                        mm = split3(pe, bank[BANK_VO][:, r * 256:r * 256 + 256],
                                    both(XT, lambda t: t[:, k, tok:tok + P]),
                                    both(WV, lambda t: t[:, k, :]), k == 0, k == KC - 1)
                mm.then_inc(v_done, 1)

            def project_o(q, dst=BANK_VO):
                for r in range(2):
                    tok = (2 * q + r) * P
                    for h in range(2):
                        mm = split3(pe, bank[dst][:, r * 256:r * 256 + 256],
                                    both(AT, lambda t: t[:, h, tok:tok + P]),
                                    both(WO, lambda t: t[:, h, :]), h == 0, h == 1)
                mm.then_inc(o_done, 1)

            def scores(m, j, to=None):
                tok, h, dst = (j % 4) * S, j // 4, bank[BANK_S[j % 2] if to is None else to]
                q = both(Q, lambda t: t[:, h, tok:tok + S])
                k = both(K, lambda t: t[:, h, tok:tok + S])
                split3(pe, dst[:, 0:128], both(q, lambda t: t[:, 0:P]), both(k, lambda t: t[:, 0:P]), True, True)
                split3(pe, dst[:, 128:384], both(q, lambda t: t[:, P:S]), k, True, True).then_inc(s_done, 1)

            def turn_probs(m, j):
                pe.wait_ge(s_norm, m + 1)
                p = ex[:, j % 4, 0:384]
                turn(bank[BANK_T[j % 2]], [p[:, n * P:(n + 1) * P] for n in range(3)]).then_inc(t_done, 1)

            def values(m, j, par, dst=None, h=None, b=None):
                pe.wait_ge(t_lo, m + 1)
                if b is None:
                    b, h = j % 4, j // 4
                if dst is None:
                    dst = bank[BANK_PV[(j // 2) % 2]][:, (j % 2) * 256:(j % 2) * 256 + 256]
                v = both(V, lambda t: t[:, par, 2 * b:2 * b + 2, h * P:h * P + P])
                p = both(PT, lambda t: t[:, j % 2, :])
                split3(pe, dst, both(v, lambda t: t[:, 0, :]), both(p, lambda t: t[:, 0:256]), True, False)
                split3(pe, dst[:, 128:256], both(v, lambda t: t[:, 1, :]), both(p, lambda t: t[:, 256:384]),
                       False, True).then_inc(pv_done, 1)

            for at, (kind, b) in enumerate(FRONT):
                front_step(at, kind, b)

            def pair(g, par, last):
                for j in range(HEAD_STEPS if last else SP_):
                    m = SP_ * g + j
                    if j % 4 == 0:
                        pe.wait_ge(qk_lo, SP_ * g + j + 4)
                    pe.wait_ge(s_masked, m - 1)
                    scores(m, j)
                    pe.wait_ge(t_lo, m - 3)
                    turn_probs(m - 2, (j - 2) % SP_)
                    if j < 2:
                        done = chunks_done(g - 1, 6)
                    else:
                        done = chunks_done(g, j // 2 * 2 - 2, last)
                    project_qk(j % 4, SP_ * g + 4 + j, done)
                    if j < 4:
                        if j == 0:
                            pe.wait_ge(w_lo, chunks_done(g - 1, 7))
                            pe.wait_ge(v_lo, 4 * g + 4)
                        else:
                            pe.wait_ge(o_added, 4 * (g - 1) + j)
                        if j % 2 == 0:
                            pe.wait_ge(at_lo, 4 * g - 1 + j // 2)
                        project_o(j)
                    else:
                        if j == 4:
                            pe.wait_ge(w_lo, chunks_done(g, 3))
                            pe.wait_ge(o_added, 4 * g)
                        else:
                            pe.wait_ge(v_lo, 4 * (g + 1) + j - 4)
                        project_v(j - 4)
                    if j == 2:
                        pe.wait_ge(v_lo, 4 * g + 4)
                    if j % 2 == 0:
                        pe.wait_ge(at_lo, 4 * g + j // 2 - 2)
                    values(m - 2, (j - 2) % SP_, par if j >= 2 else 1 - par)

            def product(s, c, n, half, slot, tile):
                back = 3 * c + n - 4
                if back >= 0:
                    reader, steps = ((act_ready, 2), (silu_ready, 1), (us_ready, 1))[n]
                    pe.wait_ge(reader, s - steps + 1)
                if n == 2:
                    at = slice(tile * P, (tile + 1) * P) if isinstance(tile, int) else bass.ds(tile * P, P)
                    pe.matmul(mix_bank(c, n)[:, :], sel[:, at], wT[:, half * HALF:half * HALF + HALF],
                              start=True, stop=True).then_inc(b_done, 1)
                    return
                for k in range(KC):
                    at = n * 256 + k * P
                    mm = split3(pe, mix_bank(c, n)[:, :], both(W, lambda a: a[:, slot, at:at + P]),
                                both(XT, lambda a: a[:, k, half * HALF:half * HALF + HALF]),
                                k == 0, k == KC - 1)
                mm.then_inc((g_done, u_done)[n], 1)

            def down(s, half, slot, last=False):
                pe.wait_ge(act_lo, s + 1)
                for r in range(4):
                    t = 4 * half + r
                    mm = split3(pe, bank[t // 2][:, (t % 2) * 256:(t % 2) * 256 + 256],
                                both(CT, lambda a: a[:, half, r * P:(r + 1) * P]),
                                both(W, lambda a: a[:, slot, 512:768]),
                                False, True, skip_group_check=True)
                    if last and r % 2:
                        mm.then_inc(d_last, 1)
                if not last:
                    mm.then_inc(d_done, 1)

            over_pairs(pe, pair)

            def tail_step(kind, n):
                if kind == "scores":
                    if n == M0:
                        pe.wait_ge(qk_lo, M)
                    pe.wait_ge(s_masked, n - 1)
                    scores(n, n % SP_)
                if kind == "turn":
                    pe.wait_ge(t_lo, n - 1)
                    turn_probs(n, n % SP_)
                if kind == "values":
                    if n != M0 - 1:
                        if n == M0 + 1:
                            pe.wait_ge(qk_lo, M)
                        else:
                            pe.wait_ge(at_lo, at_count(n - 3))
                    at = n % 2 * 256 if n < M0 else 0
                    values(n, n % SP_, LAST % 2, bank[LATE_PV[n]][:, at:at + 256])
                if kind == "out":
                    pe.wait_ge(at_lo, at_count(M0 + n))
                    pe.wait_ge(w_lo, chunks_done(LAST, 7, True))
                    if n == 1:
                        pe.wait_ge(s_masked, M)
                    else:
                        pe.wait_ge(o_added, 4 * LAST + max(n - 1, 0))
                    project_o(n, LATE_OUT[n % 2])
                if kind == "xn_turn":
                    pe.wait_ge(h_norm, n + 1)
                    if n < 2:
                        pe.wait_ge(t_lo, M - 1 + n)
                    else:
                        pe.wait_ge(ht_lo, n - 1)
                    turn(bank[LATE_TURN[n % 2]], blocks(lambda r: xb[:, 2 * n + r, :])).then_inc(ht_done, 1)
                if kind == "logits":
                    pe.wait_ge(ht_lo, n + 1)
                    if n == 0:
                        pe.wait_ge(gate_lo, 1)
                        pe.wait_ge(s_masked, M - 1)
                    if n:
                        pe.wait_ge(lt_copied, n)
                    for k in range(KC):
                        mm = split3(pe, logits_T(n)[0], both(WS, lambda a: a[:, k * E:(k + 1) * E]),
                                    both(XT, lambda a: a[:, k, n * S:(n + 1) * S]), k == 0, k == KC - 1)
                    mm.then_inc(lt_done, 1)
                if kind == "logits_turn":
                    pe.wait_ge(lt_copied, n + 1)
                    if n == 0:
                        pe.wait_ge(o_added, 4 * LAST + 3)
                    for r in range(2):
                        t = 2 * n + r
                        mm = pe.transpose(bank[LATE_LOGITS][:, t * E:(t + 1) * E],
                                          logits_T(n)[1][:, r * P:(r + 1) * P], ident[0:E, 0:E])
                    mm.then_inc(gl_done, 1)
                if kind in "gu":
                    pe.wait_ge(m_lo, 1)
                    pe.wait_ge(ht_lo, 2 * n + 2)
                    pe.wait_ge(at_lo, at_count(M - 1))
                    product(n, n, "gu".index(kind), n, 0, 0)
                if kind == "weights_turn":
                    zero(0)
                    zero(1)
                    pe.wait_ge(r_parts, 1)
                    pe.wait_ge(o_added, 4 * PAIRS)
                    for half in range(2):
                        for r in range(4):
                            mm = pe.transpose(bank[LATE_WT[half]][:, :].bitcast(BF16)[0:96, r * P:(r + 1) * P],
                                              wparts[:, 4 * half + r, :], identb[:, :])
                        mm.then_inc(r_turned, 1)

            for kind, n in TAIL:
                tail_step(kind, n)

            pe.wait_ge(sel_dma, 32)
            for half in range(2):
                pe.wait_ge(wT_ready, half + 1)
                product(half, half, 2, half, 0, 0)
            zero(2)
            zero(3)
            pe.wait_ge(m_lo, 2)
            product(2, 2, 0, 0, 1, 1)
            down(0, 0, 0)
            with pe.Fori(0, (NT - 1) // 2) as i:
                for c in range(2, 6):
                    s, tile, half, slot = 4 * i + c, 2 * i + c // 2, c % 2, (c // 2) % 2
                    for n in (1, 2):
                        product(s, c, n, half, slot, tile)
                    down(s - 1, 1 - half, (slot + 1) % 2 if half == 0 else slot)
                    if half:
                        pe.wait_ge(m_lo, tile + 2)
                    product(s + 1, c + 1, 0, 1 - half, (slot + 1) % 2 if half else slot, None)
            down(2 * NT - 1, 1, (NT - 1) % 2, True)

        @block.scalar
        def _(act):
            act.preload_act_table(ACT.Exp)

            def split(n):
                act.wait_ge(in_dma[n], 16)
                act.activation(inputs[n][1][0], inputs[n][0], ACT.Copy).then_inc(in_hi, 1)

            def evac(n):
                kind, c, half, _ = jobs[n]
                if n == 0:
                    act.wait_ge(const_dma, 48)
                act.wait_ge(a_done, n + 1)
                bias, dst = job_bias(kind, c), job_target(kind, c, half)[0]
                if bias is None:
                    act.activation(dst, bank[FJ[n % 3]][:, :], ACT.Copy).then_inc(a_hi, 1)
                else:
                    act.activation(dst, bank[FJ[n % 3]][:, :], ACT.Identity, bias=bias).then_inc(a_hi, 1)

            def exps(dst, src, slot, scale, done):
                for r in range(2):
                    ins = act.activation(dst[:, r * 256:r * 256 + 256], src[:, r * 256:r * 256 + 256], ACT.Exp,
                                         bias=c_nm[:, slot, r:r + 1], scale=scale,
                                         accum_out=c_sums[:, slot, r:r + 1])
                ins.then_inc(done, 1)

            def w_split(j, count, dst):
                act.wait_ge(stage_dma[j], count)
                act.activation(dst[0], stage[:, j, :], ACT.Copy).then_inc(w_hi, 1)

            def front_step(kind, b):
                tok = b * S
                if kind == "input":
                    split(b)
                if kind == "split":
                    evac(b)
                if kind == "exps":
                    act.wait_ge(f_nm, b + 1)
                    if b >= 2:
                        act.wait_ge(ft_done, b - 1)
                    exps(chain_ex(b), bank[FS], b, 1.0 / 16, f_exp)
                if kind == "norm":
                    act.wait_ge(f_rec, b + 1)
                    for r in range(2):
                        p = chain_ex(b)[:, r * 256:r * 256 + 256]
                        ins = act.activation(p, p, ACT.Copy, scale=c_rec[:, b, r:r + 1])
                    ins.then_inc(f_norm, 1)
                if kind == "pt":
                    act.wait_ge(ft_done, b + 1)
                    act.activation(PT[0][:, 0, :], bank[FT][:, :], ACT.Copy).then_inc(pt_hi, 1)
                if kind == "ct":
                    act.wait_ge(fpv_done, b + 1)
                    for c in range(2):
                        ins = act.activation(CT[0][:, 0, c * 256:c * 256 + 256], bank[FPV][:, c * 256:c * 256 + 256],
                                             ACT.Identity, bias=bqkv[:, 4 + c:5 + c])
                    ins.then_inc(ct_hi, 1)
                if kind == "cross_exps":
                    act.wait_ge(e_nm, b + 1)
                    exps(ex[:, 2 + b, :], bank[FES], 4 + b, 1.0, e_exp)
                if kind == "x1t":
                    act.wait_ge(fxt_done, b + 1)
                    act.activation(AT[0][:, :, tok:tok + S], two(bank[FXT][:, :]), ACT.Copy).then_inc(x1t_hi, 1)
                if kind == "cross_pt":
                    act.wait_ge(fet_done, b + 1)
                    act.activation(PT[0][:, 1, :], bank[FET][:, :], ACT.Copy).then_inc(et_hi, 1)
                if kind == "squares":
                    act.wait_ge(x2_ready, b + 1)
                    squares(x2, b, sq_ready)
                if kind == "xn":
                    act.wait_ge(rms_rstd, b + 1)
                    for t in (2 * b, 2 * b + 1):
                        ins = act.activation(xb[:, t, :], x2[:, t, :], ACT.Copy, scale=rstd[:, 16 + t:17 + t])
                    ins.then_inc(xn_ready, 1)
                if kind == "xnt":
                    act.wait_ge(fnt_done, b + 1)
                    for c in range(2):
                        ins = act.activation(XT[0][:, c, tok:tok + S], bank[FNT][:, c * 256:c * 256 + 256],
                                             ACT.Copy, scale=lnw[:, c:c + 1])
                    ins.then_inc(xnt_hi, 1)
                if kind == "weights":
                    for sem_, count in {6: ((v_done, 4),), 7: ((qk_done, 5),), 9: ((qk_done, 6),),
                                        10: ((qk_done, 8),), 11: ((qk_done, 10),)}.get(b, ()):
                        act.wait_ge(sem_, count)
                    w_split(FIRST_SLOTS[b], 16 * (1 + (b >= 5 and FIRST_SLOTS[b] < FIRST_CHUNKS)), first_target(b))
                if kind == "qk_split":
                    h, qk, half, _ = PIECES[b]
                    piece_high(Q if qk == "q" else K, h, half, b)
                if kind == "v_split":
                    v_high(b % 4, b // 4, b)
                if kind == "head_exps":
                    if b >= 4:
                        act.wait_ge(t_done, b - 3)
                    act.wait_ge(s_masked, b + 1)
                    exp_scores(b)
                if kind == "head_probs":
                    probs_high(b + 2, b)
                if kind == "head_attn":
                    piece_out(2 * b + 2, b % 2, b // 2, b % 2)

            def squares(src, b, done):
                for r in range(2):
                    t = 2 * b + r
                    ins = act.activation(xb[:, t, :], src[:, t, :], ACT.Square, accum_out=msq[:, t:t + 1])
                ins.then_inc(done, 1)

            def qk_high(j, index):
                piece_high(Q if j % 4 < 2 else K, (j // 4 + 1) % 2, j % 2, index)

            def piece_high(dst, head, half, index):
                act.wait_ge(qk_done, index + 1)
                act.activation(dst[0][:, head, half * HALF:half * HALF + HALF],
                               bank[BANK_QK][:, :], ACT.Copy).then_inc(qk_hi, 1)

            def v_high(q, par, index):
                act.wait_ge(v_done, index + 1)
                act.activation(V[0][:, par, 2 * q:2 * q + 2, :].rearrange("p t h -> p (t h)"),
                               bank[BANK_VO][:, :], ACT.Copy).then_inc(v_hi, 1)

            def probs_high(m, j):
                act.wait_ge(t_done, m - 1)
                act.activation(PT[0][:, j % 2, 0:384], bank[BANK_T[j % 2]][:, 0:384], ACT.Copy).then_inc(t_hi, 1)

            def out_high(m, j):
                ago = (j - 2) % SP_
                piece_out(m - 1, ago // 4, ago % 4 // 2, (ago // 2) % 2)

            def piece_out(count, h, half, n):
                act.wait_ge(pv_done, count)
                act.activation(AT[0][:, h, half * HALF:half * HALF + HALF],
                               bank[BANK_PV[n]][:, :], ACT.Copy).then_inc(at_hi, 1)

            def exp_scores(j):
                for at, n, r in ((0, 128, 0), (128, 256, 1)):
                    ins = act.activation(ex[:, j % 4, at:at + n], sm[:, j % 2, at:at + n], ACT.Exp,
                                         bias=nm[:, j, r:r + 1], scale=-1.0, accum_out=sums[:, j, r:r + 1])
                ins.then_inc(s_exp, 1)

            for kind, b in FRONT:
                front_step(kind, b)

            def pair(g, par, last):
                for j in range(HEAD_STEPS if last else SP_):
                    m = SP_ * g + j
                    probs_high(m, j)
                    act.wait_ge(s_masked, m + 1)
                    exp_scores(j)
                    qk_high(j, SP_ * g + 4 + j)
                    if j >= 4:
                        v_high(j - 4, 1 - par, 4 * (g + 1) + j - 4)
                    if j % 2:
                        out_high(m, j)
                    if not last or j in LAST_CHUNKS:
                        if j in (0, 2, 4, 6):
                            act.wait_ge(qk_done, SP_ * g + 4 + j)
                        elif j in (1, 3):
                            act.wait_ge(v_done, 4 * (g + 1))
                        else:
                            act.wait_ge(o_done, 4 * g)
                        w_split(j, 16 * (g + 1 + (j < FIRST_CHUNKS)), chunk_target(j))

            over_pairs(act, pair)

            def m_split(t, slot, count):
                act.wait_ge(m_dma[slot], count)
                act.activation(W[0][:, slot, :], raw_moe[:, slot, :], ACT.Copy).then_inc(m_hi, 1)

            def tail_step(kind, n):
                if kind == "exps":
                    act.wait_ge(s_masked, n + 1)
                    exp_scores(n % SP_)
                if kind == "probs":
                    probs_high(n + 2, n % SP_)
                if kind == "attn":
                    act.wait_ge(pv_done, n + 1)
                    act.activation(late_out(AT[0], n), late_pv(n), ACT.Copy).then_inc(at_hi, 1)
                if kind == "o_weights":
                    j = (5, 7)[n]
                    act.wait_ge(o_done, 4 * LAST)
                    w_split(j, 16 * (LAST + 1), chunk_target(j))
                if kind == "gate":
                    act.wait_ge(gate_dma, 16)
                    act.activation(WS[0][:, 0:2 * E], gate_raw[:, :, :].rearrange("p k e -> p (k e)"), ACT.Copy)\
                        .then_inc(gate_hi, 1)
                if kind == "tile":
                    if n == 1:
                        act.wait_ge(o_done, 4 * PAIRS)
                    m_split(n, n, 16)
                if kind == "squares":
                    act.wait_ge(o_added, 4 * LAST + n + 1)
                    squares(hid, n, h_sq)
                if kind == "xnt":
                    act.wait_ge(ht_done, n + 1)
                    for c in range(2):
                        ins = act.activation(XT[0][:, c, n * S:n * S + S],
                                             bank[LATE_TURN[n % 2]][:, c * 256:c * 256 + 256],
                                             ACT.Copy, scale=lnw[:, 2 + c:3 + c])
                    ins.then_inc(ht_hi, 1)
                if kind == "logits_copy":
                    act.wait_ge(lt_done, n + 1)
                    act.activation(logits_T(n)[1], logits_T(n)[0], ACT.Copy).then_inc(lt_copied, 1)
                if kind == "router":
                    act.wait_ge(r_sub, 1)
                    act.activation(gl[:, :, 0:E], gw[:, :, :], ACT.Exp).then_inc(r_exp, 1)
                    act.preload_act_table(ACT.Silu)

            for kind, n in TAIL:
                tail_step(kind, n)

            def silu(s, c):
                act.wait_ge(g_done, s + 1)
                if c >= 2:
                    act.wait_ge(us_ready, s - 1)
                act.activation(ex[:, c % 2, :], mix_bank(c, 0)[:, :], ACT.Silu).then_inc(silu_ready, 1)

            def activations_high(s, c):
                half = c % 2
                act.wait_ge(act_ready, s + 1)
                if c >= 2:
                    act.wait_ge(d_done, s - 1)
                act.activation(CT[0][:, half, :], ex[:, 4 + half, :], ACT.Copy).then_inc(act_hi, 1)

            silu(0, 0)
            silu(1, 1)
            activations_high(0, 0)
            activations_high(1, 1)
            with act.Fori(0, (NT - 1) // 2) as i:
                for c in range(2, 6):
                    s, tile = 4 * i + c, 2 * i + c // 2
                    if c % 2:
                        act.wait_ge(d_done, s - 1)
                        m_split(tile + 1, (c // 2 + 1) % 2, 16 * (i + 1 + (c // 2 + 1) // 2))
                    silu(s, c)
                    activations_high(s, c)

            act.wait_ge(z_ready, 1)
            for t in range(2):
                ins = act.activation(xb[:, t, :], hid[:, t, :], ACT.Copy, accum_out=msq[:, t:t + 1])
            ins.then_inc(z_summed, 1)
            act.wait_ge(z_mean, 1)
            for t in range(2):
                ins = act.activation(xb[:, t, :], hid[:, t, :], ACT.Square, bias=shift[:, t:t + 1],
                                     accum_out=msq[:, 2 + t:3 + t])
            ins.then_inc(z_squared, 1)
            for b in range(2):
                act.wait_ge(z_shift, b + 1)
                for t in (2 * b, 2 * b + 1):
                    ins = act.activation(xb[:, t, :], hid[:, t, :], ACT.Identity, bias=shift[:, t:t + 1],
                                         scale=rstd[:, t:t + 1])
                ins.then_inc(z_out, 1)

        @block.vector
        def _(dve):
            def low(dst, src, high, done):
                dve.tensor_tensor(dst, src, high.bitcast(F32), ALU.subtract).then_inc(done, 1)

            def split(n):
                if n == 0:
                    return
                dve.wait_ge(in_hi, n + 1)
                low(inputs[n][1][1], inputs[n][0], inputs[n][1][0], in_lo)

            def evac(n):
                kind, c, half, _ = jobs[n]
                dve.wait_ge(a_hi, n + 1)
                bias, (high, lo) = job_bias(kind, c), job_target(kind, c, half)
                if bias is None:
                    low(lo, bank[FJ[n % 3]][:, :], high, a_lo)
                else:
                    dve.scalar_tensor_tensor(out=lo, in0=bank[FJ[n % 3]][:, :], scalar=bias, in1=high.bitcast(F32),
                                             op0=ALU.add, op1=ALU.subtract).then_inc(a_lo, 1)

            def negmax(src, slot, scale, peak, done, count):
                dve.tensor_reduce(mx[:, slot, :], two(src), AX_X, ALU.max).then_inc(peak, 1)
                dve.wait_ge(peak, count)
                dve.tensor_scalar(c_nm[:, slot, :], mx[:, slot, :], -scale, None, ALU.mult).then_inc(done, 1)

            def moments(src, b, added, counted, done, skipped=0):
                dve.wait_ge(added, b + 1)
                for r in range(2):
                    ins = dve.bn_stats(stats[:, 2 * b + r, :], src[:, 2 * b + r, :])
                ins.then_inc(counted, 1)
                dve.wait_ge(counted, b + 1 - skipped)
                for r in range(2):
                    ins = dve.bn_aggr(mv[:, 2 * b + r, :], stats[:, 2 * b + r, :])
                ins.then_inc(done, 1)

            def centre(dst, src, b, at, done):
                for r in range(2):
                    t = 2 * b + r
                    ins = dve.tensor_scalar(dst[:, t, :], src[:, t, :], mv[:, t, 0:1], rstd[:, at + t:at + t + 1],
                                            ALU.subtract, ALU.mult)
                ins.then_inc(done, 1)

            def rms_rows(src, b, done):
                for r in range(2):
                    t = 2 * b + r
                    ins = dve.tensor_scalar(xb[:, t, :], src[:, t, :], rstd[:, 16 + t:17 + t], None, ALU.mult)
                ins.then_inc(done, 1)

            def weighted_low(b, turned, w, done):
                for c in range(2):
                    ins = dve.scalar_tensor_tensor(out=XT[1][:, c, b * S:b * S + S],
                                                   in0=turned[:, c * 256:c * 256 + 256],
                                                   scalar=lnw[:, w + c:w + c + 1],
                                                   in1=XT[0][:, c, b * S:b * S + S].bitcast(F32),
                                                   op0=ALU.mult, op1=ALU.subtract)
                ins.then_inc(done, 1)

            def front_step(kind, b):
                tok, rows = b * S, slice(2 * b, 2 * b + 2)
                if kind == "input":
                    split(b)
                if kind == "split":
                    evac(b)
                if kind == "peak":
                    dve.wait_ge(fs_done, b + 1)
                    negmax(bank[FS][:, :], b, 1.0 / 16, f_max, f_nm, b + 1)
                if kind == "norm":
                    dve.wait_ge(f_exp, b + 1)
                    dve.reciprocal(c_rec[:, b, :], c_sums[:, b, :]).then_inc(f_rec, 1)
                if kind == "pt":
                    dve.wait_ge(pt_hi, b + 1)
                    low(PT[1][:, 0, :], bank[FT][:, :], PT[0][:, 0, :], pt_lo)
                if kind == "ct":
                    dve.wait_ge(ct_hi, b + 1)
                    for c in range(2):
                        cols = slice(c * 256, c * 256 + 256)
                        ins = dve.scalar_tensor_tensor(out=CT[1][:, 0, cols], in0=bank[FPV][:, cols],
                                                       scalar=bqkv[:, 4 + c:5 + c],
                                                       in1=CT[0][:, 0, cols].bitcast(F32),
                                                       op0=ALU.add, op1=ALU.subtract)
                    ins.then_inc(ct_lo, 1)
                if kind == "cross_peak":
                    dve.wait_ge(fes_done, b + 1)
                    negmax(bank[FES][:, :], 4 + b, 1.0, e_max, e_nm, b + 1)
                if kind == "cross_norm":
                    dve.wait_ge(e_exp, b + 1)
                    dve.reciprocal(c_rec[:, 4 + b, :], c_sums[:, 4 + b, :]).then_inc(e_rec, 1)
                if kind == "y1":
                    dve.wait_ge(fout_done, b + 1)
                    if b == 0:
                        dve.wait_ge(xb_ready, 1)
                    dve.tensor_tensor(xb[:, rows, :], two(bank[FOUT][:, :]), xb[:, rows, :], ALU.add)\
                       .then_inc(y1_ready, 1)
                    moments(xb, b, y1_ready, y1_stats, y1_var)
                if kind == "x1":
                    dve.wait_ge(y1_rstd, b + 1)
                    centre(hid, xb, b, 0, x1_ready)
                if kind == "x1t":
                    dve.wait_ge(x1t_hi, b + 1)
                    low(AT[1][:, :, tok:tok + S], two(bank[FXT][:, :]), AT[0][:, :, tok:tok + S], x1t_lo)
                if kind == "cross_pt":
                    dve.wait_ge(et_hi, b + 1)
                    low(PT[1][:, 1, :], bank[FET][:, :], PT[0][:, 1, :], et_lo)
                if kind == "y2":
                    dve.wait_ge(fxm_done, b + 1)
                    dve.tensor_tensor(hid[:, rows, :], two(bank[FXM][:, :]), hid[:, rows, :], ALU.add)\
                       .then_inc(y2_ready, 1)
                    moments(hid, b, y2_ready, y2_stats, y2_var)
                if kind == "x2":
                    dve.wait_ge(y2_rstd, b + 1)
                    centre(x2, hid, b, 8, x2_ready)
                if kind == "xnt":
                    dve.wait_ge(xnt_hi, b + 1)
                    weighted_low(b, bank[FNT], 0, xnt_lo)
                if kind == "qk_split":
                    h, qk, half, _ = PIECES[b]
                    piece_low(Q if qk == "q" else K, h, half, b)
                if kind == "v_split":
                    v_low(b % 4, b // 4, b)
                if kind == "head_mask":
                    if b == 0:
                        dve.wait_ge(const_ready, 1)
                    if b >= 2:
                        dve.wait_ge(s_exp, b - 1)
                    dve.wait_ge(s_done, b + 1)
                    mask_scores(b)
                if kind == "head_inverse":
                    dve.wait_ge(s_exp, b + 1)
                    inverse_sums(b)
                if kind == "head_probs":
                    probs_low(b + 2, b)
                if kind == "head_attn":
                    dve.wait_ge(at_hi, b + 1)
                    high, lo = both(AT, lambda t: t[:, b % 2, b // 2 * HALF:b // 2 * HALF + HALF])
                    low(lo, bank[BANK_PV[b % 2]][:, :], high, at_lo)

            def qk_low(j, index):
                piece_low(Q if j % 4 < 2 else K, (j // 4 + 1) % 2, j % 2, index)

            def piece_low(dst, head, half, index):
                dve.wait_ge(qk_hi, index + 1)
                high, lo = both(dst, lambda t: t[:, head, half * HALF:half * HALF + HALF])
                low(lo, bank[BANK_QK][:, :], high, qk_lo)

            def v_low(q, par, index):
                dve.wait_ge(v_hi, index + 1)
                high, lo = both(V, lambda t: t[:, par, 2 * q:2 * q + 2, :].rearrange("p t h -> p (t h)"))
                low(lo, bank[BANK_VO][:, :], high, v_lo)

            def probs_low(m, j):
                dve.wait_ge(t_hi, m - 1)
                low(PT[1][:, j % 2, 0:384], bank[BANK_T[j % 2]][:, 0:384], PT[0][:, j % 2, 0:384], t_lo)

            def add_o(q, index, src=BANK_VO):
                dve.wait_ge(o_done, index + 1)
                rows = slice(2 * q, 2 * q + 2)
                dve.tensor_tensor(hid[:, rows, :], two(bank[src][:, :]), hid[:, rows, :], ALU.add)\
                   .then_inc(o_added, 1)

            def inverse_sums(j):
                dve.reciprocal(rec[:, j, :], sums[:, j, :]).then_inc(s_rec, 1)

            def mask_scores(j):
                for at, n, r in ((0, 128, 0), (128, 256, 1)):
                    ins = dve.tensor_tensor_reduce(out=sm[:, j % 2, at:at + n],
                                                   in0=bank[BANK_S[j % 2]][:, at:at + n],
                                                   in1=mask[:, 256 - n:256], scale=-SCALE, scalar=3.0e38,
                                                   op0=ALU.add, op1=ALU.min, accum_out=nm[:, j, r:r + 1])
                ins.then_inc(s_masked, 1)

            for kind, b in FRONT:
                front_step(kind, b)
            dve.wait_ge(hid_copied, B)

            def pair(g, par, last):
                for j in range(HEAD_STEPS if last else SP_):
                    m = SP_ * g + j
                    dve.wait_ge(s_exp, m)
                    dve.wait_ge(s_done, m + 1)
                    inverse_sums((j - 1) % SP_)
                    mask_scores(j)
                    probs_low(m, j)
                    qk_low(j, SP_ * g + 4 + j)
                    if j < 4:
                        add_o(j, 4 * (g - 1) + j)
                    if j >= 4:
                        v_low(j - 4, 1 - par, 4 * (g + 1) + j - 4)
                    if j % 2:
                        ago = (j - 2) % SP_
                        h, half = ago // 4, ago % 4 // 2
                        dve.wait_ge(at_hi, 4 * g + (j - 1) // 2)
                        high, lo = both(AT, lambda t: t[:, h, half * HALF:half * HALF + HALF])
                        low(lo, bank[BANK_PV[(ago // 2) % 2]][:, :], high, at_lo)

            over_pairs(dve, pair)

            def m_low(t, slot):
                dve.wait_ge(m_hi, t + 1)
                low(W[1][:, slot, :], raw_moe[:, slot, :], W[0][:, slot, :], m_lo)

            steps = [0]

            def link(ins):
                steps[0] += 1
                ins.then_inc(r_step, 1)
                dve.wait_ge(r_step, steps[0])

            def spread(a, n):
                return a[:, :].unsqueeze(2).to_broadcast([P, 8, n])

            def router():
                probs = gl[:, :, 0:E]
                dve.wait_ge(gl_done, B)
                dve.wait_ge(const_ready, 1)
                logits = bank[LATE_LOGITS][:, 0:8 * E].rearrange("p (t e) -> p t e", e=E)
                link(dve.tensor_reduce(gm[:, :], logits, AX_X, ALU.max))
                ins = dve.tensor_tensor(gw[:, :, :], logits, spread(gm, E), ALU.subtract)
                ins.then_inc(r_sub, 1)
                dve.wait_ge(r_exp, 1)
                link(dve.tensor_reduce(gs[:, :], probs, AX_X, ALU.add))
                link(dve.reciprocal(gr[:, :], gs[:, :]))
                link(dve.tensor_tensor(probs, probs, spread(gr, E), ALU.mult))
                for t in range(8):
                    ins = dve.max(g8[:, t, :], gl[:, t, :])
                link(ins)
                link(dve.tensor_reduce(gs[:, :], g8[:, :, 0:TOPK], AX_X, ALU.add))
                link(dve.memset(g8[:, :, TOPK:8], -1.0))
                for t in range(8):
                    ins = dve.match_replace(grep[:, t, :], g8[:, t, :], gl[:, t, :], 0.0)
                link(ins)
                link(dve.reciprocal(gr[:, :], gs[:, :]))
                link(dve.tensor_tensor(gw[:, :, :], probs, grep[:, :, 0:E], ALU.subtract))
                link(dve.tensor_tensor(gw[:, :, :], gw[:, :, :], spread(gr, E), ALU.mult))
                link(dve.tensor_copy(wparts[:, :, 0:E], gw[:, :, :]))
                link(dve.tensor_tensor(gt[:, :, :], gw[:, :, :], wparts[:, :, 0:E], ALU.subtract))
                link(dve.tensor_copy(wparts[:, :, 32:32 + E], gt[:, :, :]))
                link(dve.tensor_tensor(gt[:, :, :], gt[:, :, :], wparts[:, :, 32:32 + E], ALU.subtract))
                dve.tensor_copy(wparts[:, :, 64:64 + E], gt[:, :, :]).then_inc(r_parts, 1)

            def tail_step(kind, n):
                if kind == "inverse":
                    dve.wait_ge(s_exp, n + 1)
                    inverse_sums(n % SP_)
                if kind == "mask":
                    dve.wait_ge(s_exp, n - 1)
                    dve.wait_ge(s_done, n + 1)
                    mask_scores(n % SP_)
                if kind == "probs":
                    probs_low(n + 2, n % SP_)
                if kind == "attn":
                    dve.wait_ge(at_hi, at_count(n))
                    low(late_out(AT[1], n), late_pv(n), late_out(AT[0], n), at_lo)
                if kind == "gate":
                    dve.wait_ge(gate_hi, 1)
                    low(WS[1][:, 0:2 * E], gate_raw[:, :, :].rearrange("p k e -> p (k e)"), WS[0][:, 0:2 * E],
                        gate_lo)
                if kind == "add":
                    add_o(n, 4 * LAST + n, LATE_OUT[n % 2])
                if kind == "xn":
                    dve.wait_ge(h_rstd, n + 1)
                    rms_rows(hid, n, h_norm)
                if kind == "xnt":
                    dve.wait_ge(ht_hi, n + 1)
                    weighted_low(n, bank[LATE_TURN[n % 2]], 2, ht_lo)
                if kind == "router":
                    router()
            for kind, n in TAIL:
                tail_step(kind, n)

            def gate_up(s, c):
                dve.wait_ge(silu_ready, s + 1)
                dve.wait_ge(u_done, s + 1)
                dve.tensor_tensor(ex[:, 2 + c % 2, :], mix_bank(c, 1)[:, :], ex[:, c % 2, :], ALU.mult)\
                   .then_inc(us_ready, 1)

            def weigh(s, c):
                dve.wait_ge(us_ready, s + 1)
                dve.wait_ge(b_done, s + 1)
                dve.tensor_tensor(ex[:, 4 + c % 2, :], mix_bank(c, 2)[:, :], ex[:, 2 + c % 2, :], ALU.mult)\
                   .then_inc(act_ready, 1)

            def activations_low(s, c):
                dve.wait_ge(act_hi, s + 1)
                low(CT[1][:, c % 2, :], ex[:, 4 + c % 2, :], CT[0][:, c % 2, :], act_lo)

            def tile_slot(c):
                return (c // 2 + 1) % 2

            gate_up(0, 0)
            for half in range(2):
                dve.wait_ge(r_turned, half + 1)
                dve.tensor_copy(wT[:, half * HALF:half * HALF + HALF],
                                bank[LATE_WT[half]][:, :].bitcast(BF16)[0:96, 0:HALF]).then_inc(wT_ready, 1)
            gate_up(1, 1)
            for c in range(2):
                weigh(c, c)
            for c in range(2):
                activations_low(c, c)
            dve.wait_ge(m_lo, 2)
            with dve.Fori(0, (NT - 1) // 2) as i:
                for c in range(2, 6):
                    if c % 2:
                        m_low(2 * i + c // 2 + 1, tile_slot(c))
                    gate_up(4 * i + c, c)
                    weigh(4 * i + c, c)
                    activations_low(4 * i + c, c)

            for b in range(B):
                rows = slice(2 * b, 2 * b + 2)
                dve.wait_ge(hx_ready, 1)
                if b < 2:
                    dve.wait_ge(d_done, 2 * NT - 1)
                else:
                    dve.wait_ge(d_last, b - 1)
                dve.tensor_tensor(hid[:, rows, :], two(bank[b][:, :]), x2[:, rows, :], ALU.add).then_inc(z_ready, 1)
                if b:
                    moments(hid, b, z_ready, z_stats, z_var, 1)
            for b in (2, 3):
                dve.wait_ge(z_rstd, b + 1)
                centre(xb, hid, b, 0, z_out_late)

        @block.gpsimd
        def _(pool):
            pool.memset(ident[:, :], 0.0).then_inc(pool_step, 1)
            pool.memset(identb[:, :], 0.0).then_inc(pool_step, 1)
            pool.memset(mask[:, :], 0.0).then_inc(pool_step, 1)
            pool.memset(mh[:, :], -0.5).then_inc(pool_step, 1)
            pool.memset(zeros[:, :], 0.0).then_inc(pool_step, 1)
            pool.memset(wparts[:, :, :], 0.0).then_inc(pool_step, 1)
            pool.memset(gl[:, :, :], -1.0).then_inc(pool_step, 1)
            pool.wait_ge(pool_step, 7)
            for m in (ident, identb):
                pool.affine_select(out=m[:, :], in_=m[:, :], compare_op=ALU.not_equal, fill=1.0, base=0,
                                   pattern=[[-1, P]], channel_multiplier=1).then_inc(ident_ready, 1)
            pool.affine_select(out=mask[:, 128:256], in_=mask[:, 128:256], compare_op=ALU.is_ge, fill=MASK, base=0,
                               pattern=[[-1, P]], channel_multiplier=1)
            pool.memset(wparts[:, :, E:E + 1], 1.0).then_inc(const_ready, 1)

            def select_rows(n):
                rows = sel[0:32, 0:E * I]
                if n == 0:
                    pool.memset(sel[0:32, :], 1.0).then_inc(pool_step, 1)
                elif n == 1:
                    pool.wait_ge(pool_step, 8)
                    pool.affine_select(out=rows, in_=rows, compare_op=ALU.is_ge, fill=0.0, base=0,
                                       pattern=[[1, E * I]], channel_multiplier=-I).then_inc(pool_step, 1)
                else:
                    pool.wait_ge(pool_step, 9)
                    pool.affine_select(out=rows, in_=rows, compare_op=ALU.is_ge, fill=0.0, base=I - 1,
                                       pattern=[[-1, E * I]], channel_multiplier=I)
                    pool.affine_select(out=sel[0:32, E * I:], in_=sel[0:32, E * I:], compare_op=ALU.is_equal,
                                       fill=0.0, base=-E, pattern=[[0, NT * P - E * I]],
                                       channel_multiplier=1).then_inc(sel_ready, 1)

            def inverse_root(src, at, n, scale, eps, eps_done, done, count):
                pool.tensor_scalar(veps[:, at:at + n], src, scale, eps, ALU.mult, ALU.add).then_inc(eps_done, 1)
                pool.wait_ge(eps_done, count)
                pool.tensor_tensor(rstd[:, at:at + n], veps[:, at:at + n], mh[:, 0:n], ALU.pow).then_inc(done, 1)

            def w_low(j, count, dst):
                pool.wait_ge(w_hi, count)
                pool.tensor_tensor(dst[1], stage[:, j, :], dst[0].bitcast(F32), ALU.subtract).then_inc(w_lo, 1)

            def normalise(m, j):
                pool.wait_ge(s_rec, m + 1)
                for at, n, r in ((0, 128, 0), (128, 256, 1)):
                    ins = pool.tensor_tensor(ex[:, j % 4, at:at + n], ex[:, j % 4, at:at + n],
                                             rec[:, j, r:r + 1].to_broadcast([P, n]), ALU.mult)
                ins.then_inc(s_norm, 1)

            for kind, b in FRONT:
                rows = slice(2 * b, 2 * b + 2)
                if kind == "input" and b == 0:
                    pool.wait_ge(in_hi, 1)
                    pool.tensor_tensor(inputs[0][1][1], inputs[0][0], inputs[0][1][0].bitcast(F32), ALU.subtract)\
                        .then_inc(wq_lo, 1)
                if kind == "sel":
                    select_rows(b)
                if kind == "x_bias":
                    pool.wait_ge(x_dma, 32)
                    pool.tensor_tensor(xb[:, :, :], xb[:, :, :], bo[:, :].unsqueeze(1).to_broadcast([P, 8, 256]),
                                       ALU.add).then_inc(xb_ready, 1)
                if kind == "y1_root":
                    pool.wait_ge(y1_var, b + 1)
                    inverse_root(mv[:, rows, 1], 2 * b, 2, 1.0, LN_EPS, y1_eps, y1_rstd, b + 1)
                if kind == "cross_norm":
                    pool.wait_ge(e_rec, b + 1)
                    for r in range(2):
                        p = ex[:, 2 + b, r * 256:r * 256 + 256]
                        ins = pool.tensor_tensor(p, p, c_rec[:, 4 + b, r:r + 1].to_broadcast([P, 256]), ALU.mult)
                    ins.then_inc(e_norm, 1)
                if kind == "y2_root":
                    pool.wait_ge(y2_var, b + 1)
                    inverse_root(mv[:, rows, 1], 8 + 2 * b, 2, 1.0, LN_EPS, y2_eps, y2_rstd, b + 1)
                if kind == "rms":
                    pool.wait_ge(sq_ready, b + 1)
                    inverse_root(msq[:, rows], 16 + 2 * b, 2, 1.0 / H, RMS_EPS, rms_eps, rms_rstd, b + 1)
                if kind == "keep":
                    pool.wait_ge(x2_ready, b + 1)
                    pool.tensor_copy(hid[:, rows, :], x2[:, rows, :]).then_inc(hid_copied, 1)
                if kind == "weights":
                    w_low(FIRST_SLOTS[b], b + 1, first_target(b))
                if kind == "head_norm":
                    normalise(b, b)

            def pair(g, par, last):
                for j in range(HEAD_STEPS - 1 if last else SP_):
                    if not last or j in LAST_CHUNKS:
                        w_low(j, chunks_done(g, j, last), chunk_target(j))
                    normalise(SP_ * g + j, j)

            def tail_step(kind, n):
                if kind == "norm":
                    normalise(n, n % SP_)
                if kind == "o_weights":
                    j = (5, 7)[n]
                    w_low(j, chunks_done(LAST, j, True), chunk_target(j))
                if kind == "rms":
                    pool.wait_ge(h_sq, n + 1)
                    inverse_root(msq[:, 2 * n:2 * n + 2], 16 + 2 * n, 2, 1.0 / H, RMS_EPS, h_eps, h_rstd, n + 1)
                if kind == "tile":
                    pool.wait_ge(m_hi, n + 1)
                    pool.tensor_tensor(W[1][:, n, :], raw_moe[:, n, :], W[0][:, n, :].bitcast(F32), ALU.subtract)\
                        .then_inc(m_lo, 1)
                if kind == "hx":
                    pool.tensor_tensor(x2[:, :, :], hid[:, :, :], x2[:, :, :], ALU.add).then_inc(hx_ready, 1)

            normalise(SP_ - 1, SP_ - 1)
            over_pairs(pool, pair)
            for kind, n in TAIL:
                tail_step(kind, n)
            pool.wait_ge(z_summed, 1)
            pool.tensor_scalar(shift[:, 0:2], msq[:, 0:2], -1.0 / H, None, ALU.mult).then_inc(z_mean, 1)
            for b in range(B):
                if b == 0:
                    pool.wait_ge(z_squared, 1)
                else:
                    pool.wait_ge(z_var, b)
                rows = slice(2 * b, 2 * b + 2)
                if b == 1:
                    pool.tensor_scalar(shift[:, rows], mv[:, rows, 0], -1.0, None, ALU.mult)
                if b == 0:
                    inverse_root(msq[:, 2:4], 0, 2, 1.0 / H, LN_EPS, z_eps, z_rstd, 1)
                else:
                    inverse_root(mv[:, rows, 1], 2 * b, 2, 1.0, LN_EPS, z_eps, z_rstd, b + 1)
                if b < 2:
                    pool.wait_ge(z_rstd, b + 1)
                    pool.tensor_tensor(shift[:, rows], shift[:, rows], rstd[:, rows], ALU.mult).then_inc(z_shift, 1)


def kernel(**inputs):
    import numpy as np
    import concourse.bacc as bacc
    from concourse.bass_utils import run_bass_kernel_spmd

    a = {k: np.asarray(v) for k, v in inputs.items()}
    f32 = np.float32

    def chunks(w):
        return w.reshape(-1, P, w.shape[-1]).transpose(1, 0, 2)

    xT = chunks(a["x"].reshape(T, H).T)
    ctxT = a["ctx_1024"].reshape(T, P).T
    w_qkv = np.stack([chunks(a["L0_attn_w_qkv"][n * H:(n + 1) * H].T).reshape(P, 512) for n in range(3)])
    w_side = np.concatenate([a["L0_xattn_Wq"].T, a["L0_xattn_Wk"].T,
                             chunks(a["L0_attn_w_out"].T).reshape(P, 512)], axis=1)
    b_qkv = a["L0_attn_b_qkv"].reshape(6, P).T
    b_x = np.stack([a["L0_xattn_bq"], a["L0_xattn_bk"]], axis=1)
    ln_w = np.concatenate([a["L0_ffn_ln1_w"].reshape(2, P).T, a["L0_ffn_ln2_w"].reshape(2, P).T], axis=1)

    q = a["L0_ffn_q_w"].reshape(NH, QHD, H)[:, :HD]
    kv = a["L0_ffn_kv_w"]
    k = kv[:NH * HD].reshape(NH, HD, H)
    v = kv[NH * HD:2 * NH * HD].reshape(PAIRS, 2 * HD, H)
    o = a["L0_ffn_o_w"].reshape(H, NH, HD)

    def q_of(n):
        return chunks(q[n].T).reshape(P, 256)

    def k_of(n):
        return chunks(k[n].T).reshape(P, 256)

    def v_of(g, c):
        return v[g].T[c * P:(c + 1) * P]

    def o_of(n):
        return o[:, n].T

    w_first = np.stack([q_of(0), k_of(0), v_of(0, 0), v_of(0, 1), q_of(1)])
    w_heads = np.stack([np.stack([k_of(2 * g + 1), v_of(g + 1, 0), q_of(2 * g + 2), v_of(g + 1, 1),
                                  k_of(2 * g + 2), o_of(2 * g), q_of(2 * g + 3), o_of(2 * g + 1)])
                        for g in range(PAIRS - 1)])
    w_last = np.stack([k_of(NH - 1), o_of(NH - 2), o_of(NH - 1)])

    w1, sh = a["L0_ffn_w1"], a["L0_ffn_sh_gu_w"]
    tiles = NT + 1
    g = np.zeros((tiles * P, H), f32)
    u = np.zeros((tiles * P, H), f32)
    d = np.zeros((tiles * P, H), f32)
    g[:E * I] = w1[:, :I].reshape(E * I, H)
    u[:E * I] = w1[:, I:].reshape(E * I, H)
    d[:E * I] = a["L0_ffn_w2"].transpose(0, 2, 1).reshape(E * I, H)
    g[E * I:FF] = sh[:2 * I]
    u[E * I:FF] = sh[2 * I:]
    d[E * I:FF] = a["L0_ffn_sh_down_w"].T

    def gu_tiles(w):
        return w.reshape(tiles, P, KC, P).transpose(0, 3, 2, 1).reshape(tiles, P, 256)

    w_moe = np.concatenate([gu_tiles(g), gu_tiles(u), d.reshape(tiles, P, H)], axis=2)
    gateT = chunks(a["L0_ffn_gate_w"].T)

    nc = bacc.Bacc("TRN2", target_bir_lowering=False, num_devices=1)
    given = dict(x=a["x"], xT=xT, ctxT=ctxT, w_qkv=w_qkv, w_side=w_side, b_qkv=b_qkv,
                 b_out=a["L0_attn_b_out"], b_x=b_x, ln_w=ln_w, w_heads_first=w_first, w_heads=w_heads,
                 w_last=w_last, w_moe=w_moe, gateT=gateT)
    given = {n: np.ascontiguousarray(w) for n, w in given.items()}
    args = {n: nc.dram_tensor(n, w.shape, mybir.dt.from_np(w.dtype), kind="ExternalInput").ap()
            for n, w in given.items()}
    out = nc.dram_tensor("out", (B, S, H), F32, kind="ExternalOutput").ap()
    program(nc, *args.values(), out)
    return run_bass_kernel_spmd(nc, [given], core_ids=[0]).results[0]["out"]
```
